# Optimizing a Trainium2 kernel written in Bass

```python
import numpy as np
import jax
import jax.numpy as jnp

def _softmax(x, axis=-1):
    return jax.nn.softmax(x, axis=axis)

def _gelu(x):
    return jax.nn.gelu(x, approximate=True)

def _silu(x):
    return jax.nn.silu(x)

def _sigmoid(x):
    return jax.nn.sigmoid(x)

def _layernorm(x, axis=-1, eps=1e-05):
    m = jnp.mean(x, axis=axis, keepdims=True)
    v = jnp.var(x, axis=axis, keepdims=True)
    return (x - m) / jnp.sqrt(v + eps)

def _scatter_add(tgt, idx, src, axis=0):
    return tgt.at[idx].add(src)

def _segment_sum(src, seg, n):
    return jax.ops.segment_sum(src, seg, n)
kernel_name = 'mk_macaron_d2_jaxref_r8_aea6db'

def setup_inputs(seed: int=0):
    np.random.seed(seed)
    _w = jnp.asarray

    def _L0_attn_setup():
        import math
        import jax, jax.numpy as jnp
        import numpy as np
        B, T, E, H, L = (2, 256, 128, 16, 128)
        key = jax.random.key(seed)
        ks = jax.random.split(key, 11)
        w = lambda k, shape: jax.random.normal(k, shape, jnp.float32) * 0.02
        return {'x': jax.random.normal(ks[0], (B, T, E), jnp.float32), 'Wq': w(ks[1], (E, E)), 'bq': jnp.zeros((E,), jnp.float32), 'Wk': w(ks[2], (E, E)), 'bk': jnp.zeros((E,), jnp.float32), 'Wv': w(ks[3], (E, E)), 'bv': jnp.zeros((E,), jnp.float32), 'Wl': w(ks[4], (E, L)), 'bl': jnp.zeros((L,), jnp.float32), 'Wo': w(ks[5], (L, E)), 'bo': jnp.zeros((E,), jnp.float32)}
    _L0_attn_in = _L0_attn_setup()

    def _L0_ffn_setup():
        import jax, jax.numpy as jnp
        import numpy as np
        EMBED_DIM = 128
        HIDDEN_DIM = 512
        NUM_EXPERTS = 8
        TOP_K = 2
        key = jax.random.key(seed)
        ks = jax.random.split(key, 4)
        std1 = float(np.sqrt(2.0 / EMBED_DIM))
        std2 = float(np.sqrt(2.0 / HIDDEN_DIM))
        x = jax.random.normal(ks[0], (1, 256, EMBED_DIM), dtype=jnp.float32)
        w_router = jax.random.normal(ks[1], (EMBED_DIM, NUM_EXPERTS), dtype=jnp.float32) * 0.02
        w1 = jax.random.normal(ks[2], (NUM_EXPERTS, EMBED_DIM, HIDDEN_DIM), dtype=jnp.float32) * std1
        b1 = jnp.zeros((NUM_EXPERTS, HIDDEN_DIM), dtype=jnp.float32)
        w2 = jax.random.normal(ks[3], (NUM_EXPERTS, HIDDEN_DIM, EMBED_DIM), dtype=jnp.float32) * std2
        b2 = jnp.zeros((NUM_EXPERTS, EMBED_DIM), dtype=jnp.float32)
        return {'x': x, 'w_router': w_router, 'w1': w1, 'b1': b1, 'w2': w2, 'b2': b2}
    _L0_ffn_in = _L0_ffn_setup()

    def _L1_attn_setup():
        import jax, jax.numpy as jnp
        import numpy as np
        from jax import lax
        D = 128
        E = 2
        DI = D * E
        DS = 16
        DK = 3
        DTR = 64
        B = 2
        L = 512

        def _silu(v):
            return v * jax.nn.sigmoid(v)

        def _forward(x, W_in, W_conv, W_xproj, W_dt, b_dt, W_out, ln_g, ln_b):
            xz = x @ W_in
            xs, z = jnp.split(xz, 2, axis=-1)
            xc = lax.conv_general_dilated(xs.transpose(0, 2, 1), W_conv, (1,), [(DK // 2, DK // 2)], dimension_numbers=('NCH', 'OIH', 'NCH'), feature_group_count=DI)
            xs = _silu(xc.transpose(0, 2, 1))
            xp = xs @ W_xproj
            dt_lo = xp[..., :DTR]
            Bp = xp[..., DTR:DTR + DS]
            Cp = xp[..., DTR + DS:]
            dt = jax.nn.softplus(dt_lo @ W_dt + b_dt)
            dtm = dt.mean(-1)
            xm = xs.mean(-1)
            decay = jnp.exp(-dtm)
            Bx = Bp * xm[..., None]

            def step(h, inp):
                d, bx = inp
                h = h * d[:, None] + bx
                return (h, h.sum(-1))
            h0 = jnp.zeros((x.shape[0], DS), x.dtype)
            _, S = lax.scan(step, h0, (decay.T, Bx.transpose(1, 0, 2)))
            y = Cp * S.T[..., None]
            y = jnp.tile(y, (1, 1, DI // DS))
            mu = y.mean(-1, keepdims=True)
            var = y.var(-1, keepdims=True)
            y = (y - mu) * lax.rsqrt(var + 1e-05) * ln_g + ln_b
            y = y * _silu(z)
            return y @ W_out
        key = jax.random.key(seed)
        ks = jax.random.split(key, 8)
        s = 0.02
        return {'x': jax.random.normal(ks[0], (B, L, D), jnp.float32), 'W_in': jax.random.normal(ks[1], (D, 2 * DI), jnp.float32) * s, 'W_conv': jax.random.normal(ks[2], (DI, 1, DK), jnp.float32) * s, 'W_xproj': jax.random.normal(ks[3], (DI, DTR + 2 * DS), jnp.float32) * s, 'W_dt': jax.random.normal(ks[4], (DTR, DI), jnp.float32) * s, 'b_dt': jax.random.normal(ks[5], (DI,), jnp.float32) * s, 'W_out': jax.random.normal(ks[6], (DI, D), jnp.float32) * s, 'ln_g': jnp.ones((DI,), jnp.float32), 'ln_b': jnp.zeros((DI,), jnp.float32)}
    _L1_attn_in = _L1_attn_setup()

    def _L1_ffn_setup():
        import jax, jax.numpy as jnp
        import numpy as np
        B, S, H = (2, 256, 128)
        E, K, F_EXP, F_SHARED = (16, 2, 64, 128)
        key = jax.random.key(seed)
        ks = jax.random.split(key, 9)
        sc = 1.0 / np.sqrt(H)
        scf = 1.0 / np.sqrt(F_EXP)
        scfs = 1.0 / np.sqrt(F_SHARED)
        return {'x': jax.random.normal(ks[0], (B, S, H), dtype=jnp.float32), 'router_w': jax.random.normal(ks[1], (H, E), dtype=jnp.float32) * sc, 'gate_w': jax.random.normal(ks[2], (E, H, F_EXP), dtype=jnp.float32) * sc, 'up_w': jax.random.normal(ks[3], (E, H, F_EXP), dtype=jnp.float32) * sc, 'down_w': jax.random.normal(ks[4], (E, F_EXP, H), dtype=jnp.float32) * scf, 'shared_gate_w': jax.random.normal(ks[5], (H, F_SHARED), dtype=jnp.float32) * sc, 'shared_up_w': jax.random.normal(ks[6], (H, F_SHARED), dtype=jnp.float32) * sc, 'shared_down_w': jax.random.normal(ks[7], (F_SHARED, H), dtype=jnp.float32) * scfs}
    _L1_ffn_in = _L1_ffn_setup()
    _d = {'L0_attn_x': _L0_attn_in['x'], 'L0_attn_Wq': _L0_attn_in['Wq'], 'L0_attn_bq': _L0_attn_in['bq'], 'L0_attn_Wk': _L0_attn_in['Wk'], 'L0_attn_bk': _L0_attn_in['bk'], 'L0_attn_Wv': _L0_attn_in['Wv'], 'L0_attn_bv': _L0_attn_in['bv'], 'L0_attn_Wl': _L0_attn_in['Wl'], 'L0_attn_bl': _L0_attn_in['bl'], 'L0_attn_Wo': _L0_attn_in['Wo'], 'L0_attn_bo': _L0_attn_in['bo'], 'L0_ffn_w_router': _L0_ffn_in['w_router'], 'L0_ffn_w1': _L0_ffn_in['w1'], 'L0_ffn_b1': _L0_ffn_in['b1'], 'L0_ffn_w2': _L0_ffn_in['w2'], 'L0_ffn_b2': _L0_ffn_in['b2'], 'L1_attn_W_in': _L1_attn_in['W_in'], 'L1_attn_W_conv': _L1_attn_in['W_conv'], 'L1_attn_W_xproj': _L1_attn_in['W_xproj'], 'L1_attn_W_dt': _L1_attn_in['W_dt'], 'L1_attn_b_dt': _L1_attn_in['b_dt'], 'L1_attn_W_out': _L1_attn_in['W_out'], 'L1_attn_ln_g': _L1_attn_in['ln_g'], 'L1_attn_ln_b': _L1_attn_in['ln_b'], 'L1_ffn_router_w': _L1_ffn_in['router_w'], 'L1_ffn_gate_w': _L1_ffn_in['gate_w'], 'L1_ffn_up_w': _L1_ffn_in['up_w'], 'L1_ffn_down_w': _L1_ffn_in['down_w'], 'L1_ffn_shared_gate_w': _L1_ffn_in['shared_gate_w'], 'L1_ffn_shared_up_w': _L1_ffn_in['shared_up_w'], 'L1_ffn_shared_down_w': _L1_ffn_in['shared_down_w']}
    _x0 = _d['L0_attn_x']
    _d['L0_attn_x'] = jax.random.normal(jax.random.fold_in(jax.random.key(seed), 1), (8, 512, 128), dtype=_x0.dtype)
    del _x0
    return _d

def reference(L0_attn_x, L0_attn_Wq, L0_attn_bq, L0_attn_Wk, L0_attn_bk, L0_attn_Wv, L0_attn_bv, L0_attn_Wl, L0_attn_bl, L0_attn_Wo, L0_attn_bo, L0_ffn_w_router, L0_ffn_w1, L0_ffn_b1, L0_ffn_w2, L0_ffn_b2, L1_attn_W_in, L1_attn_W_conv, L1_attn_W_xproj, L1_attn_W_dt, L1_attn_b_dt, L1_attn_W_out, L1_attn_ln_g, L1_attn_ln_b, L1_ffn_router_w, L1_ffn_gate_w, L1_ffn_up_w, L1_ffn_down_w, L1_ffn_shared_gate_w, L1_ffn_shared_up_w, L1_ffn_shared_down_w):

    def _L0_attn_ref(x, Wq, bq, Wk, bk, Wv, bv, Wl, bl, Wo, bo):
        import math
        import jax, jax.numpy as jnp
        import numpy as np
        B, T, E, H, L = (2, 256, 128, 16, 128)
        b, t, e = x.shape
        hd = e // H
        lhd = L // H
        scale = 1.0 / math.sqrt(hd)
        q = (x @ Wq + bq).reshape(b, t, H, hd).transpose(0, 2, 1, 3)
        k = ((x @ Wk + bk) @ Wl + bl).reshape(b, t, H, lhd).transpose(0, 2, 1, 3)
        v = ((x @ Wv + bv) @ Wl + bl).reshape(b, t, H, lhd).transpose(0, 2, 1, 3)
        attn = jax.nn.softmax(jnp.einsum('bhqd,bhkd->bhqk', q, k) * scale, axis=-1)
        out = jnp.einsum('bhqk,bhkd->bhqd', attn, v)
        out = out.transpose(0, 2, 1, 3).reshape(b, t, L)
        return out @ Wo + bo

    def _L0_ffn_ref(x, w_router, w1, b1, w2, b2):
        import jax, jax.numpy as jnp
        import numpy as np
        EMBED_DIM = 128
        HIDDEN_DIM = 512
        NUM_EXPERTS = 8
        TOP_K = 2
        orig_shape = x.shape
        xf = x.reshape(-1, EMBED_DIM)
        logits = xf @ w_router
        probs = jax.nn.softmax(logits, axis=-1)
        topk_w, topk_idx = jax.lax.top_k(probs, TOP_K)
        mask = jax.nn.one_hot(topk_idx, NUM_EXPERTS, dtype=xf.dtype)
        weights = jnp.sum(topk_w[..., None] * mask, axis=1)
        h = jnp.einsum('te,ieh->tih', xf, w1) + b1
        h = jax.nn.gelu(h)
        out = jnp.einsum('tih,ihe->tie', h, w2) + b2
        out = jnp.sum(out * weights[..., None], axis=1)
        return out.reshape(orig_shape)

    def _L1_attn_ref(x, W_in, W_conv, W_xproj, W_dt, b_dt, W_out, ln_g, ln_b):
        import jax, jax.numpy as jnp
        import numpy as np
        from jax import lax
        D = 128
        E = 2
        DI = D * E
        DS = 16
        DK = 3
        DTR = 64
        B = 2
        L = 512

        def _silu(v):
            return v * jax.nn.sigmoid(v)

        def _forward(x, W_in, W_conv, W_xproj, W_dt, b_dt, W_out, ln_g, ln_b):
            xz = x @ W_in
            xs, z = jnp.split(xz, 2, axis=-1)
            xc = lax.conv_general_dilated(xs.transpose(0, 2, 1), W_conv, (1,), [(DK // 2, DK // 2)], dimension_numbers=('NCH', 'OIH', 'NCH'), feature_group_count=DI)
            xs = _silu(xc.transpose(0, 2, 1))
            xp = xs @ W_xproj
            dt_lo = xp[..., :DTR]
            Bp = xp[..., DTR:DTR + DS]
            Cp = xp[..., DTR + DS:]
            dt = jax.nn.softplus(dt_lo @ W_dt + b_dt)
            dtm = dt.mean(-1)
            xm = xs.mean(-1)
            decay = jnp.exp(-dtm)
            Bx = Bp * xm[..., None]

            def step(h, inp):
                d, bx = inp
                h = h * d[:, None] + bx
                return (h, h.sum(-1))
            h0 = jnp.zeros((x.shape[0], DS), x.dtype)
            _, S = lax.scan(step, h0, (decay.T, Bx.transpose(1, 0, 2)))
            y = Cp * S.T[..., None]
            y = jnp.tile(y, (1, 1, DI // DS))
            mu = y.mean(-1, keepdims=True)
            var = y.var(-1, keepdims=True)
            y = (y - mu) * lax.rsqrt(var + 1e-05) * ln_g + ln_b
            y = y * _silu(z)
            return y @ W_out
        return _forward(x, W_in, W_conv, W_xproj, W_dt, b_dt, W_out, ln_g, ln_b)

    def _L1_ffn_ref(x, router_w, gate_w, up_w, down_w, shared_gate_w, shared_up_w, shared_down_w):
        import jax, jax.numpy as jnp
        import numpy as np
        B, S, H = (2, 256, 128)
        E, K, F_EXP, F_SHARED = (16, 2, 64, 128)
        b, s, h = x.shape
        T = b * s
        x_flat = x.reshape(T, h)
        shared_out = jax.nn.silu(x @ shared_gate_w) * (x @ shared_up_w) @ shared_down_w
        router_probs = jax.nn.softmax(x_flat @ router_w, axis=-1)
        topk_probs, topk_idx = jax.lax.top_k(router_probs, K)
        coeff = jnp.einsum('tk,tke->te', topk_probs, jax.nn.one_hot(topk_idx, E, dtype=x.dtype))

        def expert_step(acc, ws):
            g, u, d, c = ws
            inter = jax.nn.silu(x_flat @ g) * (x_flat @ u)
            return (acc + inter @ d * c[:, None], None)
        routed, _ = jax.lax.scan(expert_step, jnp.zeros((T, h), dtype=x.dtype), (gate_w, up_w, down_w, coeff.T))
        return routed.reshape(b, s, h) + shared_out
    x = L0_attn_x
    x = x + 0.5 * _L0_ffn_ref(_layernorm(x, axis=-1), L0_ffn_w_router, L0_ffn_w1, L0_ffn_b1, L0_ffn_w2, L0_ffn_b2)
    x = x + _L0_attn_ref(_layernorm(x, axis=-1), L0_attn_Wq, L0_attn_bq, L0_attn_Wk, L0_attn_bk, L0_attn_Wv, L0_attn_bv, L0_attn_Wl, L0_attn_bl, L0_attn_Wo, L0_attn_bo)
    x = x + 0.5 * _L0_ffn_ref(_layernorm(x, axis=-1), L0_ffn_w_router, L0_ffn_w1, L0_ffn_b1, L0_ffn_w2, L0_ffn_b2)
    x = x + 0.5 * _L1_ffn_ref(_layernorm(x, axis=-1), L1_ffn_router_w, L1_ffn_gate_w, L1_ffn_up_w, L1_ffn_down_w, L1_ffn_shared_gate_w, L1_ffn_shared_up_w, L1_ffn_shared_down_w)
    x = x + _L1_attn_ref(_layernorm(x, axis=-1), L1_attn_W_in, L1_attn_W_conv, L1_attn_W_xproj, L1_attn_W_dt, L1_attn_b_dt, L1_attn_W_out, L1_attn_ln_g, L1_attn_ln_b)
    x = x + 0.5 * _L1_ffn_ref(_layernorm(x, axis=-1), L1_ffn_router_w, L1_ffn_gate_w, L1_ffn_up_w, L1_ffn_down_w, L1_ffn_shared_gate_w, L1_ffn_shared_up_w, L1_ffn_shared_down_w)
    return x

_drawn_inputs = setup_inputs


def setup_inputs(seed=0):
    import zlib

    import numpy as np

    out = dict(_drawn_inputs(seed))
    spreads = {'L0_attn_bq': (0.0, 0.8),
     'L0_attn_bk': (0.0, 0.8),
     'L0_attn_bv': (0.0, 0.684),
     'L0_attn_bl': (0.0, 0.1),
     'L0_attn_bo': (0.0, 0.1),
     'L0_ffn_b1': (0.0, 0.1),
     'L0_ffn_b2': (0.0, 0.1),
     'L1_attn_ln_g': (1.0, 0.6),
     'L1_attn_ln_b': (0.0, 0.8)}
    factors = {'L0_attn_Wq': 8.0,
     'L0_attn_Wk': 8.0,
     'L0_attn_Wv': 8.0,
     'L0_attn_Wl': 5.9,
     'L1_attn_W_in': 8.0,
     'L1_attn_W_conv': 8.0,
     'L1_attn_W_xproj': 8.0,
     'L1_attn_W_dt': 8.0,
     'L1_attn_W_out': 8.0}
    for name, (base, spread) in spreads.items():
        noise = np.random.default_rng([zlib.crc32(name.encode()), seed]).standard_normal(out[name].shape)
        drawn = base * np.exp(spread * noise) if base else spread * noise
        out[name] = jnp.asarray(drawn.astype(out[name].dtype))
    for name, factor in factors.items():
        out[name] = (out[name] * factor).astype(out[name].dtype)
    return out
```

```python
from contextlib import ExitStack

import concourse.bass as bass
from concourse import mybir

ALU = mybir.AluOpType
ACT = mybir.ActivationFunctionType
F32 = mybir.dt.float32
BF16 = mybir.dt.bfloat16
I32 = mybir.dt.int32
AX_X = mybir.AxisListType.X

P = 128
B, T, E = 8, 512, 128
TILES = T // P
NE0, HID = 8, 512
HC = HID // P
NE1, FE = 16, 64
PAIRS = NE1 // 2
H, HD = 16, 8
HG = 4
DI, DS, DTR = 256, 16, 64
DC = DI // P
EPS = 1e-5
ARENA = 31200
BIG = 1e30
RSQRT_MAGIC = float(0x5F3759DF)

V_B1, V_B2 = 0, 32
V_BQ, V_BK, V_BV, V_BL = 40, 41, 42, 43
V_BDT, V_G, V_B = 44, 46, 48
NVEC = 50
N_ROWS, N_WEIGHTS = 9, 24

PHASES = ("moe0", "attn", "moe0", "moe1", "ssm", "moe1")


class Chain:

    def __init__(self, eng, sem, per):
        self.eng, self.sem, self.per, self.k, self.base = eng, sem, per, 0, 0

    def begin(self, n):
        self.base, self.k = n * self.per, 0

    def __call__(self, ins):
        self.k += 1
        ins.then_inc(self.sem, 1)
        self.eng.wait_ge(self.sem, self.base + self.k)

    def end(self):
        assert self.k == self.per, (self.k, self.per)


def build(nc, a, out, phases=PHASES):
    nc.disable_value_cache = True
    with ExitStack() as ctx:
        def sb(name, shape, dt=F32):
            return ctx.enter_context(nc.sbuf_tensor(name, shape, dt))

        def sem(name):
            return ctx.enter_context(nc.semaphore(name))

        bank = [ctx.enter_context(nc.psum_tensor(f"bank{i}", [P, 512], F32)) for i in range(8)]

        x_res = sb("x_res", [P, B * TILES, E])
        xnT = [sb(f"xnT{i}", [P, T]) for i in range(2)]
        xn = sb("xn", [P, TILES, E])
        w1 = sb("w1", [P, NE0, HID])
        w2 = sb("w2", [P, NE0, HC, E])
        wr0 = sb("wr0", [P, NE0])
        gate_w = sb("gate_w", [P, NE1, FE])
        up_w = sb("up_w", [P, NE1, FE])
        down_w = sb("down_w", [P, PAIRS, E])
        sh_g = sb("sh_g", [P, P])
        sh_u = sb("sh_u", [P, P])
        sh_d = sb("sh_d", [P, E])
        wr1 = sb("wr1", [P, NE1])
        ident = sb("ident", [P, P])
        identb = sb("identb", [P, P], BF16)
        first = sb("first", [P, TILES, NE1])
        vec_rows = sb("vec_rows", [NVEC, P])
        vecs = sb("vecs", [P, NVEC])
        wq, wk, wv, wl, wo = [sb(f"w_{k}", [P, P]) for k in ("q", "k", "v", "l", "o")]
        wq_p, wl_p = sb("wq_p", [P, P]), sb("wl_p", [P, P])
        bl_bc = sb("bl_bc", [P, P])
        bo_bc = sb("bo_bc", [P, TILES, P])
        w_in = sb("w_in", [P, 2 * DI])
        w_conv = sb("w_conv", [P, DC, 3])
        w_x = sb("w_x", [P, DC, DTR + 2 * DS + 1])
        w_dt = sb("w_dt", [DTR, DI])
        w_out = sb("w_out", [P, DC, E])
        stats = sb("stats", [P, TILES, 6])
        mv = sb("mv", [P, TILES, 2])
        var = sb("var", [P, TILES])
        rs_y = sb("rs_y", [P, TILES])
        rs_t = sb("rs_t", [P, TILES])
        lg = sb("lg", [P, TILES, NE1])
        rt_a = sb("rt_a", [P, TILES, NE1])
        rt_b = sb("rt_b", [P, TILES, NE1])
        rt_c = sb("rt_c", [P, TILES, NE1])
        rt_th = sb("rt_th", [P, TILES, NE1])
        rt_m = sb("rt_m", [P, TILES])
        rt_n = sb("rt_n", [P, TILES])
        coef = sb("coef", [P, TILES, NE1])
        arena = sb("arena", [P, ARENA])

        used = {"at": 0}

        def view(rows, cols, dt=F32):
            n = cols * (2 if dt == BF16 else 4) // 4
            at = used["at"]
            used["at"] = at + n
            assert used["at"] <= ARENA, used
            v = arena[0:rows, at:at + n]
            return v.bitcast(BF16) if dt == BF16 else v


        x_first, x_rest, w_loaded = sem("x_first"), sem("x_rest"), sem("w_loaded")
        rows_loaded, ident_ready, tables_ready = sem("rows_loaded"), sem("ident_ready"), sem("tables_ready")
        pool_chain, vecs_ps, vecs_ready = sem("pool_chain"), sem("vecs_ps"), sem("vecs_ready")
        x_upd = sem("x_upd")
        xn_ready, xnT_ps, xnT_ready = sem("xn_ready"), sem("xnT_ps"), sem("xnT_ready")
        ln_chain = sem("ln_chain")
        stored = sem("stored")
        LN_STEPS = 14

        def x_of(b):
            return x_res[:, bass.ds(b * TILES, TILES), :]

        def need(eng, semaphore, value):
            if not isinstance(value, int) or value > 0:
                eng.wait_ge(semaphore, value)

        def prior(b):
            return b - 1 if isinstance(b, int) else (b * (B - 3) + 1) // (B - 2)

        def flat(v):
            return v.rearrange("p a b -> p (a b)")

        def rsqrt(chain, v):
            chain(nc.vector.tensor_scalar(rs_t[:].bitcast(I32), v.bitcast(I32), 1, None, ALU.arith_shift_right))
            chain(nc.vector.tensor_scalar(rs_y[:].bitcast(I32), rs_t[:].bitcast(I32), -1.0, RSQRT_MAGIC, ALU.mult, ALU.add))
            for _ in range(3):
                chain(nc.vector.tensor_tensor(rs_t[:], rs_y[:], rs_y[:], ALU.mult))
                chain(nc.vector.scalar_tensor_tensor(out=rs_t[:], in0=rs_t[:], scalar=-0.5, in1=v, op0=ALU.mult, op1=ALU.mult))
                chain(nc.vector.scalar_tensor_tensor(out=rs_y[:], in0=rs_t[:], scalar=1.5, in1=rs_y[:], op0=ALU.add, op1=ALU.mult))

        def norm_dve(v, f, b):
            chain = Chain(v, ln_chain, LN_STEPS)
            chain.begin(f)
            x = x_of(b)
            need(v, xn_ready, f)
            if isinstance(f, int):
                need(v, x_upd, f - B + 1)
            for i in range(TILES):
                last = nc.vector.bn_stats(stats[:, i, :], x[:, i, :])
            chain(last)
            nc.vector.nop(nofuse=True)
            for i in range(TILES):
                last = nc.vector.bn_aggr(mv[:, i, :], stats[:, i, :])
            chain(last)
            chain(nc.vector.tensor_scalar(var[:], mv[:, :, 1], EPS, None, ALU.add))
            rsqrt(chain, var[:])
            chain.end()
            need(v, xnT_ps, f)
            for i in range(TILES):
                last = nc.vector.tensor_scalar(xn[:, i, :], x[:, i, :], mv[:, i, 0:1], rs_y[:, i:i + 1], ALU.subtract, ALU.mult)
            last.then_inc(xn_ready, 1)

        def norm_pe(f):
            need(nc.tensor, xn_ready, f + 1)
            need(nc.tensor, xnT_ready, f)
            for i in range(TILES):
                last = nc.tensor.transpose(bank[7][:, i * P:(i + 1) * P], xn[:, i, :], ident[:])
            last.then_inc(xnT_ps, 1)

        def norm_act(f, par):
            nc.scalar.wait_ge(xnT_ps, f + 1)
            nc.scalar.copy(xnT[par][:], bank[7][:]).then_inc(xnT_ready, 1)

        def after_phases(eng, n):
            if n:
                eng.wait_ge(x_upd, B * n)

        def sequences(eng, body, c0=0):
            body(c0, 0, True, False)
            with eng.Fori(0, (B - 2) // 2) as i:
                body(2 * i + (c0 + 1), 1, False, False)
                body(2 * i + (c0 + 2), 0, False, False)
            body(c0 + B - 1, 1, False, True)

        moe_sems = {}

        def moe_phase(n, kind):
            ne = NE0 if kind == 0 else NE1
            c0 = B * phases[:n].count(phases[n])
            f0 = B * n - c0
            names = ("lg_ready", "z_ready", "th_ready", "coef_ready", "ct_ps", "ct_sb", "row_loaded", "bc_ready", "bc_half",
                     "up_ready", "act_done", "down_done", "y_used", "mixed", "gated", "hid_ready", "acc_ready", "back_ready",
                     "rt_chain")
            if kind not in moe_sems:
                moe_sems[kind] = {k: sem(f"moe{kind}_{k}") for k in names}
            s = moe_sems[kind]
            used["at"] = 0
            coefB = view(P, 8 * T).rearrange("p (e t) -> p e t", e=8)
            row = view(1, NE1 * T).rearrange("p (e t) -> p e t", e=NE1)
            coefT = view(NE1, T)
            hid = [view(P, T) for _ in range(4)]
            silu = [view(P, T) for _ in range(2)]
            tmp = [view(P, T) for _ in range(2)]
            acc = [view(P, T) for _ in range(2)]
            wr = wr0 if kind == 0 else wr1
            RT_STEPS = 18
            ROW_DMAS = 1 if kind == 0 else 2
            coefB_used = s["y_used"] if kind == 0 else s["hid_ready"]
            wide = lambda m: m[:].unsqueeze(2).to_broadcast([P, TILES, ne])

            def router_pe(b, par):
                nc.tensor.wait_ge(xnT_ready, f0 + b + 1)
                need(nc.tensor, s["ct_sb"], b)
                if not isinstance(b, int) or b > 1:
                    nc.tensor.wait_ge(x_upd, f0 + b - 1)
                for i in range(TILES):
                    last = nc.tensor.matmul(bank[6][:, i * ne:(i + 1) * ne], xnT[par][:, i * P:(i + 1) * P], wr[:, 0:ne],
                                            start=True, stop=True)
                last.then_inc(s["lg_ready"], 1)

            def coef_pe(b):
                nc.tensor.wait_ge(s["coef_ready"], b + 1)
                for i in range(TILES):
                    last = nc.tensor.transpose(bank[6][0:ne, i * P:(i + 1) * P], coef[:, i, 0:ne], ident[:])
                last.then_inc(s["ct_ps"], 1)

            def router_act(b):
                nc.scalar.wait_ge(s["z_ready"], b + 1)
                nc.scalar.activation(rt_th[:, :, 0:ne], lg[:, :, 0:ne], ACT.Tanh, scale=0.5).then_inc(s["th_ready"], 1)

            def coef_act(b):
                nc.scalar.wait_ge(s["ct_ps"], b + 1)
                need(nc.scalar, s["row_loaded"], 16 * ROW_DMAS * b)
                nc.scalar.copy(coefT[0:ne, :], bank[6][0:ne, :]).then_inc(s["ct_sb"], 1)

            def router_dve(v, b):
                chain = Chain(v, s["rt_chain"], RT_STEPS)
                chain.begin(b)
                ps = bank[6][:, 0:TILES * ne].rearrange("p (i e) -> p i e", i=TILES)
                z, q, r, sel, th = (m[:, :, 0:ne] for m in (lg, rt_a, rt_b, rt_c, rt_th))
                v.wait_ge(s["lg_ready"], b + 1)
                need(v, s["coef_ready"], b)
                chain(nc.vector.tensor_reduce(rt_m[:], ps, AX_X, ALU.max))
                nc.vector.tensor_tensor(z, ps, wide(rt_m), ALU.subtract).then_inc(s["z_ready"], 1)
                v.wait_ge(s["z_ready"], b + 1)
                chain(nc.vector.tensor_scalar(q, z, 0.0, None, ALU.is_equal))
                chain(nc.vector.tensor_tensor(q, q, first[:, :, 0:ne], ALU.mult))
                chain(nc.vector.tensor_reduce(rt_n[:], q, AX_X, ALU.max))
                chain(nc.vector.tensor_tensor(sel, q, wide(rt_n), ALU.is_equal))
                chain(nc.vector.scalar_tensor_tensor(out=r, in0=sel, scalar=-BIG, in1=z, op0=ALU.mult, op1=ALU.add))
                chain(nc.vector.tensor_reduce(rt_m[:], r, AX_X, ALU.max))
                chain(nc.vector.tensor_tensor(q, r, wide(rt_m), ALU.is_equal))
                chain(nc.vector.tensor_tensor(q, q, first[:, :, 0:ne], ALU.mult))
                chain(nc.vector.tensor_reduce(rt_n[:], q, AX_X, ALU.max))
                chain(nc.vector.tensor_tensor(q, q, wide(rt_n), ALU.is_equal))
                chain(nc.vector.tensor_tensor(sel, q, sel, ALU.add))
                v.wait_ge(s["th_ready"], b + 1)
                chain(nc.vector.tensor_scalar(r, th, -1.0, 1.0, ALU.mult, ALU.add))
                chain(nc.vector.reciprocal(r, r))
                chain(nc.vector.scalar_tensor_tensor(out=r, in0=th, scalar=1.0, in1=r, op0=ALU.add, op1=ALU.mult))
                chain(nc.vector.tensor_reduce(rt_n[:], r, AX_X, ALU.add))
                chain(nc.vector.reciprocal(rt_m[:], rt_n[:]))
                chain(nc.vector.tensor_tensor(r, r, sel, ALU.mult))
                chain.end()
                need(v, s["ct_ps"], b)
                nc.vector.scalar_tensor_tensor(out=coef[:, :, 0:ne], in0=r, scalar=0.5, in1=wide(rt_m), op0=ALU.mult,
                                               op1=ALU.mult).then_inc(s["coef_ready"], 1)

            def row_sp(b, par, first_, last_):
                nc.sync.wait_ge(s["ct_sb"], b + 1)
                need(nc.sync, s["bc_ready"], 8 * b)
                for k in range(ROW_DMAS):
                    nc.sync.dma_start(row[0:1, 8 * k:8 * k + 8, :], coefT[k:ne:ROW_DMAS, :]).then_inc(s["row_loaded"], 16)

            def broadcast_pool(b, par, first_, last_):
                nc.gpsimd.wait_ge(s["row_loaded"], 16 * ROW_DMAS * (b + 1))
                need(nc.gpsimd, coefB_used, 8 * b)
                nc.gpsimd.nop(nofuse=True)
                for e in range(8):
                    if kind == 1:
                        nc.gpsimd.partition_broadcast(coefB[:, e, :], row[0:1, 8 + e, :]).then_inc(s["bc_half"], 1)
                        nc.gpsimd.wait_ge(s["bc_half"], 8 * b + e + 1)
                        nc.gpsimd.nop(nofuse=True)
                        nc.gpsimd.partition_broadcast(coefB[0:FE, e, :], row[0:1, e, :], channels=FE).then_inc(s["bc_ready"], 1)
                    else:
                        nc.gpsimd.partition_broadcast(coefB[:, e, :], row[0:1, e, :]).then_inc(s["bc_ready"], 1)

            def back_pe(b, par):
                nc.tensor.wait_ge(s["ct_sb"], b + 1)
                if kind == 0:
                    nc.tensor.wait_ge(s["mixed"], (NE0 - 1) * (b + 1))
                else:
                    nc.tensor.wait_ge(s["acc_ready"], b + 1)
                for i in range(TILES):
                    last = nc.tensor.transpose(bank[6][:, i * P:(i + 1) * P], acc[par][:, i * P:(i + 1) * P], ident[:])
                last.then_inc(s["back_ready"], 1)

            def back_dve(v, b):
                v.wait_ge(s["back_ready"], b + 1)
                nc.vector.tensor_tensor(flat(x_of(b % B)), bank[6][:], flat(x_of(b % B)), ALU.add).then_inc(x_upd, 1)

            more = n + 1 < len(phases)

            CH = NE0 * HC

            def up0(b, par, k):
                need(nc.tensor, s["act_done"], CH * b + k - 3)
                nc.tensor.matmul(bank[k % 4][:], w1[:, k // HC, (k % HC) * P:(k % HC + 1) * P], xnT[par][:],
                                 start=True, stop=True).then_inc(s["up_ready"], 1)

            def down0(b, k):
                e, c = k // HC, k % HC
                nc.tensor.wait_ge(s["act_done"], CH * b + k + 1)
                if c == 0:
                    need(nc.tensor, s["y_used"], NE0 * b + e - 1)
                nc.tensor.matmul(bank[4 + e % 2][:], w2[:, e, c, :], hid[k % 4][:], start=(c == 0),
                                 stop=(c == HC - 1)).then_inc(s["down_done"], 1)

            def gelu0(b, k):
                nc.scalar.wait_ge(s["up_ready"], CH * b + k + 1)
                need(nc.scalar, s["down_done"], CH * b + k - 3)
                nc.scalar.activation(hid[k % 4][:], bank[k % 4][:], ACT.Gelu_apprx_tanh,
                                     bias=vecs[:, V_B1 + k:V_B1 + k + 1]).then_inc(s["act_done"], 1)

            def combine0(v, b, par, e):
                v.wait_ge(s["down_done"], CH * b + HC * (e + 1))
                v.wait_ge(s["bc_ready"], NE0 * b + e + 1)
                into = acc[par] if e == 0 else tmp[e % 2]
                if e:
                    need(v, s["mixed"], (NE0 - 1) * b + (e - 2 if e > 2 else 1 - e))
                nc.vector.scalar_tensor_tensor(out=into[:], in0=bank[4 + e % 2][:], scalar=vecs[:, V_B2 + e:V_B2 + e + 1],
                                               in1=coefB[:, e, :], op0=ALU.add, op1=ALU.mult).then_inc(s["y_used"], 1)
                if e:
                    v.wait_ge(s["y_used"], NE0 * b + e + 1)
                    if e > 1:
                        v.wait_ge(s["mixed"], (NE0 - 1) * b + e - 1)
                    nc.vector.tensor_tensor(acc[par][:], tmp[e % 2][:], acc[par][:], ALU.add).then_inc(s["mixed"], 1)

            def pe0(b, par, first_, last_):
                for k in range(CH):
                    up0(b, par, k)
                    if k >= 2:
                        down0(b, k - 2)
                    elif not first_:
                        down0(b - 1, CH - 2 + k)
                    if k == 10 and not first_:
                        back_pe(b - 1, 1 - par)
                    if k == 16 and (more or not last_):
                        norm_pe(f0 + b + 1)
                    if k == 22 and not last_:
                        router_pe(b + 1, 1 - par)
                    if k == 26 and not last_:
                        coef_pe(b + 1)

            def act0(b, par, first_, last_):
                for k in range(CH):
                    gelu0(b, k)
                    if k == 17 and (more or not last_):
                        norm_act(f0 + b + 1, 1 - par)
                    if k == 23 and not last_:
                        router_act(b + 1)
                    if k == 27 and not last_:
                        coef_act(b + 1)

            def dve0(v, b, par, first_, last_):
                if not first_:
                    combine0(v, b - 1, 1 - par, NE0 - 1)
                for e in range(NE0 - 1):
                    combine0(v, b, par, e)
                    if e == 1 and not first_:
                        back_dve(v, b - 1)
                    if e == 2 and (more or not last_):
                        norm_dve(v, f0 + b + 1, (b + 1) % B)
                    if e == 4 and not last_:
                        router_dve(v, b + 1)

            IT = PAIRS + 1

            def up1(b, par, j):
                q = (par + j) % 2
                need(nc.tensor, s["gated"], IT * b + j - 1)
                g, u = (sh_g[:], sh_u[:]) if j == 0 else (flat(gate_w[:, 2 * j - 2:2 * j, :]), flat(up_w[:, 2 * j - 2:2 * j, :]))
                nc.tensor.matmul(bank[2 * q][:], g, xnT[par][:], start=True, stop=True)
                nc.tensor.matmul(bank[2 * q + 1][:], u, xnT[par][:], start=True, stop=True).then_inc(s["up_ready"], 1)

            def down1(b, par, j):
                if j == 0:
                    nc.tensor.wait_ge(s["gated"], IT * b + 1)
                    need(nc.tensor, s["acc_ready"], b - 1 if c0 else prior(b))
                else:
                    nc.tensor.wait_ge(s["hid_ready"], PAIRS * b + j)
                w = sh_d[:] if j == 0 else down_w[:, j - 1, :]
                nc.tensor.matmul(bank[4 + par][:], w, hid[j % 3][:], start=(j == 0), stop=(j == IT - 1)).then_inc(s["down_done"], 1)

            def silu1(b, par, j):
                q = (par + j) % 2
                nc.scalar.wait_ge(s["up_ready"], IT * b + j + 1)
                nc.scalar.activation(silu[q][:], bank[2 * q][:], ACT.Silu).then_inc(s["act_done"], 1)

            def gate1(v, b, par, j):
                q = (par + j) % 2
                v.wait_ge(s["act_done"], IT * b + j + 1)
                if j == 0:
                    need(v, s["down_done"], IT * b + j - 2)
                    nc.vector.scalar_tensor_tensor(out=hid[0][:], in0=silu[q][:], scalar=0.5, in1=bank[2 * q + 1][:],
                                                   op0=ALU.mult, op1=ALU.mult).then_inc(s["gated"], 1)
                    return
                need(v, s["hid_ready"], PAIRS * b + (j - 2 if j > 2 else 1 - j))
                nc.vector.tensor_tensor(tmp[q][:], silu[q][:], bank[2 * q + 1][:], ALU.mult).then_inc(s["gated"], 1)
                v.wait_ge(s["gated"], IT * b + j + 1)
                v.wait_ge(s["bc_ready"], PAIRS * b + j)
                need(v, s["down_done"], IT * b + j - 2)
                nc.vector.tensor_tensor(hid[j % 3][:], tmp[q][:], coefB[:, j - 1, :], ALU.mult).then_inc(s["hid_ready"], 1)

            def sum1(v, b, par):
                v.wait_ge(s["down_done"], IT * (b + 1))
                nc.vector.tensor_copy(acc[par][:], bank[4 + par][:]).then_inc(s["acc_ready"], 1)

            def pe1(b, par, first_, last_):
                for j in range(IT):
                    up1(b, par, j)
                    if j >= 2:
                        down1(b, par, j - 2)
                    elif not first_:
                        down1(b - 1, 1 - par, IT - 2 + j)
                    if j == 3 and not first_:
                        back_pe(b - 1, 1 - par)
                    if j == 5 and (more or not last_):
                        norm_pe(f0 + b + 1)
                    if j == 6 and not last_:
                        router_pe(b + 1, 1 - par)
                if not last_:
                    coef_pe(b + 1)

            def act1(b, par, first_, last_):
                for j in range(IT):
                    silu1(b, par, j)
                    if j == 5 and (more or not last_):
                        norm_act(f0 + b + 1, 1 - par)
                    if j == 6 and not last_:
                        router_act(b + 1)
                if not last_:
                    coef_act(b + 1)

            def dve1(v, b, par, first_, last_):
                for j in range(IT):
                    gate1(v, b, par, j)
                    if j == 1 and not first_:
                        sum1(v, b - 1, 1 - par)
                    if j == 2 and not first_:
                        back_dve(v, b - 1)
                    if j == 2 and (more or not last_):
                        norm_dve(v, f0 + b + 1, (b + 1) % B)
                    if j == 5 and not last_:
                        router_dve(v, b + 1)

            def tensor(t):
                after_phases(t, n)
                router_pe(c0, 0)
                coef_pe(c0)
                sequences(t, pe0 if kind == 0 else pe1, c0)
                if kind == 0:
                    down0(c0 + B - 1, CH - 2)
                    down0(c0 + B - 1, CH - 1)
                else:
                    down1(c0 + B - 1, 1, IT - 2)
                    down1(c0 + B - 1, 1, IT - 1)
                back_pe(c0 + B - 1, 1)

            def scalar(c):
                after_phases(c, n)
                router_act(c0)
                coef_act(c0)
                sequences(c, act0 if kind == 0 else act1, c0)

            def vector(v):
                after_phases(v, n)
                router_dve(v, c0)
                sequences(v, lambda b, par, f, l: (dve0 if kind == 0 else dve1)(v, b, par, f, l), c0)
                if kind == 0:
                    combine0(v, c0 + B - 1, 1, NE0 - 1)
                else:
                    sum1(v, c0 + B - 1, 1)
                back_dve(v, c0 + B - 1)

            def gpsimd(g):
                after_phases(g, n)
                sequences(g, broadcast_pool, c0)

            def sync(q):
                after_phases(q, n)
                sequences(q, row_sp, c0)

            return {"tensor": tensor, "scalar": scalar, "vector": vector, "gpsimd": gpsimd, "sync": sync}

        def attn_phase(n):
            f0 = B * n
            names = ("q_ps", "kk_ps", "vv_ps", "k_ps", "v_ps", "q_sb", "kk_sb", "vv_sb", "k_sb", "v_sb", "q_split", "k_split",
                     "q_chain", "k_chain", "zeroed", "m_consts", "qk_ones", "v9_ready", "mx_ready", "mx_read", "m_chain",
                     "m_split", "mT_ps", "mT_sb", "st_ready", "exp_done", "av_done", "o_sb", "oT_ps", "o_tok", "o_chain",
                     "otT_ps", "ot_sb", "z_ready", "x_bo")
            s = {k: sem(f"p{n}_{k}") for k in names}
            saved = {c: sem(f"p{n}_{c}_saved") for c in "qk"}
            ld = [[sem(f"p{n}_qk_loaded{i}{g}") for g in range(H // HG)] for i in range(2)]
            m_ld = [[sem(f"p{n}_m_loaded{i}{g}") for g in range(H // HG)] for i in range(2)]
            used["at"] = 0
            qa = [view(P, H * T, BF16).rearrange("p (h t) -> p h t", h=H) for _ in range(2)]
            ka = [view(P, H * T, BF16).rearrange("p (h t) -> p h t", h=H) for _ in range(2)]
            v_all = view(P, B * TILES * H * (HD + 1)).rearrange("p (n h d) -> p n h d", h=H, d=HD + 1)
            v9 = [view(P, TILES * H * (HD + 1)).rearrange("p (n h d) -> p n h d", h=H, d=HD + 1) for _ in range(2)]
            shared_at = used["at"]
            q_sb, kk_sb, vv_sb, k_sb = (view(P, T) for _ in range(4))
            rest = {"q": view(P, T), "k": view(P, T)}
            parts = {c: [view(P, 3 * T, BF16).rearrange("p (j t) -> p j t", j=3) for _ in range(2)] for c in "qk"}
            used["at"] = shared_at
            probs = [view(P, HG * T).rearrange("p (h t) -> p h t", h=HG) for _ in range(2)]
            o_sb = view(P, T)
            o_tok = view(P, T).rearrange("p (i e) -> p i e", i=TILES)
            ot_sb = view(P, T)
            xbo = view(P, T)
            mneg = view(P, TILES * H).rearrange("p (i h) -> p i h", i=TILES)
            mrest = view(P, TILES * HG).rearrange("p (i h) -> p i h", i=TILES)
            mparts = view(P, TILES * 3 * HG, BF16).rearrange("p (i j h) -> p i j h", i=TILES, j=3)
            rec = view(P, TILES * HG).rearrange("p (i h) -> p i h", i=TILES)
            mT = [[view(3 * HG, T, BF16) for _ in range(H // HG)] for _ in range(2)]
            zero3, ones3 = view(3, T, BF16), view(3, T, BF16)
            scratch = {c: nc.dram_tensor(f"p{n}_{c}_parts", (B, 3, P, T), BF16, kind="Internal").ap() for c in "qk"}
            scale = float(HD) ** -0.5

            STEPS = (H // HG) * TILES

            def pe_a(b, par, first_, last_):
                x = xnT[par][:]
                nc.tensor.wait_ge(xnT_ready, f0 + b + 1)
                for i, (w, ps, sb_) in enumerate(((wq_p[:], "q_ps", "q_sb"), (wk[:], "kk_ps", "kk_sb"), (wv[:], "vv_ps", "vv_sb"))):
                    need(nc.tensor, s[sb_], b)
                    nc.tensor.matmul(bank[i][:], w, x, start=True, stop=True).then_inc(s[ps], 1)
                nc.tensor.wait_ge(s["kk_sb"], b + 1)
                need(nc.tensor, s["k_sb"], b)
                nc.tensor.matmul(bank[3][:], wl_p[:], kk_sb[:], start=True, stop=True).then_inc(s["k_ps"], 1)
                nc.tensor.wait_ge(s["vv_sb"], b + 1)
                need(nc.tensor, s["v_sb"], b)
                for i in range(TILES):
                    last = nc.tensor.matmul(bank[4][:, i * P:(i + 1) * P], vv_sb[:, i * P:(i + 1) * P], wl[:], start=True, stop=True)
                last.then_inc(s["v_ps"], 1)
                if not last_:
                    norm_pe(f0 + b + 1)

            def act_a(b, par, first_, last_):
                def biased(i, ps, dst, at, done, free, count):
                    nc.scalar.wait_ge(s[ps], b + 1)
                    need(nc.scalar, s[free], count)
                    nc.scalar.activation(dst[:], bank[i][:], ACT.Identity, bias=vecs[:, at:at + 1]).then_inc(s[done], 1)
                biased(1, "kk_ps", kk_sb, V_BK, "kk_sb", "k_ps", b)
                biased(2, "vv_ps", vv_sb, V_BV, "vv_sb", "v_ps", b)
                biased(0, "q_ps", q_sb, V_BQ, "q_sb", "q_split", b)
                biased(3, "k_ps", k_sb, V_BL, "k_sb", "k_split", b)
                if not last_:
                    norm_act(f0 + b + 1, 1 - par)

            def split(eng, c, src, b, par):
                eng.wait_ge(s[c + "_sb"], b + 1)
                need(eng, saved[c], 16 * b)
                chain = Chain(eng, s[c + "_chain"], 3)
                chain.begin(b)
                p_, r = parts[c][par], rest[c]
                eng.nop(nofuse=True)
                chain(eng.tensor_copy(p_[:, 0, :], src[:]))
                chain(eng.tensor_tensor(r[:], src[:], p_[:, 0, :], ALU.subtract))
                eng.nop(nofuse=True)
                chain(eng.tensor_copy(p_[:, 1, :], r[:]))
                chain.end()
                eng.tensor_tensor(p_[:, 2, :], r[:], p_[:, 1, :], ALU.subtract).then_inc(s[c + "_split"], 1)

            def dve_a(v, b, par, first_, last_):
                if not last_:
                    norm_dve(v, f0 + b + 1, b + 1)
                v.wait_ge(s["v_ps"], b + 1)
                nc.vector.tensor_tensor(
                    v_all[:, bass.ds(b * TILES, TILES), :, 0:HD], bank[4][:].rearrange("p (i h d) -> p i h d", i=TILES, d=HD),
                    bl_bc[:].rearrange("p (h d) -> p h d", d=HD).unsqueeze(1).to_broadcast([P, TILES, H, HD]),
                    ALU.add).then_inc(s["v_sb"], 1)
                need(v, s["q_split"], b)
                split(nc.vector, "q", q_sb, b, par)

            def pool_a(b, par, first_, last_):
                need(nc.gpsimd, s["k_split"], b)
                split(nc.gpsimd, "k", k_sb, b, par)

            def sp_a(b, par, first_, last_):
                for c in "qk":
                    nc.sync.wait_ge(s[c + "_split"], b + 1)
                    nc.sync.dma_start(scratch[c][bass.ds(b, 1)].rearrange("o j p t -> p (o j) t"), parts[c][par][:]).then_inc(saved[c], 16)

            NLD = 7
            M0, M1 = 6 * HD, 6 * HD + 3
            GB = H // HG

            def load(b, par, g):
                q, k = (scratch[c][bass.ds(b, 1)].rearrange("o j (d h) t -> (o j d) h t", h=H)[:, g * HG:(g + 1) * HG, :] for c in "qk")
                hs = slice(g * HG, (g + 1) * HG)
                for r, j, w in ((0, 0, 3), (3, 1, 2), (5, 2, 1)):
                    src = q[j * HD:(j + 1) * HD].unsqueeze(0).to_broadcast([w, HD, HG, T])
                    nc.sync.dma_start(qa[par][r * HD:(r + w) * HD, hs, :], src).then_inc(ld[par][g], 16)
                for r, j, w in ((0, 0, 3), (3, 0, 2), (5, 0, 1)):
                    nc.sync.dma_start(ka[par][r * HD:(r + w) * HD, hs, :], k[j * HD:(j + w) * HD]).then_inc(ld[par][g], 16)
                nc.sync.dma_start(qa[par][M0:M1, hs, :], zero3.unsqueeze(1).to_broadcast([3, HG, T])).then_inc(ld[par][g], 16)

            def max_pe(b, par, t):
                h, i = t // TILES, t % TILES
                if t % (HG * TILES) == 0:
                    nc.tensor.wait_ge(ld[par][h // HG], 16 * NLD * (b // 2 + 1))
                need(nc.tensor, s["mx_read"], H * TILES * b + t - 1)
                nc.tensor.matmul(bank[t % 2][:], qa[par][:, h, i * P:(i + 1) * P], ka[par][:, h, :], start=True, stop=True).then_inc(s["mx_ready"], 1)

            def max_dve(v, b, t):
                h, i = t // TILES, t % TILES
                v.wait_ge(s["mx_ready"], H * TILES * b + t + 1)
                nc.vector.tensor_reduce(mneg[:, i, h:h + 1], bank[t % 2][:], AX_X, ALU.max, negate=True).then_inc(s["mx_read"], 1)

            def msplit_dve(v, b, g):
                chain = Chain(v, s["m_chain"], 3)
                chain.begin(b * (H // HG) + g)
                v.wait_ge(s["mx_read"], H * TILES * b + HG * TILES * (g + 1))
                need(v, s["mT_ps"], b * (H // HG) + g)
                m = mneg[:, :, g * HG:(g + 1) * HG]
                chain(nc.vector.tensor_copy(mparts[:, :, 0, :], m))
                chain(nc.vector.tensor_tensor(mrest[:], m, mparts[:, :, 0, :], ALU.subtract))
                chain(nc.vector.tensor_copy(mparts[:, :, 1, :], mrest[:]))
                chain.end()
                nc.vector.tensor_tensor(mparts[:, :, 2, :], mrest[:], mparts[:, :, 1, :], ALU.subtract).then_inc(s["m_split"], 1)

            def mT_pe(b, g):
                nc.tensor.wait_ge(s["m_split"], b * GB + g + 1)
                for i in range(TILES):
                    last = nc.tensor.transpose(bank[7][:].bitcast(BF16)[0:3 * HG, i * P:(i + 1) * P],
                                               mparts[:, i, :, :].rearrange("p j h -> p (j h)"), identb[:])
                last.then_inc(s["mT_ps"], 1)

            def mT_act(b, par, g):
                nc.scalar.wait_ge(s["mT_ps"], b * GB + g + 1)
                nc.scalar.copy(mT[par][g][:], bank[7][:].bitcast(BF16)[0:3 * HG, 0:T]).then_inc(s["mT_sb"], 1)

            def m_sp(b, par, g):
                nc.sync.wait_ge(s["mT_sb"], b * GB + g + 1)
                nc.sync.dma_start(qa[par][M0:M1, g * HG:(g + 1) * HG, :], mT[par][g][:]).then_inc(m_ld[par][g], 16)

            def st_pe(b, par, st, hh):
                g, kt = st // TILES, st % TILES
                t = HG * st + hh
                if kt == 0 and hh == 0:
                    nc.tensor.wait_ge(m_ld[par][g], 16 * ((b // 2) + 1))
                need(nc.tensor, s["exp_done"], H * TILES * b + t - 3)
                nc.tensor.matmul(bank[2 + t % 4][:], ka[par][:, g * HG + hh, kt * P:(kt + 1) * P], qa[par][:, g * HG + hh, :],
                                 start=True, stop=True).then_inc(s["st_ready"], 1)

            def exp_act(b, st, hh):
                t = HG * st + hh
                if hh == 0:
                    need(nc.scalar, s["av_done"], STEPS * b + st - 1)
                nc.scalar.wait_ge(s["st_ready"], H * TILES * b + t + 1)
                nc.scalar.activation(probs[st % 2][:, hh, :], bank[2 + t % 4][:], ACT.Exp, scale=scale).then_inc(s["exp_done"], 1)

            def av_pe(b, par, st):
                g, kt = st // TILES, st % TILES
                nc.tensor.wait_ge(s["exp_done"], H * TILES * b + HG * (st + 1))
                if st == 0:
                    nc.tensor.wait_ge(s["v9_ready"], b + 1)
                if kt == 0:
                    need(nc.tensor, s["o_sb"], GB * b + g)
                for hh in range(HG):
                    last = nc.tensor.matmul(bank[6][32 * hh:32 * hh + HD + 1, :], v9[par][:, kt, g * HG + hh, :], probs[st % 2][:, hh, :],
                                            start=(kt == 0), stop=(kt == TILES - 1))
                last.then_inc(s["av_done"], 1)

            def o_act(b, g):
                nc.scalar.wait_ge(s["av_done"], STEPS * b + TILES * (g + 1))
                need(nc.scalar, s["oT_ps"], GB * b + g)
                nc.scalar.copy(o_sb[:], bank[6][:]).then_inc(s["o_sb"], 1)

            def o_pe(b, g):
                nc.tensor.wait_ge(s["o_sb"], GB * b + g + 1)
                for i in range(TILES):
                    last = nc.tensor.transpose(bank[7][:, i * P:(i + 1) * P], o_sb[:, i * P:(i + 1) * P], ident[:])
                last.then_inc(s["oT_ps"], 1)

            def o_dve(v, b, g):
                v.wait_ge(s["oT_ps"], GB * b + g + 1)
                if g == 0:
                    need(v, s["otT_ps"], b)
                o = bank[7][:].rearrange("p (i h c) -> p i h c", i=TILES, h=HG)
                need(v, s["o_tok"], GB * b + g)
                nc.vector.reciprocal(rec[:], o[:, :, :, HD]).then_inc(s["o_chain"], 1)
                v.wait_ge(s["o_chain"], GB * b + g + 1)
                nc.vector.tensor_tensor(
                    o_tok[:, :, g * HG * HD:(g + 1) * HG * HD].rearrange("p i (h d) -> p i h d", h=HG), o[:, :, :, 0:HD],
                    rec[:].unsqueeze(3).to_broadcast([P, TILES, HG, HD]), ALU.mult).then_inc(s["o_tok"], 1)

            def ot_pe(b):
                nc.tensor.wait_ge(s["o_tok"], GB * (b + 1))
                for i in range(TILES):
                    last = nc.tensor.transpose(bank[7][:, i * P:(i + 1) * P], o_tok[:, i, :], ident[:])
                last.then_inc(s["otT_ps"], 1)

            def ot_act(b):
                nc.scalar.wait_ge(s["otT_ps"], b + 1)
                nc.scalar.copy(ot_sb[:], bank[7][:]).then_inc(s["ot_sb"], 1)

            def z_pe(b):
                nc.tensor.wait_ge(s["ot_sb"], b + 1)
                for i in range(TILES):
                    last = nc.tensor.matmul(bank[7][:, i * P:(i + 1) * P], ot_sb[:, i * P:(i + 1) * P], wo[:], start=True, stop=True)
                last.then_inc(s["z_ready"], 1)

            def xbo_pool(b):
                need(nc.gpsimd, x_upd, f0 + b)
                nc.gpsimd.tensor_tensor(xbo[:], flat(x_of(b)), flat(bo_bc[:]), ALU.add).then_inc(s["x_bo"], 1)

            def z_dve(v, b):
                v.wait_ge(s["z_ready"], b + 1)
                v.wait_ge(s["x_bo"], b + 1)
                nc.vector.tensor_tensor(flat(x_of(b)), bank[7][:], xbo[:], ALU.add).then_inc(x_upd, 1)

            def pe_b(b, par, first_, last_):
                for st in range(STEPS):
                    g, kt = st // TILES, st % TILES
                    for hh in range(2):
                        st_pe(b, par, st, hh)
                        if not last_:
                            max_pe(b + 1, 1 - par, HG * st + hh)
                    if st:
                        av_pe(b, par, st - 1)
                    elif not first_:
                        av_pe(b - 1, 1 - par, STEPS - 1)
                    for hh in range(2, HG):
                        st_pe(b, par, st, hh)
                        if not last_:
                            max_pe(b + 1, 1 - par, HG * st + hh)
                    if st == 0:
                        need(nc.tensor, s["o_tok"], GB * b - 1)
                        nc.tensor.wait_ge(s["mT_sb"], GB * b + GB - 1)
                        mT_pe(b, GB - 1)
                    elif kt == 0 and not last_:
                        if g == 1:
                            need(nc.tensor, x_upd, f0 + b)
                        else:
                            nc.tensor.wait_ge(s["o_tok"], GB * b + g - 1)
                        nc.tensor.wait_ge(s["mT_sb"], GB * b + GB + g - 1)
                        mT_pe(b + 1, g - 1)
                    if st == 1 and not first_:
                        nc.tensor.wait_ge(s["mT_sb"], GB * b + GB)
                        o_pe(b - 1, GB - 1)
                    elif st > 1 and kt == 1:
                        if last_:
                            nc.tensor.wait_ge(x_upd, f0 + b)
                            nc.tensor.wait_ge(s["o_tok"], GB * b + g - 1)
                        else:
                            nc.tensor.wait_ge(s["mT_sb"], GB * b + GB + g)
                        o_pe(b, g - 1)
                    if st == 2 and not first_:
                        ot_pe(b - 1)
                    if st == 3 and not first_:
                        z_pe(b - 1)

            def act_b(b, par, first_, last_):
                for st in range(STEPS):
                    g, kt = st // TILES, st % TILES
                    for hh in range(HG):
                        exp_act(b, st, hh)
                        if hh == 1 and kt == 0:
                            if st:
                                o_act(b, g - 1)
                            elif not first_:
                                o_act(b - 1, GB - 1)
                    if kt == 0:
                        if st == 0:
                            mT_act(b, par, GB - 1)
                        elif not last_:
                            mT_act(b + 1, 1 - par, g - 1)
                    if st == 2 and not first_:
                        ot_act(b - 1)

            def dve_b(v, b, par, first_, last_):
                for st in range(STEPS):
                    g, kt = st // TILES, st % TILES
                    if not last_:
                        for hh in range(HG):
                            max_dve(v, b + 1, HG * st + hh)
                    if kt == 3 and not last_:
                        msplit_dve(v, b + 1, g)
                    if kt == 1:
                        if st > 1:
                            o_dve(v, b, g - 1)
                        elif not first_:
                            o_dve(v, b - 1, GB - 1)
                    if st == 3 and not first_:
                        z_dve(v, b - 1)

            def sp_b(b, par, first_, last_):
                m_sp(b, par, GB - 1)
                if last_:
                    return
                for g in range(GB):
                    nc.sync.wait_ge(s["st_ready"], H * TILES * b + HG * TILES * (g + 1))
                    load((b + 2) % B, par, g)
                    if g < GB - 1:
                        m_sp(b + 1, 1 - par, g)

            def pool_b(b, par, first_, last_):
                need(nc.gpsimd, s["av_done"], STEPS * prior(b))
                nc.gpsimd.nop(nofuse=True)
                nc.gpsimd.tensor_copy(v9[par][:].rearrange("p n h d -> p (n h d)"),
                                      v_all[:, bass.ds(b * TILES, TILES), :, :].rearrange("p n h d -> p (n h d)")).then_inc(s["v9_ready"], 1)
                xbo_pool(b)

            def tensor(t):
                after_phases(t, n)
                sequences(t, pe_a)
                nc.tensor.wait_ge(s["k_sb"], B)
                nc.tensor.wait_ge(s["q_sb"], B)
                nc.tensor.wait_ge(s["vv_sb"], B)
                nc.tensor.wait_ge(s["v_sb"], B)
                nc.tensor.wait_ge(s["zeroed"], 6)
                nc.tensor.wait_ge(s["qk_ones"], 32)
                nc.tensor.wait_ge(xnT_ready, f0 + B)
                for t_ in range(H * TILES):
                    max_pe(0, 0, t_)
                    if t_ % (HG * TILES) == HG * TILES - 1 and t_ < H * TILES - 1:
                        need(nc.tensor, s["mT_sb"], t_ // (HG * TILES))
                        mT_pe(0, t_ // (HG * TILES))
                sequences(t, pe_b)
                av_pe(B - 1, 1, STEPS - 1)
                nc.tensor.wait_ge(s["o_tok"], GB * B - 1)
                o_pe(B - 1, GB - 1)
                ot_pe(B - 1)
                for g in range(GB):
                    nc.tensor.wait_ge(ld[0][g], 16 * NLD * (B // 2 + 1))
                z_pe(B - 1)
                norm_pe(f0 + B)

            def scalar(c):
                after_phases(c, n)
                sequences(c, act_a)
                nc.scalar.wait_ge(s["q_split"], B)
                nc.scalar.wait_ge(s["k_split"], B)
                nc.scalar.wait_ge(s["v_ps"], B)
                for c_ in "qk":
                    nc.scalar.wait_ge(saved[c_], 16 * B)
                for g in range(GB - 1):
                    mT_act(0, 0, g)
                sequences(c, act_b)
                o_act(B - 1, GB - 1)
                ot_act(B - 1)
                norm_act(f0 + B, 0)

            def vector(v):
                after_phases(v, n)
                for m in (qa[0], ka[0]):
                    nc.vector.memset(m[:], 0.0).then_inc(s["zeroed"], 1)
                nc.vector.memset(bank[6][:], 0.0).then_inc(s["zeroed"], 1)
                nc.vector.memset(v_all[:, :, :, HD:], 1.0).then_inc(s["zeroed"], 1)
                sequences(v, lambda b, par, f, l: dve_a(v, b, par, f, l))
                for c_ in "qk":
                    v.wait_ge(saved[c_], 16 * B)
                v.wait_ge(s["v_ps"], B)
                v.wait_ge(s["k_split"], B)
                nc.vector.memset(zero3, 0.0).then_inc(s["m_consts"], 1)
                nc.vector.memset(ones3, 1.0).then_inc(s["m_consts"], 1)
                for t_ in range(H * TILES):
                    max_dve(v, 0, t_)
                    if t_ % (HG * TILES) == HG * TILES - 1:
                        msplit_dve(v, 0, t_ // (HG * TILES))
                sequences(v, lambda b, par, f, l: dve_b(v, b, par, f, l))
                o_dve(v, B - 1, GB - 1)
                z_dve(v, B - 1)
                norm_dve(v, f0 + B, 0)

            def gpsimd(g):
                after_phases(g, n)
                for m in (qa[1], ka[1]):
                    nc.gpsimd.memset(m[:], 0.0).then_inc(s["zeroed"], 1)
                sequences(g, pool_a)
                nc.gpsimd.wait_ge(s["v_sb"], B)
                nc.gpsimd.wait_ge(s["q_split"], B)
                for c_ in "qk":
                    nc.gpsimd.wait_ge(saved[c_], 16 * B)
                sequences(g, pool_b)

            def sync(q):
                after_phases(q, n)
                sequences(q, sp_a)
                for c_ in "qk":
                    q.wait_ge(saved[c_], 16 * B)
                q.wait_ge(s["zeroed"], 6)
                q.wait_ge(s["m_consts"], 2)
                for m in ka:
                    q.dma_start(m[M0:M1, :, :], ones3.unsqueeze(1).to_broadcast([3, H, T])).then_inc(s["qk_ones"], 16)
                for i in range(2):
                    for g in range(GB):
                        load(i, i, g)
                for g in range(GB - 1):
                    m_sp(0, 0, g)
                sequences(q, sp_b)

            return {"tensor": tensor, "scalar": scalar, "vector": vector, "gpsimd": gpsimd, "sync": sync}

        def ssm_phase(n):
            f0 = B * n
            names = ("xs_ps", "xs_sb", "edges", "conv_chain", "conv", "xs_act", "z_act", "dtlo_ps", "dtlo_sb", "bc_ps", "bc_sb",
                     "bs_chain", "bs", "dt_ps", "relu", "e_sb", "ln", "dsum_chain", "dsum", "dm_ps", "decay", "decay_rows",
                     "bs_ps", "scanned", "s_ps", "s_tok", "y", "y_chain", "yn", "ynT_ps", "yg", "yz", "z_ready")
            s = {k: sem(f"p{n}_{k}") for k in names}
            used["at"] = 0
            z_all = view(P, DC * B * T).rearrange("p (c b t) -> p c b t", c=DC, b=B)
            dtlo_all = view(DTR, B * T).rearrange("p (b t) -> p b t", b=B)
            decays = view(1, B * T).rearrange("p (b t) -> p b t", b=B)
            c_all = view(P, B * TILES * DS).rearrange("p (n d) -> p n d", d=DS)
            bs_all = view(P, TILES * B).rearrange("p (i b) -> p i b", i=TILES)
            s_tok = view(P, B * TILES).rearrange("p (b i) -> p b i", b=B)
            decay8, state8 = view(B, T), view(B, T)
            at = used["at"]
            xs_pad = [view(P, T + 2) for _ in range(DC)]
            conv = [view(P, T) for _ in range(DC)]
            xs = [[view(P, T) for _ in range(DC)] for _ in range(2)]
            bcx = view(P, TILES * (2 * DS + 1)).rearrange("p (i n) -> p i n", i=TILES)
            bx = view(P, TILES * DS).rearrange("p (i d) -> p i d", i=TILES)
            used["at"] = at
            relu_t = [view(P, DC * T).rearrange("p (c t) -> p c t", c=DC) for _ in range(2)]
            e_t = view(P, DC * T).rearrange("p (c t) -> p c t", c=DC)
            ln_t = view(P, DC * T).rearrange("p (c t) -> p c t", c=DC)
            dsum_t = [view(P, T) for _ in range(2)]
            used["at"] = at
            y = view(P, TILES * DS).rearrange("p (i d) -> p i d", i=TILES)
            yn = view(P, T)
            yg = [view(P, T) for _ in range(DC)]
            yz = [[view(P, T) for _ in range(DC)] for _ in range(2)]
            at_bc, n_bc = DTR, 2 * DS + 1

            def pe_1(b, par, first_, last_):
                nc.tensor.wait_ge(xnT_ready, f0 + b + 1)
                for c in range(DC):
                    need(nc.tensor, s["xs_sb"], DC * b)
                    nc.tensor.matmul(bank[c][:], w_in[:, c * P:(c + 1) * P], xnT[par][:], start=True, stop=True).then_inc(s["xs_ps"], 1)
                for c in range(DC):
                    need(nc.tensor, s["z_act"], DC * b)
                    nc.tensor.matmul(bank[2 + c][:], w_in[:, DI + c * P:DI + (c + 1) * P], xnT[par][:], start=True, stop=True).then_inc(s["xs_ps"], 1)
                if not last_:
                    norm_pe(f0 + b + 1)
                nc.tensor.wait_ge(s["xs_act"], DC * (b + 1))
                need(nc.tensor, s["dtlo_sb"], b)
                for c in range(DC):
                    last = nc.tensor.matmul(bank[4][0:DTR, :], w_x[:, c, 0:DTR], xs[par][c][:], start=(c == 0), stop=(c == DC - 1))
                last.then_inc(s["dtlo_ps"], 1)
                need(nc.tensor, s["bc_sb"], b)
                for i in range(TILES):
                    for c in range(DC):
                        last = nc.tensor.matmul(bank[5][:, i * n_bc:(i + 1) * n_bc], xs[par][c][:, i * P:(i + 1) * P], w_x[:, c, at_bc:],
                                                start=(c == 0), stop=(c == DC - 1))
                last.then_inc(s["bc_ps"], 1)

            def act_1(b, par, first_, last_):
                for c in range(DC):
                    nc.scalar.wait_ge(s["xs_ps"], 2 * DC * b + c + 1)
                    need(nc.scalar, s["conv"], DC * (b - 1) + c + 1)
                    nc.scalar.copy(xs_pad[c][:, 1:T + 1], bank[c][:]).then_inc(s["xs_sb"], 1)
                for c in range(DC):
                    nc.scalar.wait_ge(s["xs_ps"], 2 * DC * b + DC + c + 1)
                    nc.scalar.activation(z_all[:, c, bass.ds(b, 1), :], bank[2 + c][:], ACT.Silu).then_inc(s["z_act"], 1)
                if not last_:
                    norm_act(f0 + b + 1, 1 - par)
                for c in range(DC):
                    nc.scalar.wait_ge(s["conv"], DC * b + c + 1)
                    need(nc.scalar, s["bc_ps"], prior(b))
                    nc.scalar.activation(xs[par][c][:], conv[c][:], ACT.Silu).then_inc(s["xs_act"], 1)
                nc.scalar.wait_ge(s["dtlo_ps"], b + 1)
                nc.scalar.copy(dtlo_all[:, bass.ds(b, 1), :], bank[4][0:DTR, :]).then_inc(s["dtlo_sb"], 1)

            def dve_1(v, b, par, first_, last_):
                chain = Chain(v, s["conv_chain"], 2 * DC)
                chain.begin(b)
                for c in range(DC):
                    v.wait_ge(s["xs_sb"], DC * b + c + 1)
                    need(v, s["xs_act"], DC * (b - 1) + c + 1)
                    w = [w_conv[:, c, k:k + 1] for k in range(3)]
                    chain(nc.vector.tensor_scalar(conv[c][:], xs_pad[c][:, 1:T + 1], w[1], None, ALU.mult))
                    chain(nc.vector.scalar_tensor_tensor(out=conv[c][:], in0=xs_pad[c][:, 0:T], scalar=w[0], in1=conv[c][:],
                                                         op0=ALU.mult, op1=ALU.add))
                    nc.vector.scalar_tensor_tensor(out=conv[c][:], in0=xs_pad[c][:, 2:T + 2], scalar=w[2], in1=conv[c][:],
                                                   op0=ALU.mult, op1=ALU.add).then_inc(s["conv"], 1)
                chain.end()
                if not last_:
                    norm_dve(v, f0 + b + 1, b + 1)
                chain = Chain(v, s["bs_chain"], 2)
                chain.begin(b)
                v.wait_ge(s["bc_ps"], b + 1)
                need(v, s["bs"], b)
                nc.vector.tensor_copy(bcx[:], bank[5][:, 0:TILES * n_bc].rearrange("p (i n) -> p i n", i=TILES)).then_inc(s["bc_sb"], 1)
                v.wait_ge(s["bc_sb"], b + 1)
                chain(nc.vector.tensor_tensor(bx[:], bcx[:, :, 0:DS], bcx[:, :, 2 * DS:].to_broadcast([P, TILES, DS]), ALU.mult))
                chain(nc.vector.tensor_reduce(bs_all[:, :, bass.ds(b, 1)], bx[:], AX_X, ALU.add))
                chain.end()
                nc.vector.tensor_copy(c_all[:, bass.ds(b * TILES, TILES), :], bcx[:, :, DS:2 * DS]).then_inc(s["bs"], 1)

            def pe_2(b, par, first_, last_):
                for c in range(DC):
                    need(nc.tensor, s["e_sb"], prior(b))
                    last = nc.tensor.matmul(bank[2 * par + c][:], w_dt[:, c * P:(c + 1) * P],
                                            dtlo_all[:, bass.ds(b, 1), :].rearrange("p o t -> p (o t)"), start=True, stop=True)
                last.then_inc(s["dt_ps"], 1)
                if not first_:
                    mean_pe(b - 1, 1 - par)

            def mean_pe(b, par):
                nc.tensor.wait_ge(s["dsum"], b + 1)
                nc.tensor.matmul(bank[4 + par][0:1, :], w_x[:, 0, DTR + 2 * DS:], dsum_t[par][:], start=True, stop=True).then_inc(s["dm_ps"], 1)

            def act_2(b, par, first_, last_):
                nc.scalar.wait_ge(s["dt_ps"], b + 1)
                need(nc.scalar, s["dsum"], prior(b))
                for c in range(DC):
                    bias = vecs[:, V_BDT + c:V_BDT + c + 1]
                    nc.scalar.activation(relu_t[par][:, c, :], bank[2 * par + c][:], ACT.Relu, bias=bias).then_inc(s["relu"], 1)
                need(nc.scalar, s["ln"], b)
                for c in range(DC):
                    bias = vecs[:, V_BDT + c:V_BDT + c + 1]
                    nc.scalar.activation(e_t[:, c, :], bank[2 * par + c][:], ACT.Abs, bias=bias).then_inc(s["relu"], 1)
                nc.scalar.wait_ge(s["relu"], 2 * DC * (b + 1))
                nc.scalar.activation(e_t[:], e_t[:], ACT.Exp, scale=-1.0).then_inc(s["e_sb"], 1)
                if not first_:
                    decay_act(b - 1, 1 - par)
                nc.scalar.wait_ge(s["e_sb"], b + 1)
                need(nc.scalar, s["dsum"], b)
                nc.scalar.activation(ln_t[:], e_t[:], ACT.Ln, bias=1.0).then_inc(s["ln"], 1)

            def decay_act(b, par):
                nc.scalar.wait_ge(s["dm_ps"], b + 1)
                nc.scalar.activation(decays[0:1, bass.ds(b, 1), :], bank[4 + par][0:1, :], ACT.Exp, scale=-1.0).then_inc(s["decay"], 1)

            def dve_2(v, b, par, first_, last_):
                chain = Chain(v, s["dsum_chain"], 2)
                chain.begin(b)
                v.wait_ge(s["relu"], 2 * DC * b + DC)
                need(v, s["dm_ps"], prior(b))
                d = dsum_t[par]
                chain(nc.vector.tensor_tensor(d[:], relu_t[par][:, 0, :], relu_t[par][:, 1, :], ALU.add))
                v.wait_ge(s["ln"], b + 1)
                chain(nc.vector.tensor_tensor(d[:], d[:], ln_t[:, 0, :], ALU.add))
                chain.end()
                nc.vector.tensor_tensor(d[:], d[:], ln_t[:, 1, :], ALU.add).then_inc(s["dsum"], 1)

            def dve_4a(v, b):
                chain = Chain(v, s["y_chain"], 15)
                chain.begin(b)
                chain(nc.vector.tensor_tensor(y[:], c_all[:, bass.ds(b * TILES, TILES), :],
                                              s_tok[:, bass.ds(b, 1), :].rearrange("p o i -> p (o i)").unsqueeze(2).to_broadcast([P, TILES, DS]),
                                              ALU.mult))
                for i in range(TILES):
                    last = nc.vector.bn_stats(stats[:, i, :], y[:, i, :])
                chain(last)
                nc.vector.nop(nofuse=True)
                for i in range(TILES):
                    last = nc.vector.bn_aggr(mv[:, i, :], stats[:, i, :])
                chain(last)
                chain(nc.vector.tensor_scalar(var[:], mv[:, :, 1], EPS, None, ALU.add))
                rsqrt(chain, var[:])
                chain.end()
                need(v, s["ynT_ps"], b)
                for i in range(TILES):
                    last = nc.vector.tensor_scalar(yn[:, i * P:(i + 1) * P].rearrange("p (r d) -> p r d", d=DS),
                                                   y[:, i, :].unsqueeze(1).to_broadcast([P, P // DS, DS]),
                                                   mv[:, i, 0:1], rs_y[:, i:i + 1], ALU.subtract, ALU.mult)
                last.then_inc(s["yn"], 1)
                v.wait_ge(s["yn"], b + 1)

            def dve_4b(v, b, par):
                for c in range(DC):
                    v.wait_ge(s["yg"], DC * b + c + 1)
                    need(v, s["z_ready"], prior(b))
                    nc.vector.tensor_tensor(yz[par][c][:], yg[c][:], z_all[:, c, bass.ds(b, 1), :].rearrange("p o t -> p (o t)"),
                                            ALU.mult).then_inc(s["yz"], 1)

            def dve_4c(v, b, par):
                v.wait_ge(s["z_ready"], b + 1)
                nc.vector.tensor_tensor(flat(x_of(b)), bank[2 + par][:], flat(x_of(b)), ALU.add).then_inc(x_upd, 1)

            def dve_4(v, b, par, first_, last_):
                if not last_:
                    dve_4a(v, b + 1)
                dve_4b(v, b, par)
                if not first_:
                    dve_4c(v, b - 1, 1 - par)

            def pe_4(b, par, first_, last_):
                nc.tensor.wait_ge(s["yn"], b + 1)
                need(nc.tensor, s["yg"], DC * prior(b))
                for i in range(TILES):
                    last = nc.tensor.transpose(bank[par][:, i * P:(i + 1) * P], yn[:, i * P:(i + 1) * P], ident[:])
                last.then_inc(s["ynT_ps"], 1)
                if not first_:
                    z_pe4(b - 1, 1 - par)

            def z_pe4(b, par):
                nc.tensor.wait_ge(s["yz"], DC * (b + 1))
                need(nc.tensor, x_upd, f0 + b - 1)
                for i in range(TILES):
                    for c in range(DC):
                        last = nc.tensor.matmul(bank[2 + par][:, i * P:(i + 1) * P], yz[par][c][:, i * P:(i + 1) * P], w_out[:, c, :],
                                                start=(c == 0), stop=(c == DC - 1))
                last.then_inc(s["z_ready"], 1)

            def act_4(b, par, first_, last_):
                nc.scalar.wait_ge(s["ynT_ps"], b + 1)
                for c in range(DC):
                    need(nc.scalar, s["yz"], DC * (b - 1) + c + 1)
                    nc.scalar.activation(yg[c][:], bank[par][:], ACT.Identity, bias=vecs[:, V_B + c:V_B + c + 1],
                                         scale=vecs[:, V_G + c:V_G + c + 1]).then_inc(s["yg"], 1)

            def tensor(t):
                after_phases(t, n)
                sequences(t, pe_1)
                nc.tensor.wait_ge(s["dtlo_sb"], B)
                nc.tensor.wait_ge(s["z_act"], DC * B)
                nc.tensor.wait_ge(s["bs"], B)
                sequences(t, pe_2)
                mean_pe(B - 1, 1)
                for i in range(TILES):
                    last = nc.tensor.transpose(bank[6][0:B, i * P:(i + 1) * P], bs_all[:, i, :], ident[:])
                last.then_inc(s["bs_ps"], 1)
                nc.tensor.wait_ge(s["scanned"], 1)
                for i in range(TILES):
                    last = nc.tensor.transpose(bank[6][:, i * B:(i + 1) * B], state8[:, i * P:(i + 1) * P], ident[0:B, 0:B])
                last.then_inc(s["s_ps"], 1)
                sequences(t, pe_4)
                z_pe4(B - 1, 1)
                norm_pe(f0 + B)

            def scalar(c):
                after_phases(c, n)
                nc.scalar.wait_ge(s["edges"], 2 * DC)
                sequences(c, act_1)
                nc.scalar.wait_ge(s["bc_ps"], B)
                nc.scalar.wait_ge(s["bs"], B)
                sequences(c, act_2)
                decay_act(B - 1, 1)
                nc.scalar.wait_ge(s["dm_ps"], B)
                sequences(c, act_4)
                norm_act(f0 + B, 0)

            def vector(v):
                after_phases(v, n)
                for c in range(DC):
                    for e in (0, T + 1):
                        nc.vector.memset(xs_pad[c][:, e:e + 1], 0.0).then_inc(s["edges"], 1)
                v.wait_ge(s["edges"], 2 * DC)
                sequences(v, lambda b, par, f, l: dve_1(v, b, par, f, l))
                v.wait_ge(s["xs_act"], DC * B)
                v.wait_ge(s["bs"], B)
                v.wait_ge(s["bc_ps"], B)
                sequences(v, lambda b, par, f, l: dve_2(v, b, par, f, l))
                v.wait_ge(s["bs_ps"], 1)
                v.wait_ge(s["decay_rows"], 16)
                nc.vector.tensor_tensor_scan(state8[:], decay8[:], bank[6][0:B, :], 0.0, ALU.mult, ALU.add).then_inc(s["scanned"], 1)
                v.wait_ge(s["s_ps"], 1)
                nc.vector.tensor_copy(s_tok[:].rearrange("p b i -> p i b"),
                                      bank[6][:, 0:TILES * B].rearrange("p (i b) -> p i b", i=TILES)).then_inc(s["s_tok"], 1)
                v.wait_ge(s["s_tok"], 1)
                v.wait_ge(s["dm_ps"], B)
                v.wait_ge(s["decay"], B)
                dve_4a(v, 0)
                sequences(v, lambda b, par, f, l: dve_4(v, b, par, f, l))
                dve_4c(v, B - 1, 1)
                norm_dve(v, f0 + B, 0)

            def gpsimd(g):
                pass

            def sync(q):
                q.wait_ge(s["decay"], B)
                q.dma_start(decay8[:], decays[0:1, :, :]).then_inc(s["decay_rows"], 16)

            return {"tensor": tensor, "scalar": scalar, "vector": vector, "gpsimd": gpsimd, "sync": sync}

        make = {"attn": attn_phase, "ssm": ssm_phase, "moe0": lambda n: moe_phase(n, 0), "moe1": lambda n: moe_phase(n, 1)}
        plan = [make[p](n) for n, p in enumerate(phases)]

        block = ctx.enter_context(nc.Block())
        xv = a["L0_attn_x"].rearrange("b (i p) e -> p (b i) e", p=P)
        ov = out.rearrange("b (i p) e -> p (b i) e", p=P)
        r1 = lambda v: v.rearrange("(o n) -> o n", o=1)

        @block.sync
        def _(q):
            q.dma_start(x_res[:, 0:TILES, :], xv[:, 0:TILES, :]).then_inc(x_first, 16)
            rows = [
                (V_B1, a["L0_ffn_b1"].rearrange("e (c p) -> (e c) p", p=P)), (V_B2, a["L0_ffn_b2"]),
                (V_BK, r1(a["L0_attn_bk"])), (V_BV, r1(a["L0_attn_bv"])),
                (V_BDT, a["L1_attn_b_dt"].rearrange("(c p) -> c p", p=P)),
                (V_G, a["L1_attn_ln_g"].rearrange("(c p) -> c p", p=P)),
                (V_B, a["L1_attn_ln_b"].rearrange("(c p) -> c p", p=P))]
            for at, v in rows:
                q.dma_start(vec_rows[at:at + v.shape[0], :], v).then_inc(rows_loaded, 16)
            for at, v in ((V_BQ, a["L0_attn_bq"]), (V_BL, a["L0_attn_bl"])):
                q.dma_start(vec_rows[at:at + 1, :].rearrange("o (d h) -> o d h", d=HD),
                            v.rearrange("(o h d) -> o d h", o=1, d=HD),
                            allow_slow_non_contiguous=True).then_inc(rows_loaded, 16)
            weights = [
                (wr0[:], a["L0_ffn_w_router"]),
                (w1[:, 0:2, :], a["L0_ffn_w1"].rearrange("e p h -> p e h")[:, 0:2, :]),
                (w2[:, 0:2, :, :], a["L0_ffn_w2"].rearrange("e (c p) o -> p e c o", p=P)[:, 0:2, :, :]),
                (w1[:, 2:, :], a["L0_ffn_w1"].rearrange("e p h -> p e h")[:, 2:, :]),
                (w2[:, 2:, :, :], a["L0_ffn_w2"].rearrange("e (c p) o -> p e c o", p=P)[:, 2:, :, :]),
                (wq[:], a["L0_attn_Wq"]), (wk[:], a["L0_attn_Wk"]), (wv[:], a["L0_attn_Wv"]), (wl[:], a["L0_attn_Wl"]),
                (wo[:], a["L0_attn_Wo"]),
                (bl_bc[0:1, :], r1(a["L0_attn_bl"])), (bo_bc[0:1, 0, :], r1(a["L0_attn_bo"])),
                (wr1[:], a["L1_ffn_router_w"]),
                (gate_w[:], a["L1_ffn_gate_w"].rearrange("e p f -> p e f")),
                (up_w[:], a["L1_ffn_up_w"].rearrange("e p f -> p e f")),
                (down_w[:], a["L1_ffn_down_w"].rearrange("(j t) f o -> (t f) j o", t=2)),
                (sh_g[:], a["L1_ffn_shared_gate_w"]), (sh_u[:], a["L1_ffn_shared_up_w"]), (sh_d[:], a["L1_ffn_shared_down_w"]),
                (w_in[:], a["L1_attn_W_in"]),
                (w_conv[:], a["L1_attn_W_conv"].rearrange("(c p) o k -> p c (o k)", p=P)),
                (w_x[:, :, 0:DTR + 2 * DS], a["L1_attn_W_xproj"].rearrange("(c p) n -> p c n", p=P)),
                (w_dt[:], a["L1_attn_W_dt"]),
                (w_out[:], a["L1_attn_W_out"].rearrange("(c p) o -> p c o", p=P))]
            for dst, src in weights:
                q.dma_start(dst, src).then_inc(w_loaded, 16)
            assert len(weights) == N_WEIGHTS and len(rows) + 2 == N_ROWS
            q.dma_start(x_res[:, TILES:, :], xv[:, TILES:, :]).then_inc(x_rest, 16)
            for p in plan:
                p["sync"](q)
            for b in range(B):
                q.wait_ge(x_upd, B * (len(phases) - 1) + b + 1)
                q.dma_start(ov[:, b * TILES:(b + 1) * TILES, :], x_of(b)).then_inc(stored, 16)
            q.wait_ge(stored, 16 * B)

        @block.gpsimd
        def _(g):
            g.memset(ident[:], 0.0).then_inc(pool_chain, 1)
            g.memset(identb[:], 0.0).then_inc(pool_chain, 1)
            g.wait_ge(pool_chain, 2)
            for m in (ident, identb):
                g.affine_select(out=m[:], in_=m[:], compare_op=ALU.not_equal, fill=1.0, base=0, pattern=[[-1, P]],
                                channel_multiplier=1).then_inc(ident_ready, 1)
            for e in range(NE1):
                g.memset(first[:, :, e:e + 1], float(NE1 - e))
            g.memset(w_x[:, :, DTR + 2 * DS:], 1.0 / DI).then_inc(tables_ready, 1)
            g.wait_ge(w_loaded, 16 * N_WEIGHTS)
            g.partition_broadcast(bl_bc[:], bl_bc[0:1, :])
            for i in range(TILES):
                last = g.partition_broadcast(bo_bc[:, TILES - 1 - i, :], bo_bc[0:1, 0, :])
            for w, w_p in ((wq, wq_p), (wl, wl_p)):
                last = g.tensor_copy(w_p[:].rearrange("p (d h) -> p d h", d=HD), w[:].rearrange("p (h d) -> p d h", d=HD))
            last.then_inc(tables_ready, 1)
            for p in plan:
                p["gpsimd"](g)

        @block.scalar
        def _(c):
            c.wait_ge(vecs_ps, 1)
            nc.scalar.copy(vecs[:], bank[0][:, 0:NVEC]).then_inc(vecs_ready, 1)
            norm_act(0, 0)
            for p in plan:
                p["scalar"](c)

        @block.vector
        def _(v):
            v.wait_ge(x_first, 16)
            norm_dve(v, 0, 0)
            v.wait_ge(x_rest, 16)
            v.wait_ge(tables_ready, 2)
            v.wait_ge(vecs_ready, 1)
            for p in plan:
                p["vector"](v)

        @block.tensor
        def _(t):
            t.wait_ge(ident_ready, 2)
            t.wait_ge(rows_loaded, 16 * N_ROWS)
            nc.tensor.transpose(bank[0][:, 0:NVEC], vec_rows[:], ident[0:NVEC, 0:NVEC]).then_inc(vecs_ps, 1)
            norm_pe(0)
            t.wait_ge(vecs_ready, 1)
            t.wait_ge(w_loaded, 16 * N_WEIGHTS)
            t.wait_ge(tables_ready, 2)
            for p in plan:
                p["tensor"](t)


_INS = ['L0_attn_x', 'L0_attn_Wq', 'L0_attn_bq', 'L0_attn_Wk', 'L0_attn_bk', 'L0_attn_Wv', 'L0_attn_bv', 'L0_attn_Wl',
        'L0_attn_bl', 'L0_attn_Wo', 'L0_attn_bo', 'L0_ffn_w_router', 'L0_ffn_w1', 'L0_ffn_b1', 'L0_ffn_w2', 'L0_ffn_b2',
        'L1_attn_W_in', 'L1_attn_W_conv', 'L1_attn_W_xproj', 'L1_attn_W_dt', 'L1_attn_b_dt', 'L1_attn_W_out',
        'L1_attn_ln_g', 'L1_attn_ln_b', 'L1_ffn_router_w', 'L1_ffn_gate_w', 'L1_ffn_up_w', 'L1_ffn_down_w',
        'L1_ffn_shared_gate_w', 'L1_ffn_shared_up_w', 'L1_ffn_shared_down_w']


def kernel(**inputs):
    import numpy as _np
    import concourse.bacc as _bacc
    from concourse import mybir as _mybir
    from concourse.bass_utils import run_bass_kernel_spmd as _run

    nc = _bacc.Bacc("TRN2", target_bir_lowering=False, num_devices=1)
    arrays, aps = {}, {}
    for name in _INS:
        v = _np.ascontiguousarray(inputs[name])
        arrays[f"in_{name}"] = v
        aps[name] = nc.dram_tensor(f"in_{name}", v.shape, _mybir.dt.from_np(v.dtype), kind="ExternalInput").ap()
    out = nc.dram_tensor("out_x", (B, T, E), F32, kind="ExternalOutput").ap()
    build(nc, aps, out)
    r = _run(nc, [arrays], core_ids=[0])
    return r.results[0]["out_x"]
```

```python
from contextlib import ExitStack

import concourse.bass as bass
from concourse import mybir

ALU = mybir.AluOpType
ACT = mybir.ActivationFunctionType
F32 = mybir.dt.float32
F32R = mybir.dt.float32r
BF16 = mybir.dt.bfloat16
AX_X = mybir.AxisListType.X

P = 128
B, T, E = 8, 512, 128
TILES = T // P
NE0, HID = 8, 512
HC = HID // P
NE1, FE = 16, 64
PAIRS = NE1 // 2
H, HD = 16, 8
HG = 4
DI, DS, DTR = 256, 16, 64
DC = DI // P
EPS = 1e-5
BIG = 1e30

V_B1, V_B2 = 0, 32
V_BQ, V_BK, V_BV, V_BL = 40, 41, 42, 43
V_BDT, V_G, V_B = 44, 46, 48
NVEC = 50
N_ROWS, N_WEIGHTS = 9, 19

PHASES = ("moe0", "attn", "moe0", "moe1", "ssm", "moe1")


class Chain:

    def __init__(self, eng, sem, per):
        self.eng, self.sem, self.per, self.k, self.base = eng, sem, per, 0, 0

    def begin(self, n):
        self.base, self.k = n * self.per, 0

    def __call__(self, ins):
        self.k += 1
        ins.then_inc(self.sem, 1)
        self.eng.wait_ge(self.sem, self.base + self.k)

    def end(self):
        assert self.k == self.per, (self.k, self.per)


def build(nc, a, out, phases=PHASES):
    nc.disable_value_cache = True
    with ExitStack() as ctx:
        def sb(name, shape, dt=F32):
            return ctx.enter_context(nc.sbuf_tensor(name, shape, dt))

        def sem(name):
            return ctx.enter_context(nc.semaphore(name))

        bank = [ctx.enter_context(nc.psum_tensor(f"bank{i}", [P, 512], F32)) for i in range(8)]

        x_res = sb("x_res", [P, B * TILES, E])
        xnT = [sb(f"xnT{i}", [P, T]) for i in range(2)]
        xn = sb("xn", [P, TILES, E])
        staged = [sb(f"staged{i}", [P, 2, HID]) for i in range(2)]
        wr0 = sb("wr0", [P, NE0])
        gate_up = sb("gate_up", [P, 2, PAIRS + 1, P])
        down_w = sb("down_w", [P, PAIRS, E])
        sh_d = sb("sh_d", [P, E])
        wr1 = sb("wr1", [P, NE1])
        ident = sb("ident", [P, P])
        identb = sb("identb", [P, P], BF16)
        first = sb("first", [P, TILES, NE1])
        vec_rows = sb("vec_rows", [NVEC, P])
        vecs = sb("vecs", [P, NVEC])
        wq, wk, wv, wl, wo = [sb(f"w_{k}", [P, P]) for k in ("q", "k", "v", "l", "o")]
        wq_p, wl_p = sb("wq_p", [P, P]), sb("wl_p", [P, P])
        bl_bc = sb("bl_bc", [P, P])
        bo_bc = sb("bo_bc", [P, TILES, P])
        w_in = sb("w_in", [P, 2 * DI])
        w_conv = sb("w_conv", [P, DC, 3])
        w_x = sb("w_x", [P, DC, DTR + 2 * DS + 1])
        w_dt = sb("w_dt", [DTR, DI])
        w_out = sb("w_out", [P, DC, E])
        stats = sb("stats", [P, TILES, 6])
        mv = sb("mv", [P, TILES, 2])
        var = sb("var", [P, TILES])
        rs_y = sb("rs_y", [P, TILES])
        neg_half = sb("neg_half", [P, TILES])
        lg = sb("lg", [P, TILES, NE1])
        rt_a = sb("rt_a", [P, TILES, NE1])
        rt_b = sb("rt_b", [P, TILES, NE1])
        rt_c = sb("rt_c", [P, TILES, NE1])
        rt_th = sb("rt_th", [P, TILES, NE1])
        rt_m = sb("rt_m", [P, TILES])
        rt_n = sb("rt_n", [P, TILES])
        coef = sb("coef", [P, TILES, NE1])

        mem = {"phase": ExitStack(), "part": ExitStack(), "now": "phase", "count": 0}

        def new_phase():
            mem["part"].close()
            mem["phase"].close()
            mem["now"] = "phase"

        def new_part():
            mem["part"].close()
            mem["now"] = "part"

        def view(rows, cols, dt=F32):
            mem["count"] += 1
            return mem[mem["now"]].enter_context(nc.sbuf_tensor(f"shared{mem['count']}", [rows, cols], dt))[:, :]

        x_first, x_rest, w_loaded = sem("x_first"), sem("x_rest"), sem("w_loaded")
        rows_loaded, ident_ready, tables_ready = sem("rows_loaded"), sem("ident_ready"), sem("tables_ready")
        pool_chain, vecs_ps, vecs_ready = sem("pool_chain"), sem("vecs_ps"), sem("vecs_ready")
        x_upd = sem("x_upd")
        xn_ready, xnT_ps, xnT_ready = sem("xn_ready"), sem("xnT_ps"), sem("xnT_ready")
        ln_chain, mv_ready, var_ready, rs_ready = sem("ln_chain"), sem("mv_ready"), sem("var_ready"), sem("rs_ready")
        stored = sem("stored")
        w_staged = [sem(f"w_staged{i}") for i in range(2)]
        xv = a["L0_attn_x"].rearrange("b (i p) e -> p (b i) e", p=P)
        LN_STEPS = 1

        def x_of(b):
            return x_res[:, bass.ds(b * TILES, TILES), :]

        def need(eng, semaphore, value):
            if not isinstance(value, int) or value > 0:
                eng.wait_ge(semaphore, value)

        def prior(b):
            return b - 1 if isinstance(b, int) else (b * (B - 3) + 1) // (B - 2)

        def flat(v):
            return v.rearrange("p a b -> p (a b)")

        def rsqrt(var_sem, k, done):
            nc.gpsimd.nop(nofuse=True)
            nc.gpsimd.tensor_scalar(var[:], mv[:, :, 1], EPS, None, ALU.add).then_inc(var_sem, 1)
            nc.gpsimd.wait_ge(var_sem, k + 1)
            nc.gpsimd.tensor_tensor(rs_y[:], var[:], neg_half[:], ALU.pow).then_inc(done, 1)

        def norm_a(v, f, b):
            chain = Chain(v, ln_chain, LN_STEPS)
            chain.begin(f)
            x = x_of(b)
            need(v, xn_ready, f)
            if isinstance(f, int):
                need(v, x_upd, f - B + 1)
                if f == 1:
                    v.wait_ge(x_rest, 16)
            for i in range(TILES):
                last = nc.vector.bn_stats(stats[:, i, :], x[:, i, :])
            chain(last)
            nc.vector.nop(nofuse=True)
            chain.end()
            for i in range(TILES):
                last = nc.vector.bn_aggr(mv[:, i, :], stats[:, i, :])
            last.then_inc(mv_ready, 1)

        def norm_b(f):
            nc.gpsimd.wait_ge(mv_ready, f + 1)
            rsqrt(var_ready, f, rs_ready)

        def norm_c(v, f, b):
            x = x_of(b)
            v.wait_ge(rs_ready, f + 1)
            need(v, xnT_ps, f)
            for i in range(TILES):
                last = nc.vector.tensor_scalar(xn[:, i, :], x[:, i, :], mv[:, i, 0:1], rs_y[:, i:i + 1], ALU.subtract, ALU.mult)
            last.then_inc(xn_ready, 1)

        def norm_pe(f):
            need(nc.tensor, xn_ready, f + 1)
            need(nc.tensor, xnT_ready, f)
            for i in range(TILES):
                last = nc.tensor.transpose(bank[7][:, i * P:(i + 1) * P], xn[:, i, :], ident[:])
            last.then_inc(xnT_ps, 1)

        def norm_act(f, par):
            nc.scalar.wait_ge(xnT_ps, f + 1)
            nc.scalar.copy(xnT[par][:], bank[7][:]).then_inc(xnT_ready, 1)

        def after_phases(eng, n):
            if n:
                eng.wait_ge(x_upd, B * n)

        def sequences(eng, body, c0=0):
            body(c0, 0, True, False)
            with eng.Fori(0, (B - 2) // 2) as i:
                body(2 * i + (c0 + 1), 1, False, False)
                body(2 * i + (c0 + 2), 0, False, False)
            body(c0 + B - 1, 1, False, True)

        def load_x_rest(q):
            q.dma_start(x_res[:, TILES:, :], xv[:, TILES:, :]).then_inc(x_rest, 16)

        def load_weights(q):
            r1 = lambda v: v.rearrange("(o n) -> o n", o=1)
            weights = [
                (wq[:], a["L0_attn_Wq"]), (wk[:], a["L0_attn_Wk"]), (wv[:], a["L0_attn_Wv"]), (wl[:], a["L0_attn_Wl"]),
                (wo[:], a["L0_attn_Wo"]),
                (bl_bc[0:1, :], r1(a["L0_attn_bl"])), (bo_bc[0:1, 0, :], r1(a["L0_attn_bo"])),
                (wr1[:], a["L1_ffn_router_w"]),
                (flat(gate_up[:, 0, 1:, :]).rearrange("p (e f) -> p e f", f=FE), a["L1_ffn_gate_w"].rearrange("e p f -> p e f")),
                (flat(gate_up[:, 1, 1:, :]).rearrange("p (e f) -> p e f", f=FE), a["L1_ffn_up_w"].rearrange("e p f -> p e f")),
                (down_w[:], a["L1_ffn_down_w"].rearrange("(j t) f o -> (t f) j o", t=2)),
                (gate_up[:, 0, 0, :], a["L1_ffn_shared_gate_w"]), (gate_up[:, 1, 0, :], a["L1_ffn_shared_up_w"]), (sh_d[:], a["L1_ffn_shared_down_w"]),
                (w_in[:], a["L1_attn_W_in"]),
                (w_conv[:], a["L1_attn_W_conv"].rearrange("(c p) o k -> p c (o k)", p=P)),
                (w_x[:, :, 0:DTR + 2 * DS], a["L1_attn_W_xproj"].rearrange("(c p) n -> p c n", p=P)),
                (w_dt[:], a["L1_attn_W_dt"]),
                (w_out[:], a["L1_attn_W_out"].rearrange("(c p) o -> p c o", p=P))]
            for dst, src in weights:
                q.dma_start(dst, src).then_inc(w_loaded, 16)
            assert len(weights) == N_WEIGHTS

        moe_sems = {}

        def moe_phase(n, kind):
            ne = NE0 if kind == 0 else NE1
            c0 = B * phases[:n].count(phases[n])
            f0 = B * n - c0
            names = ("xh_ready", "xl_ready", "w_hi", "w_lo", "lg_ready", "z_ready", "th_ready", "coef_ready", "ct_ps", "ct_sb",
                     "row_loaded", "bc_ready", "up_ready", "act_done", "down_done", "back_ready", "rt_chain")
            names += (("hh_ready", "hl_ready", "hp_ready", "y_used", "mixed") if kind == 0 else
                      ("bc_half", "gated", "hid_ready", "acc_ready"))
            if kind not in moe_sems:
                moe_sems[kind] = {k: sem(f"moe{kind}_{k}") for k in names}
            s = moe_sems[kind]
            occ = phases[:n].count(phases[n])
            IT = PAIRS + 1
            new_phase()
            coefB = view(P, 8 * T).rearrange("p (e t) -> p e t", e=8)
            row = view(1, ne * T).rearrange("p (e t) -> p e t", e=ne)
            coefT = view(NE1, T)
            hid = [view(P, T) for _ in range(4 if kind == 0 else 5)]
            tmp = [view(P, T) for _ in range(2)]
            acc = [view(P, T) for _ in range(2)]
            xh, xl = ([view(P, T, F32R) for _ in range(2)] for _ in range(2))
            if kind == 0:
                hh, hl = ([view(P, T, F32R) for _ in range(HC)] for _ in range(2))
                wh, wl_ = (view(P, NE0 * 2 * HID, F32R).rearrange("p (e k h) -> p e k h", e=NE0, k=2) for _ in range(2))
            else:
                silu = [view(P, T) for _ in range(2)]
                gh, gl = (view(P, 2 * IT * P, F32R).rearrange("p (k j m) -> p k j m", k=2, j=IT) for _ in range(2))
            wr = wr0 if kind == 0 else wr1
            RT_STEPS = 18
            ROW_DMAS = 1 if kind == 0 else 2
            wide = lambda m: m[:].unsqueeze(2).to_broadcast([P, TILES, ne])

            def router_pe(b, par):
                nc.tensor.wait_ge(xnT_ready, f0 + b + 1)
                for i in range(TILES):
                    last = nc.tensor.matmul(bank[7][:, i * ne:(i + 1) * ne], xnT[par][:, i * P:(i + 1) * P], wr[:, 0:ne],
                                            start=True, stop=True)
                last.then_inc(s["lg_ready"], 1)

            def coef_pe(b):
                nc.tensor.wait_ge(s["coef_ready"], b + 1)
                need(nc.tensor, s["ct_sb"], b)
                if not isinstance(b, int) or b > 1:
                    nc.tensor.wait_ge(x_upd, f0 + b - 1)
                for i in range(TILES):
                    last = nc.tensor.transpose(bank[6][0:ne, i * P:(i + 1) * P], coef[:, i, 0:ne], ident[:])
                last.then_inc(s["ct_ps"], 1)

            def router_act(b):
                nc.scalar.wait_ge(s["z_ready"], b + 1)
                nc.scalar.activation(rt_th[:, :, 0:ne], lg[:, :, 0:ne], ACT.Tanh, scale=0.5).then_inc(s["th_ready"], 1)

            def coef_act(b):
                nc.scalar.wait_ge(s["ct_ps"], b + 1)
                need(nc.scalar, s["row_loaded"], 16 * ROW_DMAS * b)
                nc.scalar.copy(coefT[0:ne, :], bank[6][0:ne, :]).then_inc(s["ct_sb"], 1)

            z, q, r, sel, th = (m[:, :, 0:ne] for m in (lg, rt_a, rt_b, rt_c, rt_th))

            def router_a(v, b):
                chain = Chain(v, s["rt_chain"], RT_STEPS)
                chain.begin(b)
                ps = bank[7][:, 0:TILES * ne].rearrange("p (i e) -> p i e", i=TILES)
                v.wait_ge(s["lg_ready"], b + 1)
                need(v, s["coef_ready"], b)
                chain(nc.vector.tensor_reduce(rt_m[:], ps, AX_X, ALU.max))
                nc.vector.tensor_tensor(z, ps, wide(rt_m), ALU.subtract).then_inc(s["z_ready"], 1)
                v.wait_ge(s["z_ready"], b + 1)
                chain(nc.vector.tensor_scalar(q, z, 0.0, None, ALU.is_equal))
                chain(nc.vector.tensor_tensor(q, q, first[:, :, 0:ne], ALU.mult))
                chain(nc.vector.tensor_reduce(rt_n[:], q, AX_X, ALU.max))
                chain(nc.vector.tensor_tensor(sel, q, wide(rt_n), ALU.is_equal))
                return chain

            def router_b(chain):
                chain(nc.vector.scalar_tensor_tensor(out=r, in0=sel, scalar=-BIG, in1=z, op0=ALU.mult, op1=ALU.add))
                chain(nc.vector.tensor_reduce(rt_m[:], r, AX_X, ALU.max))
                chain(nc.vector.tensor_tensor(q, r, wide(rt_m), ALU.is_equal))
                chain(nc.vector.tensor_tensor(q, q, first[:, :, 0:ne], ALU.mult))
                chain(nc.vector.tensor_reduce(rt_n[:], q, AX_X, ALU.max))
                chain(nc.vector.tensor_tensor(q, q, wide(rt_n), ALU.is_equal))
                chain(nc.vector.tensor_tensor(sel, q, sel, ALU.add))

            def router_c(v, b, chain):
                v.wait_ge(s["th_ready"], b + 1)
                chain(nc.vector.tensor_scalar(r, th, -1.0, 1.0, ALU.mult, ALU.add))
                chain(nc.vector.reciprocal(r, r))
                chain(nc.vector.scalar_tensor_tensor(out=r, in0=th, scalar=1.0, in1=r, op0=ALU.add, op1=ALU.mult))
                chain(nc.vector.tensor_reduce(rt_n[:], r, AX_X, ALU.add))
                chain(nc.vector.reciprocal(rt_m[:], rt_n[:]))
                chain(nc.vector.tensor_tensor(r, r, sel, ALU.mult))
                chain.end()
                need(v, s["ct_ps"], b)
                nc.vector.scalar_tensor_tensor(out=coef[:, :, 0:ne], in0=r, scalar=0.5, in1=wide(rt_m), op0=ALU.mult,
                                               op1=ALU.mult).then_inc(s["coef_ready"], 1)

            def router_dve(v, b):
                chain = router_a(v, b)
                router_b(chain)
                router_c(v, b, chain)

            def row_sp(b, par, first_, last_):
                nc.sync.wait_ge(s["ct_sb"], b + 1)
                need(nc.sync, s["bc_ready"], 8 * b)
                for k in range(ROW_DMAS):
                    nc.sync.dma_start(row[0:1, 8 * k:8 * k + 8, :], coefT[k:ne:ROW_DMAS, :]).then_inc(s["row_loaded"], 16)

            def pool1(b, par, first_, last_):
                if more or not last_:
                    norm_b(f0 + b + 1)
                nc.gpsimd.wait_ge(s["row_loaded"], 16 * ROW_DMAS * (b + 1))
                for e in range(PAIRS):
                    need(nc.gpsimd, s["hid_ready"], PAIRS * (b - 1) + e + 1)
                    nc.gpsimd.nop(nofuse=True)
                    nc.gpsimd.partition_broadcast(coefB[:, e, :], row[0:1, 8 + e, :]).then_inc(s["bc_half"], 1)
                    nc.gpsimd.wait_ge(s["bc_half"], PAIRS * b + e + 1)
                    nc.gpsimd.nop(nofuse=True)
                    nc.gpsimd.partition_broadcast(coefB[0:FE, e, :], row[0:1, e, :], channels=FE).then_inc(s["bc_ready"], 1)

            def back_pe(b, par):
                nc.tensor.wait_ge(s["ct_sb"], b + 1)
                if kind == 0:
                    nc.tensor.wait_ge(s["mixed"], (NE0 - 1) * (b + 1))
                else:
                    nc.tensor.wait_ge(s["acc_ready"], b + 1)
                for i in range(TILES):
                    last = nc.tensor.transpose(bank[6][:, i * P:(i + 1) * P], acc[par][:, i * P:(i + 1) * P], ident[:])
                last.then_inc(s["back_ready"], 1)

            def back_dve(v, b):
                v.wait_ge(s["back_ready"], b + 1)
                nc.vector.tensor_tensor(flat(x_of(b % B)), bank[6][:], flat(x_of(b % B)), ALU.add).then_inc(x_upd, 1)

            more = n + 1 < len(phases)

            def hi_lo(out_bank, w_hi, w_lo, x_hi, x_lo, start, stop):
                nc.tensor.matmul(out_bank, w_hi, x_hi, start=start, stop=False)
                nc.tensor.matmul(out_bank, w_hi, x_lo, start=False, stop=False)
                return nc.tensor.matmul(out_bank, w_lo, x_hi, start=False, stop=stop)

            def xh_act(b, par):
                nc.scalar.wait_ge(xnT_ready, f0 + b + 1)
                nc.scalar.copy(xh[par][:], xnT[par][:]).then_inc(s["xh_ready"], 1)

            def xl_dve(v, b, par):
                v.wait_ge(s["xh_ready"], b + 1)
                nc.vector.tensor_tensor(xl[par][:], xnT[par][:], xh[par][:], ALU.subtract).then_inc(s["xl_ready"], 1)

            CH = NE0 * HC

            LAG = HC - 1

            def load0(e):
                need(nc.sync, s["w_lo"], NE0 * occ + e - 1)
                nc.sync.dma_start(staged[e % 2][:, 0, :], a["L0_ffn_w1"][e]).then_inc(w_staged[e % 2], 16)
                nc.sync.dma_start(staged[e % 2][:, 1, :].rearrange("p (c o) -> p c o", o=E),
                                  a["L0_ffn_w2"][e].rearrange("(c p) o -> p c o", p=P)).then_inc(w_staged[e % 2], 16)

            def w_hi_act(e):
                nc.scalar.wait_ge(w_staged[e % 2], 32 * (occ * NE0 // 2 + e // 2 + 1))
                nc.scalar.copy(wh[:, e, :, :], staged[e % 2][:]).then_inc(s["w_hi"], 1)

            def w_lo_dve(v, e):
                v.wait_ge(s["w_hi"], NE0 * occ + e + 1)
                nc.vector.tensor_tensor(wl_[:, e, :, :], staged[e % 2][:], wh[:, e, :, :], ALU.subtract).then_inc(s["w_lo"], 1)

            def up0(b, par, k, first_):
                e, c = k // HC, k % HC
                if k == 0:
                    nc.tensor.wait_ge(s["xl_ready"], b + 1)
                if first_ and c == 0:
                    nc.tensor.wait_ge(s["w_lo"], NE0 * occ + e + 1)
                need(nc.tensor, s["act_done"], CH * b + k - 3)
                cols = slice(c * P, (c + 1) * P)
                hi_lo(bank[k % 4][:], wh[:, e, 0, cols], wl_[:, e, 0, cols], xh[par][:], xl[par][:], True, True).then_inc(s["up_ready"], 1)

            def down0(b, k):
                e, c = k // HC, k % HC
                if c < HC - 1:
                    nc.tensor.wait_ge(s["hl_ready"], (HC - 1) * (NE0 * b + e) + c + 1)
                else:
                    nc.tensor.wait_ge(s["hp_ready"], NE0 * b + e + 1)
                if c == 0:
                    need(nc.tensor, s["y_used"], NE0 * b + e - 1)
                cols = slice(c * P, (c + 1) * P)
                hi_lo(bank[4 + e % 2][:], wh[:, e, 1, cols], wl_[:, e, 1, cols], hh[c][:], hl[c][:], c == 0,
                      c == HC - 1).then_inc(s["down_done"], 1)

            def gelu0(b, k):
                e, c = k // HC, k % HC
                nc.scalar.wait_ge(s["up_ready"], CH * b + k + 1)
                if c < HC - 1:
                    need(nc.scalar, s["hl_ready"], (HC - 1) * (NE0 * b + e - 1) + c + 1)
                else:
                    need(nc.scalar, s["hp_ready"], NE0 * b + e)
                nc.scalar.activation(hid[c][:], bank[k % 4][:], ACT.Gelu_apprx_tanh,
                                     bias=vecs[:, V_B1 + k:V_B1 + k + 1]).then_inc(s["act_done"], 1)
                nc.scalar.wait_ge(s["act_done"], CH * b + k + 1)
                need(nc.scalar, s["down_done"], CH * b + k - 3)
                nc.scalar.copy(hh[c][:], hid[c][:]).then_inc(s["hh_ready"], 1)

            def hl_dve(v, b, k):
                e, c = k // HC, k % HC
                v.wait_ge(s["hh_ready"], CH * b + k + 1)
                nc.vector.tensor_tensor(hl[c][:], hid[c][:], hh[c][:], ALU.subtract).then_inc(s["hl_ready"], 1)

            def split_pool(b, e):
                c = HC - 1
                nc.gpsimd.wait_ge(s["hh_ready"], CH * b + HC * (e + 1))
                nc.gpsimd.tensor_tensor(hl[c][:], hid[c][:], hh[c][:], ALU.subtract).then_inc(s["hp_ready"], 1)

            def combine0(v, b, par, e):
                v.wait_ge(s["down_done"], CH * b + HC * (e + 1))
                v.wait_ge(s["bc_ready"], NE0 * b + e + 1)
                into = acc[par] if e == 0 else tmp[e % 2]
                if e:
                    need(v, s["mixed"], (NE0 - 1) * b + (e - 2 if e > 2 else 1 - e))
                nc.vector.scalar_tensor_tensor(out=into[:], in0=bank[4 + e % 2][:], scalar=vecs[:, V_B2 + e:V_B2 + e + 1],
                                               in1=coefB[:, e, :], op0=ALU.add, op1=ALU.mult).then_inc(s["y_used"], 1)

            def mix_pool(b, par, e):
                nc.gpsimd.wait_ge(s["y_used"], NE0 * b + e + 1)
                if e > 1:
                    nc.gpsimd.wait_ge(s["mixed"], (NE0 - 1) * b + e - 1)
                nc.gpsimd.tensor_tensor(acc[par][:], tmp[e % 2][:], acc[par][:], ALU.add).then_inc(s["mixed"], 1)

            def pe0(b, par, first_, last_):
                for k in range(CH):
                    up0(b, par, k, first_)
                    if k >= LAG:
                        down0(b, k - LAG)
                    elif not first_:
                        down0(b - 1, CH - LAG + k)
                    if k == 10 and not first_:
                        back_pe(b - 1, 1 - par)
                    if k == 19 and (more or not last_):
                        norm_pe(f0 + b + 1)
                    if k == 22 and not last_:
                        router_pe(b + 1, 1 - par)
                    if k == 29 and not last_:
                        coef_pe(b + 1)

            def act0(b, par, first_, last_):
                for k in range(CH):
                    if first_ and k % HC == 1 and k // HC + 2 < NE0:
                        w_hi_act(k // HC + 2)
                    gelu0(b, k)
                    if k == 20 and (more or not last_):
                        norm_act(f0 + b + 1, 1 - par)
                    if k == 21 and not last_:
                        xh_act(b + 1, 1 - par)
                    if k == 24 and not last_:
                        router_act(b + 1)
                    if k == 30 and not last_:
                        coef_act(b + 1)

            def dve0(v, b, par, first_, last_):
                for k in range(CH):
                    e, c = k // HC, k % HC
                    if c < HC - 1:
                        hl_dve(v, b, k)
                    if first_ and c == 2 and e + 2 < NE0:
                        w_lo_dve(v, e + 2)
                    if c == 2 and (e or not first_):
                        combine0(v, *((b, par, e - 1) if e else (b - 1, 1 - par, NE0 - 1)))
                    if k == 12 and not first_:
                        back_dve(v, b - 1)
                    if more or not last_:
                        if k == 13:
                            norm_a(v, f0 + b + 1, (b + 1) % B)
                        if k == 17:
                            norm_c(v, f0 + b + 1, (b + 1) % B)
                    if not last_:
                        if k == 22:
                            xl_dve(v, b + 1, 1 - par)
                        if k == 24:
                            router = router_a(v, b + 1)
                        if k == 25:
                            router_b(router)
                        if k == 27:
                            router_c(v, b + 1, router)

            def pool0(b, par, first_, last_):
                nc.gpsimd.wait_ge(s["row_loaded"], 16 * (b + 1))
                for e in range(NE0):
                    need(nc.gpsimd, s["y_used"], NE0 * (b - 1) + e + 1)
                    nc.gpsimd.nop(nofuse=True)
                    nc.gpsimd.partition_broadcast(coefB[:, e, :], row[0:1, e, :]).then_inc(s["bc_ready"], 1)
                    split_pool(b, e)
                    if e == 3 and (more or not last_):
                        norm_b(f0 + b + 1)
                    if e != 1 and (e or not first_):
                        mix_pool(*((b, par, e - 1) if e else (b - 1, 1 - par, NE0 - 1)))

            def sync0(b, par, first_, last_):
                if first_:
                    load0(2)
                    load0(3)
                row_sp(b, par, first_, last_)
                if first_:
                    for e in range(4, NE0):
                        load0(e)
                    if n == 0:
                        load_weights(nc.sync)

            SPLITS = ((0, 2), (2, IT))

            def g_hi_act():
                for k, (j0, j1) in enumerate(SPLITS):
                    nc.scalar.copy(gh[:, :, j0:j1, :], gate_up[:, :, j0:j1, :]).then_inc(s["w_hi"], 1)

            def g_lo_dve(v, k):
                j0, j1 = SPLITS[k]
                v.wait_ge(s["w_hi"], 2 * occ + k + 1)
                nc.vector.tensor_tensor(gl[:, :, j0:j1, :], gate_up[:, :, j0:j1, :], gh[:, :, j0:j1, :],
                                        ALU.subtract).then_inc(s["w_lo"], 1)

            def up1(b, par, j, first_):
                q = (par + j) % 2
                if j == 0:
                    nc.tensor.wait_ge(s["xl_ready"], b + 1)
                if first_ and j in (0, 2):
                    nc.tensor.wait_ge(s["w_lo"], 2 * occ + j // 2 + 1)
                need(nc.tensor, s["gated"], IT * b + j - 1)
                hi_lo(bank[2 * q][:], gh[:, 0, j, :], gl[:, 0, j, :], xh[par][:], xl[par][:], True, True)
                hi_lo(bank[2 * q + 1][:], gh[:, 1, j, :], gl[:, 1, j, :], xh[par][:], xl[par][:], True, True).then_inc(s["up_ready"], 1)

            def down1(b, par, j):
                if j == 0:
                    nc.tensor.wait_ge(s["gated"], IT * b + 1)
                    need(nc.tensor, s["acc_ready"], b - 1 if c0 else prior(b))
                else:
                    nc.tensor.wait_ge(s["hid_ready"], PAIRS * b + j)
                w = sh_d[:] if j == 0 else down_w[:, j - 1, :]
                nc.tensor.matmul(bank[4 + par][:], w, hid[slot(j)][:], start=(j == 0), stop=(j == IT - 1)).then_inc(s["down_done"], 1)

            def slot(j):
                return 4 if j == 0 else (j - 1) % 4

            def silu1(b, par, j):
                q = (par + j) % 2
                nc.scalar.wait_ge(s["up_ready"], IT * b + j + 1)
                nc.scalar.activation(silu[q][:], bank[2 * q][:], ACT.Silu).then_inc(s["act_done"], 1)

            def gate1(v, b, par, j):
                q = (par + j) % 2
                v.wait_ge(s["act_done"], IT * b + j + 1)
                if j == 0:
                    need(v, s["down_done"], IT * (b - 1) + 1)
                    nc.vector.scalar_tensor_tensor(out=hid[slot(0)][:], in0=silu[q][:], scalar=0.5, in1=bank[2 * q + 1][:],
                                                   op0=ALU.mult, op1=ALU.mult).then_inc(s["gated"], 1)
                    return
                need(v, s["hid_ready"], PAIRS * b + (j - 2 if j > 2 else 1 - j))
                nc.vector.tensor_tensor(tmp[q][:], silu[q][:], bank[2 * q + 1][:], ALU.mult).then_inc(s["gated"], 1)

            def weigh1(v, b, par, j):
                q = (par + j) % 2
                v.wait_ge(s["gated"], IT * b + j + 1)
                v.wait_ge(s["bc_ready"], PAIRS * b + j)
                need(v, s["down_done"], IT * b + j - (3 if j > 4 else 4))
                nc.vector.tensor_tensor(hid[slot(j)][:], tmp[q][:], coefB[:, j - 1, :], ALU.mult).then_inc(s["hid_ready"], 1)

            def sum1(v, b, par):
                v.wait_ge(s["down_done"], IT * (b + 1))
                nc.vector.tensor_copy(acc[par][:], bank[4 + par][:]).then_inc(s["acc_ready"], 1)

            LAG1 = 3

            def pe1(b, par, first_, last_):
                for j in range(IT):
                    up1(b, par, j, first_)
                    if j >= LAG1:
                        down1(b, par, j - LAG1)
                    elif not first_:
                        down1(b - 1, 1 - par, IT - LAG1 + j)
                    if j == 3 and (more or not last_):
                        norm_pe(f0 + b + 1)
                    if j == 4 and not last_:
                        router_pe(b + 1, 1 - par)
                    if j == 4 and not first_:
                        back_pe(b - 1, 1 - par)
                    if j == 7 and not last_:
                        coef_pe(b + 1)

            def act1(b, par, first_, last_):
                for j in range(IT):
                    silu1(b, par, j)
                    if j == 3 and (more or not last_):
                        norm_act(f0 + b + 1, 1 - par)
                        if not last_:
                            xh_act(b + 1, 1 - par)
                    if j == 4 and not last_:
                        router_act(b + 1)
                    if j == 7 and not last_:
                        coef_act(b + 1)

            def dve1(v, b, par, first_, last_):
                for j in range(IT):
                    gate1(v, b, par, j)
                    if j > 1:
                        weigh1(v, b, par, j - 1)
                    elif j == 0 and not first_:
                        weigh1(v, b - 1, 1 - par, IT - 1)
                    if j == 3 and not first_:
                        sum1(v, b - 1, 1 - par)
                    if j == 5 and not first_:
                        back_dve(v, b - 1)
                    if more or not last_:
                        if j == 0:
                            norm_a(v, f0 + b + 1, (b + 1) % B)
                        if j == 1:
                            norm_c(v, f0 + b + 1, (b + 1) % B)
                    if not last_:
                        if j == 3:
                            xl_dve(v, b + 1, 1 - par)
                        if j == 4:
                            router = router_a(v, b + 1)
                        if j == 5:
                            router_b(router)
                        if j == 6:
                            router_c(v, b + 1, router)

            def tensor(t):
                after_phases(t, n)
                if kind == 1:
                    t.wait_ge(w_loaded, 16 * N_WEIGHTS)
                router_pe(c0, 0)
                coef_pe(c0)
                sequences(t, pe0 if kind == 0 else pe1, c0)
                if kind == 0:
                    for k in range(LAG):
                        down0(c0 + B - 1, CH - LAG + k)
                else:
                    for j in range(IT - LAG1, IT):
                        down1(c0 + B - 1, 1, j)
                back_pe(c0 + B - 1, 1)

            def scalar(c):
                after_phases(c, n)
                xh_act(c0, 0)
                if kind == 0:
                    w_hi_act(0)
                    w_hi_act(1)
                else:
                    c.wait_ge(w_loaded, 16 * N_WEIGHTS)
                    g_hi_act()
                router_act(c0)
                coef_act(c0)
                sequences(c, act0 if kind == 0 else act1, c0)

            def vector(v):
                after_phases(v, n)
                xl_dve(v, c0, 0)
                if kind == 0:
                    w_lo_dve(v, 0)
                    w_lo_dve(v, 1)
                else:
                    g_lo_dve(v, 0)
                    g_lo_dve(v, 1)
                router_dve(v, c0)
                sequences(v, lambda b, par, f, l: (dve0 if kind == 0 else dve1)(v, b, par, f, l), c0)
                if kind == 0:
                    combine0(v, c0 + B - 1, 1, NE0 - 1)
                else:
                    weigh1(v, c0 + B - 1, 1, IT - 1)
                    sum1(v, c0 + B - 1, 1)
                back_dve(v, c0 + B - 1)

            def gpsimd(g):
                after_phases(g, n)
                sequences(g, pool0 if kind == 0 else pool1, c0)
                if kind == 0:
                    mix_pool(c0 + B - 1, 1, NE0 - 1)

            def sync(q):
                if kind == 0:
                    load0(0)
                    load0(1)
                    if n == 0:
                        load_x_rest(q)
                after_phases(q, n)
                sequences(q, sync0 if kind == 0 else row_sp, c0)

            return {"tensor": tensor, "scalar": scalar, "vector": vector, "gpsimd": gpsimd, "sync": sync}

        def attn_phase(n):
            f0 = B * n
            names = ("q_ps", "kk_ps", "vv_ps", "k_ps", "v_ps", "q_sb", "kk_sb", "vv_sb", "k_sb", "v_sb", "q_split", "k_split",
                     "q_chain", "k_chain", "zeroed", "m_consts", "qk_ones", "v9_ready", "mx_ready", "mx_read", "m_chain",
                     "m_split", "mT_ps", "mT_sb", "st_ready", "exp_done", "av_done", "o_sb", "oT_ps", "o_tok", "o_chain",
                     "otT_ps", "ot_sb", "z_ready", "x_bo")
            s = {k: sem(f"p{n}_{k}") for k in names}
            saved = {c: sem(f"p{n}_{c}_saved") for c in "qk"}
            ld = [[sem(f"p{n}_qk_loaded{i}{g}") for g in range(H // HG)] for i in range(2)]
            m_ld = [[sem(f"p{n}_m_loaded{i}{g}") for g in range(H // HG)] for i in range(2)]
            new_phase()
            qa = [view(P, H * T, BF16).rearrange("p (h t) -> p h t", h=H) for _ in range(2)]
            ka = [view(P, H * T, BF16).rearrange("p (h t) -> p h t", h=H) for _ in range(2)]
            v_all = view(P, B * TILES * H * (HD + 1)).rearrange("p (n h d) -> p n h d", h=H, d=HD + 1)
            v9 = [view(P, TILES * H * (HD + 1)).rearrange("p (n h d) -> p n h d", h=H, d=HD + 1) for _ in range(2)]
            new_part()
            q_sb, kk_sb, vv_sb, k_sb = (view(P, T) for _ in range(4))
            rest = {"q": view(P, T), "k": view(P, T)}
            parts = {c: [view(P, 3 * T, BF16).rearrange("p (j t) -> p j t", j=3) for _ in range(2)] for c in "qk"}
            new_part()
            probs = [view(P, HG * T).rearrange("p (h t) -> p h t", h=HG) for _ in range(2)]
            o_sb = view(P, T)
            o_tok = view(P, T).rearrange("p (i e) -> p i e", i=TILES)
            ot_sb = view(P, T)
            xbo = view(P, T)
            mneg = view(P, TILES * H).rearrange("p (i h) -> p i h", i=TILES)
            mrest = view(P, TILES * HG).rearrange("p (i h) -> p i h", i=TILES)
            mparts = view(P, TILES * 3 * HG, BF16).rearrange("p (i j h) -> p i j h", i=TILES, j=3)
            rec = view(P, TILES * HG).rearrange("p (i h) -> p i h", i=TILES)
            mT = [[view(3 * HG, T, BF16) for _ in range(H // HG)] for _ in range(2)]
            zero3, ones3 = view(3, T, BF16), view(3, T, BF16)
            scratch = {c: nc.dram_tensor(f"p{n}_{c}_parts", (B, 3, P, T), BF16, kind="Internal").ap() for c in "qk"}
            scale = float(HD) ** -0.5

            STEPS = (H // HG) * TILES

            def pe_a(b, par, first_, last_):
                x = xnT[par][:]
                nc.tensor.wait_ge(xnT_ready, f0 + b + 1)
                for i, (w, ps, sb_) in enumerate(((wq_p[:], "q_ps", "q_sb"), (wk[:], "kk_ps", "kk_sb"), (wv[:], "vv_ps", "vv_sb"))):
                    need(nc.tensor, s[sb_], b)
                    nc.tensor.matmul(bank[i][:], w, x, start=True, stop=True).then_inc(s[ps], 1)
                nc.tensor.wait_ge(s["kk_sb"], b + 1)
                need(nc.tensor, s["k_sb"], b)
                nc.tensor.matmul(bank[3][:], wl_p[:], kk_sb[:], start=True, stop=True).then_inc(s["k_ps"], 1)
                nc.tensor.wait_ge(s["vv_sb"], b + 1)
                need(nc.tensor, s["v_sb"], b)
                for i in range(TILES):
                    last = nc.tensor.matmul(bank[4][:, i * P:(i + 1) * P], vv_sb[:, i * P:(i + 1) * P], wl[:], start=True, stop=True)
                last.then_inc(s["v_ps"], 1)
                if not last_:
                    norm_pe(f0 + b + 1)

            def act_a(b, par, first_, last_):
                def biased(i, ps, dst, at, done, free, count):
                    nc.scalar.wait_ge(s[ps], b + 1)
                    need(nc.scalar, s[free], count)
                    nc.scalar.activation(dst[:], bank[i][:], ACT.Identity, bias=vecs[:, at:at + 1]).then_inc(s[done], 1)
                biased(1, "kk_ps", kk_sb, V_BK, "kk_sb", "k_ps", b)
                biased(2, "vv_ps", vv_sb, V_BV, "vv_sb", "v_ps", b)
                biased(0, "q_ps", q_sb, V_BQ, "q_sb", "q_split", b)
                biased(3, "k_ps", k_sb, V_BL, "k_sb", "k_split", b)
                if not last_:
                    norm_act(f0 + b + 1, 1 - par)

            def split(eng, c, src, b, par):
                eng.wait_ge(s[c + "_sb"], b + 1)
                need(eng, saved[c], 16 * b)
                chain = Chain(eng, s[c + "_chain"], 3)
                chain.begin(b)
                p_, r = parts[c][par], rest[c]
                eng.nop(nofuse=True)
                chain(eng.tensor_copy(p_[:, 0, :], src[:]))
                chain(eng.tensor_tensor(r[:], src[:], p_[:, 0, :], ALU.subtract))
                eng.nop(nofuse=True)
                chain(eng.tensor_copy(p_[:, 1, :], r[:]))
                chain.end()
                eng.tensor_tensor(p_[:, 2, :], r[:], p_[:, 1, :], ALU.subtract).then_inc(s[c + "_split"], 1)

            def dve_a(v, b, par, first_, last_):
                if not last_:
                    norm_a(v, f0 + b + 1, b + 1)
                    norm_c(v, f0 + b + 1, b + 1)
                v.wait_ge(s["v_ps"], b + 1)
                nc.vector.tensor_tensor(
                    v_all[:, bass.ds(b * TILES, TILES), :, 0:HD], bank[4][:].rearrange("p (i h d) -> p i h d", i=TILES, d=HD),
                    bl_bc[:].rearrange("p (h d) -> p h d", d=HD).unsqueeze(1).to_broadcast([P, TILES, H, HD]),
                    ALU.add).then_inc(s["v_sb"], 1)
                need(v, s["q_split"], b)
                split(nc.vector, "q", q_sb, b, par)

            def pool_a(b, par, first_, last_):
                if not last_:
                    norm_b(f0 + b + 1)
                need(nc.gpsimd, s["k_split"], b)
                split(nc.gpsimd, "k", k_sb, b, par)

            def sp_a(b, par, first_, last_):
                for c in "qk":
                    nc.sync.wait_ge(s[c + "_split"], b + 1)
                    nc.sync.dma_start(scratch[c][bass.ds(b, 1)].rearrange("o j p t -> p (o j) t"), parts[c][par][:]).then_inc(saved[c], 16)

            NLD = 7
            M0, M1 = 6 * HD, 6 * HD + 3
            GB = H // HG

            def load(b, par, g):
                q, k = (scratch[c][bass.ds(b, 1)].rearrange("o j (d h) t -> (o j d) h t", h=H)[:, g * HG:(g + 1) * HG, :] for c in "qk")
                hs = slice(g * HG, (g + 1) * HG)
                for r, j, w in ((0, 0, 3), (3, 1, 2), (5, 2, 1)):
                    src = q[j * HD:(j + 1) * HD].unsqueeze(0).to_broadcast([w, HD, HG, T])
                    nc.sync.dma_start(qa[par][r * HD:(r + w) * HD, hs, :], src).then_inc(ld[par][g], 16)
                for r, j, w in ((0, 0, 3), (3, 0, 2), (5, 0, 1)):
                    nc.sync.dma_start(ka[par][r * HD:(r + w) * HD, hs, :], k[j * HD:(j + w) * HD]).then_inc(ld[par][g], 16)
                nc.sync.dma_start(qa[par][M0:M1, hs, :], zero3.unsqueeze(1).to_broadcast([3, HG, T])).then_inc(ld[par][g], 16)

            def max_pe(b, par, t):
                h, i = t // TILES, t % TILES
                if t % (HG * TILES) == 0:
                    nc.tensor.wait_ge(ld[par][h // HG], 16 * NLD * (b // 2 + 1))
                need(nc.tensor, s["mx_read"], H * TILES * b + t - 1)
                nc.tensor.matmul(bank[t % 2][:], qa[par][:, h, i * P:(i + 1) * P], ka[par][:, h, :], start=True, stop=True).then_inc(s["mx_ready"], 1)

            def max_dve(v, b, t):
                h, i = t // TILES, t % TILES
                v.wait_ge(s["mx_ready"], H * TILES * b + t + 1)
                nc.vector.tensor_reduce(mneg[:, i, h:h + 1], bank[t % 2][:], AX_X, ALU.max, negate=True).then_inc(s["mx_read"], 1)

            def msplit_dve(v, b, g):
                chain = Chain(v, s["m_chain"], 3)
                chain.begin(b * (H // HG) + g)
                v.wait_ge(s["mx_read"], H * TILES * b + HG * TILES * (g + 1))
                need(v, s["mT_ps"], b * (H // HG) + g)
                m = mneg[:, :, g * HG:(g + 1) * HG]
                chain(nc.vector.tensor_copy(mparts[:, :, 0, :], m))
                chain(nc.vector.tensor_tensor(mrest[:], m, mparts[:, :, 0, :], ALU.subtract))
                chain(nc.vector.tensor_copy(mparts[:, :, 1, :], mrest[:]))
                chain.end()
                nc.vector.tensor_tensor(mparts[:, :, 2, :], mrest[:], mparts[:, :, 1, :], ALU.subtract).then_inc(s["m_split"], 1)

            def mT_pe(b, g):
                nc.tensor.wait_ge(s["m_split"], b * GB + g + 1)
                for i in range(TILES):
                    last = nc.tensor.transpose(bank[7][:].bitcast(BF16)[0:3 * HG, i * P:(i + 1) * P],
                                               mparts[:, i, :, :].rearrange("p j h -> p (j h)"), identb[:])
                last.then_inc(s["mT_ps"], 1)

            def mT_act(b, par, g):
                nc.scalar.wait_ge(s["mT_ps"], b * GB + g + 1)
                nc.scalar.copy(mT[par][g][:], bank[7][:].bitcast(BF16)[0:3 * HG, 0:T]).then_inc(s["mT_sb"], 1)

            def m_sp(b, par, g):
                nc.sync.wait_ge(s["mT_sb"], b * GB + g + 1)
                nc.sync.dma_start(qa[par][M0:M1, g * HG:(g + 1) * HG, :], mT[par][g][:]).then_inc(m_ld[par][g], 16)

            def st_pe(b, par, st, hh):
                g, kt = st // TILES, st % TILES
                t = HG * st + hh
                if kt == 0 and hh == 0:
                    nc.tensor.wait_ge(m_ld[par][g], 16 * ((b // 2) + 1))
                need(nc.tensor, s["exp_done"], H * TILES * b + t - 3)
                nc.tensor.matmul(bank[2 + t % 4][:], ka[par][:, g * HG + hh, kt * P:(kt + 1) * P], qa[par][:, g * HG + hh, :],
                                 start=True, stop=True).then_inc(s["st_ready"], 1)

            def exp_act(b, st, hh):
                t = HG * st + hh
                if hh == 0:
                    need(nc.scalar, s["av_done"], STEPS * b + st - 1)
                nc.scalar.wait_ge(s["st_ready"], H * TILES * b + t + 1)
                nc.scalar.activation(probs[st % 2][:, hh, :], bank[2 + t % 4][:], ACT.Exp, scale=scale).then_inc(s["exp_done"], 1)

            def av_pe(b, par, st):
                g, kt = st // TILES, st % TILES
                nc.tensor.wait_ge(s["exp_done"], H * TILES * b + HG * (st + 1))
                if st == 0:
                    nc.tensor.wait_ge(s["v9_ready"], b + 1)
                if kt == 0:
                    need(nc.tensor, s["o_sb"], GB * b + g)
                for hh in range(HG):
                    last = nc.tensor.matmul(bank[6][32 * hh:32 * hh + HD + 1, :], v9[par][:, kt, g * HG + hh, :], probs[st % 2][:, hh, :],
                                            start=(kt == 0), stop=(kt == TILES - 1))
                last.then_inc(s["av_done"], 1)

            def o_act(b, g):
                nc.scalar.wait_ge(s["av_done"], STEPS * b + TILES * (g + 1))
                need(nc.scalar, s["oT_ps"], GB * b + g)
                nc.scalar.copy(o_sb[:], bank[6][:]).then_inc(s["o_sb"], 1)

            def o_pe(b, g):
                nc.tensor.wait_ge(s["o_sb"], GB * b + g + 1)
                for i in range(TILES):
                    last = nc.tensor.transpose(bank[7][:, i * P:(i + 1) * P], o_sb[:, i * P:(i + 1) * P], ident[:])
                last.then_inc(s["oT_ps"], 1)

            def o_dve(v, b, g):
                v.wait_ge(s["oT_ps"], GB * b + g + 1)
                if g == 0:
                    need(v, s["otT_ps"], b)
                o = bank[7][:].rearrange("p (i h c) -> p i h c", i=TILES, h=HG)
                need(v, s["o_tok"], GB * b + g)
                nc.vector.reciprocal(rec[:], o[:, :, :, HD]).then_inc(s["o_chain"], 1)
                v.wait_ge(s["o_chain"], GB * b + g + 1)
                nc.vector.tensor_tensor(
                    o_tok[:, :, g * HG * HD:(g + 1) * HG * HD].rearrange("p i (h d) -> p i h d", h=HG), o[:, :, :, 0:HD],
                    rec[:].unsqueeze(3).to_broadcast([P, TILES, HG, HD]), ALU.mult).then_inc(s["o_tok"], 1)

            def ot_pe(b):
                nc.tensor.wait_ge(s["o_tok"], GB * (b + 1))
                for i in range(TILES):
                    last = nc.tensor.transpose(bank[7][:, i * P:(i + 1) * P], o_tok[:, i, :], ident[:])
                last.then_inc(s["otT_ps"], 1)

            def ot_act(b):
                nc.scalar.wait_ge(s["otT_ps"], b + 1)
                nc.scalar.copy(ot_sb[:], bank[7][:]).then_inc(s["ot_sb"], 1)

            def z_pe(b):
                nc.tensor.wait_ge(s["ot_sb"], b + 1)
                for i in range(TILES):
                    last = nc.tensor.matmul(bank[7][:, i * P:(i + 1) * P], ot_sb[:, i * P:(i + 1) * P], wo[:], start=True, stop=True)
                last.then_inc(s["z_ready"], 1)

            def xbo_pool(b):
                need(nc.gpsimd, x_upd, f0 + b)
                nc.gpsimd.tensor_tensor(xbo[:], flat(x_of(b)), flat(bo_bc[:]), ALU.add).then_inc(s["x_bo"], 1)

            def z_dve(v, b):
                v.wait_ge(s["z_ready"], b + 1)
                v.wait_ge(s["x_bo"], b + 1)
                nc.vector.tensor_tensor(flat(x_of(b)), bank[7][:], xbo[:], ALU.add).then_inc(x_upd, 1)

            def pe_b(b, par, first_, last_):
                for st in range(STEPS):
                    g, kt = st // TILES, st % TILES
                    for hh in range(2):
                        st_pe(b, par, st, hh)
                        if not last_:
                            max_pe(b + 1, 1 - par, HG * st + hh)
                    if st:
                        av_pe(b, par, st - 1)
                    elif not first_:
                        av_pe(b - 1, 1 - par, STEPS - 1)
                    for hh in range(2, HG):
                        st_pe(b, par, st, hh)
                        if not last_:
                            max_pe(b + 1, 1 - par, HG * st + hh)
                    if st == 0:
                        need(nc.tensor, s["o_tok"], GB * b - 1)
                        nc.tensor.wait_ge(s["mT_sb"], GB * b + GB - 1)
                        mT_pe(b, GB - 1)
                    elif kt == 0 and not last_:
                        if g == 1:
                            need(nc.tensor, x_upd, f0 + b)
                        else:
                            nc.tensor.wait_ge(s["o_tok"], GB * b + g - 1)
                        nc.tensor.wait_ge(s["mT_sb"], GB * b + GB + g - 1)
                        mT_pe(b + 1, g - 1)
                    if st == 1 and not first_:
                        nc.tensor.wait_ge(s["mT_sb"], GB * b + GB)
                        o_pe(b - 1, GB - 1)
                    elif st > 1 and kt == 1:
                        if last_:
                            nc.tensor.wait_ge(x_upd, f0 + b)
                            nc.tensor.wait_ge(s["o_tok"], GB * b + g - 1)
                        else:
                            nc.tensor.wait_ge(s["mT_sb"], GB * b + GB + g)
                        o_pe(b, g - 1)
                    if st == 2 and not first_:
                        ot_pe(b - 1)
                    if st == 3 and not first_:
                        z_pe(b - 1)

            def act_b(b, par, first_, last_):
                for st in range(STEPS):
                    g, kt = st // TILES, st % TILES
                    for hh in range(HG):
                        exp_act(b, st, hh)
                        if hh == 1 and kt == 0:
                            if st:
                                o_act(b, g - 1)
                            elif not first_:
                                o_act(b - 1, GB - 1)
                    if kt == 0:
                        if st == 0:
                            mT_act(b, par, GB - 1)
                        elif not last_:
                            mT_act(b + 1, 1 - par, g - 1)
                    if st == 2 and not first_:
                        ot_act(b - 1)

            def dve_b(v, b, par, first_, last_):
                for st in range(STEPS):
                    g, kt = st // TILES, st % TILES
                    if not last_:
                        for hh in range(HG):
                            max_dve(v, b + 1, HG * st + hh)
                    if kt == 3 and not last_:
                        msplit_dve(v, b + 1, g)
                    if kt == 1:
                        if st > 1:
                            o_dve(v, b, g - 1)
                        elif not first_:
                            o_dve(v, b - 1, GB - 1)
                    if st == 3 and not first_:
                        z_dve(v, b - 1)

            def sp_b(b, par, first_, last_):
                m_sp(b, par, GB - 1)
                if last_:
                    return
                for g in range(GB):
                    nc.sync.wait_ge(s["st_ready"], H * TILES * b + HG * TILES * (g + 1))
                    load((b + 2) % B, par, g)
                    if g < GB - 1:
                        m_sp(b + 1, 1 - par, g)

            def pool_b(b, par, first_, last_):
                need(nc.gpsimd, s["av_done"], STEPS * prior(b))
                nc.gpsimd.nop(nofuse=True)
                nc.gpsimd.tensor_copy(v9[par][:].rearrange("p n h d -> p (n h d)"),
                                      v_all[:, bass.ds(b * TILES, TILES), :, :].rearrange("p n h d -> p (n h d)")).then_inc(s["v9_ready"], 1)
                xbo_pool(b)

            def tensor(t):
                after_phases(t, n)
                t.wait_ge(w_loaded, 16 * N_WEIGHTS)
                t.wait_ge(tables_ready, 2)
                sequences(t, pe_a)
                nc.tensor.wait_ge(s["k_sb"], B)
                nc.tensor.wait_ge(s["q_sb"], B)
                nc.tensor.wait_ge(s["vv_sb"], B)
                nc.tensor.wait_ge(s["v_sb"], B)
                nc.tensor.wait_ge(s["zeroed"], 6)
                nc.tensor.wait_ge(s["qk_ones"], 32)
                nc.tensor.wait_ge(xnT_ready, f0 + B)
                for t_ in range(H * TILES):
                    max_pe(0, 0, t_)
                    if t_ % (HG * TILES) == HG * TILES - 1 and t_ < H * TILES - 1:
                        need(nc.tensor, s["mT_sb"], t_ // (HG * TILES))
                        mT_pe(0, t_ // (HG * TILES))
                sequences(t, pe_b)
                av_pe(B - 1, 1, STEPS - 1)
                nc.tensor.wait_ge(s["o_tok"], GB * B - 1)
                o_pe(B - 1, GB - 1)
                ot_pe(B - 1)
                for g in range(GB):
                    nc.tensor.wait_ge(ld[0][g], 16 * NLD * (B // 2 + 1))
                z_pe(B - 1)
                norm_pe(f0 + B)

            def scalar(c):
                after_phases(c, n)
                sequences(c, act_a)
                nc.scalar.wait_ge(s["q_split"], B)
                nc.scalar.wait_ge(s["k_split"], B)
                nc.scalar.wait_ge(s["v_ps"], B)
                for c_ in "qk":
                    nc.scalar.wait_ge(saved[c_], 16 * B)
                for g in range(GB - 1):
                    mT_act(0, 0, g)
                sequences(c, act_b)
                o_act(B - 1, GB - 1)
                ot_act(B - 1)
                norm_act(f0 + B, 0)

            def vector(v):
                after_phases(v, n)
                v.wait_ge(tables_ready, 2)
                for m in (qa[0], ka[0]):
                    nc.vector.memset(m[:], 0.0).then_inc(s["zeroed"], 1)
                nc.vector.memset(bank[6][:], 0.0).then_inc(s["zeroed"], 1)
                nc.vector.memset(v_all[:, :, :, HD:], 1.0).then_inc(s["zeroed"], 1)
                sequences(v, lambda b, par, f, l: dve_a(v, b, par, f, l))
                for c_ in "qk":
                    v.wait_ge(saved[c_], 16 * B)
                v.wait_ge(s["v_ps"], B)
                v.wait_ge(s["k_split"], B)
                nc.vector.memset(zero3, 0.0).then_inc(s["m_consts"], 1)
                nc.vector.memset(ones3, 1.0).then_inc(s["m_consts"], 1)
                for t_ in range(H * TILES):
                    max_dve(v, 0, t_)
                    if t_ % (HG * TILES) == HG * TILES - 1:
                        msplit_dve(v, 0, t_ // (HG * TILES))
                sequences(v, lambda b, par, f, l: dve_b(v, b, par, f, l))
                o_dve(v, B - 1, GB - 1)
                z_dve(v, B - 1)
                norm_a(v, f0 + B, 0)
                norm_c(v, f0 + B, 0)

            def gpsimd(g):
                g.wait_ge(w_loaded, 16 * N_WEIGHTS)
                g.partition_broadcast(bl_bc[:], bl_bc[0:1, :])
                for i in range(TILES):
                    last = g.partition_broadcast(bo_bc[:, TILES - 1 - i, :], bo_bc[0:1, 0, :])
                for w, w_p in ((wq, wq_p), (wl, wl_p)):
                    last = g.tensor_copy(w_p[:].rearrange("p (d h) -> p d h", d=HD), w[:].rearrange("p (h d) -> p d h", d=HD))
                last.then_inc(tables_ready, 1)
                after_phases(g, n)
                for m in (qa[1], ka[1]):
                    nc.gpsimd.memset(m[:], 0.0).then_inc(s["zeroed"], 1)
                sequences(g, pool_a)
                nc.gpsimd.wait_ge(s["v_sb"], B)
                nc.gpsimd.wait_ge(s["q_split"], B)
                for c_ in "qk":
                    nc.gpsimd.wait_ge(saved[c_], 16 * B)
                sequences(g, pool_b)
                norm_b(f0 + B)

            def sync(q):
                after_phases(q, n)
                sequences(q, sp_a)
                for c_ in "qk":
                    q.wait_ge(saved[c_], 16 * B)
                q.wait_ge(s["zeroed"], 6)
                q.wait_ge(s["m_consts"], 2)
                for m in ka:
                    q.dma_start(m[M0:M1, :, :], ones3.unsqueeze(1).to_broadcast([3, H, T])).then_inc(s["qk_ones"], 16)
                for i in range(2):
                    for g in range(GB):
                        load(i, i, g)
                for g in range(GB - 1):
                    m_sp(0, 0, g)
                sequences(q, sp_b)

            return {"tensor": tensor, "scalar": scalar, "vector": vector, "gpsimd": gpsimd, "sync": sync}

        def ssm_phase(n):
            f0 = B * n
            names = ("xs_ps", "xs_sb", "edges", "conv_chain", "conv", "xs_act", "z_act", "dtlo_ps", "dtlo_sb", "bc_ps", "bc_sb",
                     "bs_chain", "bs", "dt_ps", "relu", "e_sb", "ln", "dsum_chain", "dsum", "dm_ps", "decay", "decay_rows",
                     "bs_ps", "scanned", "s_ps", "s_tok", "y", "y_chain", "y_mv", "y_var", "y_rs", "yn", "ynT_ps", "yg", "yz", "z_ready")
            s = {k: sem(f"p{n}_{k}") for k in names}
            new_phase()
            z_all = view(P, DC * B * T).rearrange("p (c b t) -> p c b t", c=DC, b=B)
            dtlo_all = view(DTR, B * T).rearrange("p (b t) -> p b t", b=B)
            decays = view(1, B * T).rearrange("p (b t) -> p b t", b=B)
            c_all = view(P, B * TILES * DS).rearrange("p (n d) -> p n d", d=DS)
            bs_all = view(P, TILES * B).rearrange("p (i b) -> p i b", i=TILES)
            s_tok = view(P, B * TILES).rearrange("p (b i) -> p b i", b=B)
            decay8, state8 = view(B, T), view(B, T)
            new_part()
            xs_pad = [view(P, T + 2) for _ in range(DC)]
            conv = [view(P, T) for _ in range(DC)]
            xs = [[view(P, T) for _ in range(DC)] for _ in range(2)]
            bcx = view(P, TILES * (2 * DS + 1)).rearrange("p (i n) -> p i n", i=TILES)
            bx = view(P, TILES * DS).rearrange("p (i d) -> p i d", i=TILES)
            new_part()
            relu_t = [view(P, DC * T).rearrange("p (c t) -> p c t", c=DC) for _ in range(2)]
            e_t = view(P, DC * T).rearrange("p (c t) -> p c t", c=DC)
            ln_t = view(P, DC * T).rearrange("p (c t) -> p c t", c=DC)
            dsum_t = [view(P, T) for _ in range(2)]
            new_part()
            y = view(P, TILES * DS).rearrange("p (i d) -> p i d", i=TILES)
            yn = view(P, T)
            yg = [view(P, T) for _ in range(DC)]
            yz = [[view(P, T) for _ in range(DC)] for _ in range(2)]
            at_bc, n_bc = DTR, 2 * DS + 1

            def pe_1(b, par, first_, last_):
                nc.tensor.wait_ge(xnT_ready, f0 + b + 1)
                for c in range(DC):
                    need(nc.tensor, s["xs_sb"], DC * b)
                    nc.tensor.matmul(bank[c][:], w_in[:, c * P:(c + 1) * P], xnT[par][:], start=True, stop=True).then_inc(s["xs_ps"], 1)
                for c in range(DC):
                    need(nc.tensor, s["z_act"], DC * b)
                    nc.tensor.matmul(bank[2 + c][:], w_in[:, DI + c * P:DI + (c + 1) * P], xnT[par][:], start=True, stop=True).then_inc(s["xs_ps"], 1)
                if not last_:
                    norm_pe(f0 + b + 1)
                nc.tensor.wait_ge(s["xs_act"], DC * (b + 1))
                need(nc.tensor, s["dtlo_sb"], b)
                for c in range(DC):
                    last = nc.tensor.matmul(bank[4][0:DTR, :], w_x[:, c, 0:DTR], xs[par][c][:], start=(c == 0), stop=(c == DC - 1))
                last.then_inc(s["dtlo_ps"], 1)
                need(nc.tensor, s["bc_sb"], b)
                for i in range(TILES):
                    for c in range(DC):
                        last = nc.tensor.matmul(bank[5][:, i * n_bc:(i + 1) * n_bc], xs[par][c][:, i * P:(i + 1) * P], w_x[:, c, at_bc:],
                                                start=(c == 0), stop=(c == DC - 1))
                last.then_inc(s["bc_ps"], 1)

            def act_1(b, par, first_, last_):
                for c in range(DC):
                    nc.scalar.wait_ge(s["xs_ps"], 2 * DC * b + c + 1)
                    need(nc.scalar, s["conv"], DC * (b - 1) + c + 1)
                    nc.scalar.copy(xs_pad[c][:, 1:T + 1], bank[c][:]).then_inc(s["xs_sb"], 1)
                for c in range(DC):
                    nc.scalar.wait_ge(s["xs_ps"], 2 * DC * b + DC + c + 1)
                    nc.scalar.activation(z_all[:, c, bass.ds(b, 1), :], bank[2 + c][:], ACT.Silu).then_inc(s["z_act"], 1)
                if not last_:
                    norm_act(f0 + b + 1, 1 - par)
                for c in range(DC):
                    nc.scalar.wait_ge(s["conv"], DC * b + c + 1)
                    need(nc.scalar, s["bc_ps"], prior(b))
                    nc.scalar.activation(xs[par][c][:], conv[c][:], ACT.Silu).then_inc(s["xs_act"], 1)
                nc.scalar.wait_ge(s["dtlo_ps"], b + 1)
                nc.scalar.copy(dtlo_all[:, bass.ds(b, 1), :], bank[4][0:DTR, :]).then_inc(s["dtlo_sb"], 1)

            def dve_1(v, b, par, first_, last_):
                chain = Chain(v, s["conv_chain"], 2 * DC)
                chain.begin(b)
                for c in range(DC):
                    v.wait_ge(s["xs_sb"], DC * b + c + 1)
                    need(v, s["xs_act"], DC * (b - 1) + c + 1)
                    w = [w_conv[:, c, k:k + 1] for k in range(3)]
                    chain(nc.vector.tensor_scalar(conv[c][:], xs_pad[c][:, 1:T + 1], w[1], None, ALU.mult))
                    chain(nc.vector.scalar_tensor_tensor(out=conv[c][:], in0=xs_pad[c][:, 0:T], scalar=w[0], in1=conv[c][:],
                                                         op0=ALU.mult, op1=ALU.add))
                    nc.vector.scalar_tensor_tensor(out=conv[c][:], in0=xs_pad[c][:, 2:T + 2], scalar=w[2], in1=conv[c][:],
                                                   op0=ALU.mult, op1=ALU.add).then_inc(s["conv"], 1)
                chain.end()
                if not last_:
                    norm_a(v, f0 + b + 1, b + 1)
                    norm_c(v, f0 + b + 1, b + 1)
                chain = Chain(v, s["bs_chain"], 2)
                chain.begin(b)
                v.wait_ge(s["bc_ps"], b + 1)
                need(v, s["bs"], b)
                nc.vector.tensor_copy(bcx[:], bank[5][:, 0:TILES * n_bc].rearrange("p (i n) -> p i n", i=TILES)).then_inc(s["bc_sb"], 1)
                v.wait_ge(s["bc_sb"], b + 1)
                chain(nc.vector.tensor_tensor(bx[:], bcx[:, :, 0:DS], bcx[:, :, 2 * DS:].to_broadcast([P, TILES, DS]), ALU.mult))
                chain(nc.vector.tensor_reduce(bs_all[:, :, bass.ds(b, 1)], bx[:], AX_X, ALU.add))
                chain.end()
                nc.vector.tensor_copy(c_all[:, bass.ds(b * TILES, TILES), :], bcx[:, :, DS:2 * DS]).then_inc(s["bs"], 1)

            def pe_2(b, par, first_, last_):
                for c in range(DC):
                    need(nc.tensor, s["e_sb"], prior(b))
                    last = nc.tensor.matmul(bank[2 * par + c][:], w_dt[:, c * P:(c + 1) * P],
                                            dtlo_all[:, bass.ds(b, 1), :].rearrange("p o t -> p (o t)"), start=True, stop=True)
                last.then_inc(s["dt_ps"], 1)
                if not first_:
                    mean_pe(b - 1, 1 - par)

            def mean_pe(b, par):
                nc.tensor.wait_ge(s["dsum"], b + 1)
                nc.tensor.matmul(bank[4 + par][0:1, :], w_x[:, 0, DTR + 2 * DS:], dsum_t[par][:], start=True, stop=True).then_inc(s["dm_ps"], 1)

            def act_2(b, par, first_, last_):
                nc.scalar.wait_ge(s["dt_ps"], b + 1)
                need(nc.scalar, s["dsum"], prior(b))
                for c in range(DC):
                    bias = vecs[:, V_BDT + c:V_BDT + c + 1]
                    nc.scalar.activation(relu_t[par][:, c, :], bank[2 * par + c][:], ACT.Relu, bias=bias).then_inc(s["relu"], 1)
                need(nc.scalar, s["ln"], b)
                for c in range(DC):
                    bias = vecs[:, V_BDT + c:V_BDT + c + 1]
                    nc.scalar.activation(e_t[:, c, :], bank[2 * par + c][:], ACT.Abs, bias=bias).then_inc(s["relu"], 1)
                nc.scalar.wait_ge(s["relu"], 2 * DC * (b + 1))
                nc.scalar.activation(e_t[:], e_t[:], ACT.Exp, scale=-1.0).then_inc(s["e_sb"], 1)
                if not first_:
                    decay_act(b - 1, 1 - par)
                nc.scalar.wait_ge(s["e_sb"], b + 1)
                need(nc.scalar, s["dsum"], b)
                nc.scalar.activation(ln_t[:], e_t[:], ACT.Ln, bias=1.0).then_inc(s["ln"], 1)

            def decay_act(b, par):
                nc.scalar.wait_ge(s["dm_ps"], b + 1)
                nc.scalar.activation(decays[0:1, bass.ds(b, 1), :], bank[4 + par][0:1, :], ACT.Exp, scale=-1.0).then_inc(s["decay"], 1)

            def dve_2(v, b, par, first_, last_):
                chain = Chain(v, s["dsum_chain"], 2)
                chain.begin(b)
                v.wait_ge(s["relu"], 2 * DC * b + DC)
                need(v, s["dm_ps"], prior(b))
                d = dsum_t[par]
                chain(nc.vector.tensor_tensor(d[:], relu_t[par][:, 0, :], relu_t[par][:, 1, :], ALU.add))
                v.wait_ge(s["ln"], b + 1)
                chain(nc.vector.tensor_tensor(d[:], d[:], ln_t[:, 0, :], ALU.add))
                chain.end()
                nc.vector.tensor_tensor(d[:], d[:], ln_t[:, 1, :], ALU.add).then_inc(s["dsum"], 1)

            def dve_4a(v, b):
                chain = Chain(v, s["y_chain"], 2)
                chain.begin(b)
                chain(nc.vector.tensor_tensor(y[:], c_all[:, bass.ds(b * TILES, TILES), :],
                                              s_tok[:, bass.ds(b, 1), :].rearrange("p o i -> p (o i)").unsqueeze(2).to_broadcast([P, TILES, DS]),
                                              ALU.mult))
                for i in range(TILES):
                    last = nc.vector.bn_stats(stats[:, i, :], y[:, i, :])
                chain(last)
                nc.vector.nop(nofuse=True)
                for i in range(TILES):
                    last = nc.vector.bn_aggr(mv[:, i, :], stats[:, i, :])
                last.then_inc(s["y_mv"], 1)
                chain.end()
                v.wait_ge(s["y_rs"], b + 1)
                need(v, s["ynT_ps"], b)
                for i in range(TILES):
                    last = nc.vector.tensor_scalar(yn[:, i * P:(i + 1) * P].rearrange("p (r d) -> p r d", d=DS),
                                                   y[:, i, :].unsqueeze(1).to_broadcast([P, P // DS, DS]),
                                                   mv[:, i, 0:1], rs_y[:, i:i + 1], ALU.subtract, ALU.mult)
                last.then_inc(s["yn"], 1)
                v.wait_ge(s["yn"], b + 1)

            def dve_4b(v, b, par):
                for c in range(DC):
                    v.wait_ge(s["yg"], DC * b + c + 1)
                    need(v, s["z_ready"], prior(b))
                    nc.vector.tensor_tensor(yz[par][c][:], yg[c][:], z_all[:, c, bass.ds(b, 1), :].rearrange("p o t -> p (o t)"),
                                            ALU.mult).then_inc(s["yz"], 1)

            def dve_4c(v, b, par):
                v.wait_ge(s["z_ready"], b + 1)
                nc.vector.tensor_tensor(flat(x_of(b)), bank[2 + par][:], flat(x_of(b)), ALU.add).then_inc(x_upd, 1)

            def dve_4(v, b, par, first_, last_):
                if not last_:
                    dve_4a(v, b + 1)
                dve_4b(v, b, par)
                if not first_:
                    dve_4c(v, b - 1, 1 - par)

            def pe_4(b, par, first_, last_):
                nc.tensor.wait_ge(s["yn"], b + 1)
                need(nc.tensor, s["yg"], DC * prior(b))
                for i in range(TILES):
                    last = nc.tensor.transpose(bank[par][:, i * P:(i + 1) * P], yn[:, i * P:(i + 1) * P], ident[:])
                last.then_inc(s["ynT_ps"], 1)
                if not first_:
                    z_pe4(b - 1, 1 - par)

            def z_pe4(b, par):
                nc.tensor.wait_ge(s["yz"], DC * (b + 1))
                need(nc.tensor, x_upd, f0 + b - 1)
                for i in range(TILES):
                    for c in range(DC):
                        last = nc.tensor.matmul(bank[2 + par][:, i * P:(i + 1) * P], yz[par][c][:, i * P:(i + 1) * P], w_out[:, c, :],
                                                start=(c == 0), stop=(c == DC - 1))
                last.then_inc(s["z_ready"], 1)

            def act_4(b, par, first_, last_):
                nc.scalar.wait_ge(s["ynT_ps"], b + 1)
                for c in range(DC):
                    need(nc.scalar, s["yz"], DC * (b - 1) + c + 1)
                    nc.scalar.activation(yg[c][:], bank[par][:], ACT.Identity, bias=vecs[:, V_B + c:V_B + c + 1],
                                         scale=vecs[:, V_G + c:V_G + c + 1]).then_inc(s["yg"], 1)

            def tensor(t):
                after_phases(t, n)
                t.wait_ge(w_loaded, 16 * N_WEIGHTS)
                sequences(t, pe_1)
                nc.tensor.wait_ge(s["dtlo_sb"], B)
                nc.tensor.wait_ge(s["z_act"], DC * B)
                nc.tensor.wait_ge(s["bs"], B)
                sequences(t, pe_2)
                mean_pe(B - 1, 1)
                for i in range(TILES):
                    last = nc.tensor.transpose(bank[6][0:B, i * P:(i + 1) * P], bs_all[:, i, :], ident[:])
                last.then_inc(s["bs_ps"], 1)
                nc.tensor.wait_ge(s["scanned"], 1)
                for i in range(TILES):
                    last = nc.tensor.transpose(bank[6][:, i * B:(i + 1) * B], state8[:, i * P:(i + 1) * P], ident[0:B, 0:B])
                last.then_inc(s["s_ps"], 1)
                sequences(t, pe_4)
                z_pe4(B - 1, 1)
                norm_pe(f0 + B)

            def scalar(c):
                after_phases(c, n)
                nc.scalar.wait_ge(s["edges"], 2 * DC)
                sequences(c, act_1)
                nc.scalar.wait_ge(s["bc_ps"], B)
                nc.scalar.wait_ge(s["bs"], B)
                sequences(c, act_2)
                decay_act(B - 1, 1)
                nc.scalar.wait_ge(s["dm_ps"], B)
                sequences(c, act_4)
                norm_act(f0 + B, 0)

            def vector(v):
                after_phases(v, n)
                v.wait_ge(w_loaded, 16 * N_WEIGHTS)
                for c in range(DC):
                    for e in (0, T + 1):
                        nc.vector.memset(xs_pad[c][:, e:e + 1], 0.0).then_inc(s["edges"], 1)
                v.wait_ge(s["edges"], 2 * DC)
                sequences(v, lambda b, par, f, l: dve_1(v, b, par, f, l))
                v.wait_ge(s["xs_act"], DC * B)
                v.wait_ge(s["bs"], B)
                v.wait_ge(s["bc_ps"], B)
                sequences(v, lambda b, par, f, l: dve_2(v, b, par, f, l))
                v.wait_ge(s["bs_ps"], 1)
                v.wait_ge(s["decay_rows"], 16)
                nc.vector.tensor_tensor_scan(state8[:], decay8[:], bank[6][0:B, :], 0.0, ALU.mult, ALU.add).then_inc(s["scanned"], 1)
                v.wait_ge(s["s_ps"], 1)
                nc.vector.tensor_copy(s_tok[:].rearrange("p b i -> p i b"),
                                      bank[6][:, 0:TILES * B].rearrange("p (i b) -> p i b", i=TILES)).then_inc(s["s_tok"], 1)
                v.wait_ge(s["s_tok"], 1)
                v.wait_ge(s["dm_ps"], B)
                v.wait_ge(s["decay"], B)
                dve_4a(v, 0)
                sequences(v, lambda b, par, f, l: dve_4(v, b, par, f, l))
                dve_4c(v, B - 1, 1)
                norm_a(v, f0 + B, 0)
                norm_c(v, f0 + B, 0)

            def y_pool(b, par, first_, last_):
                nc.gpsimd.wait_ge(s["y_mv"], b + 1)
                rsqrt(s["y_var"], b, s["y_rs"])

            def gpsimd(g):
                after_phases(g, n)
                sequences(g, lambda b, par, f, l: None if l else norm_b(f0 + b + 1))
                sequences(g, y_pool)
                norm_b(f0 + B)

            def sync(q):
                q.wait_ge(s["decay"], B)
                q.dma_start(decay8[:], decays[0:1, :, :]).then_inc(s["decay_rows"], 16)

            return {"tensor": tensor, "scalar": scalar, "vector": vector, "gpsimd": gpsimd, "sync": sync}

        make = {"attn": attn_phase, "ssm": ssm_phase, "moe0": lambda n: moe_phase(n, 0), "moe1": lambda n: moe_phase(n, 1)}
        plan = [make[p](n) for n, p in enumerate(phases)]
        new_phase()

        block = ctx.enter_context(nc.Block())
        ov = out.rearrange("b (i p) e -> p (b i) e", p=P)
        r1 = lambda v: v.rearrange("(o n) -> o n", o=1)

        @block.sync
        def _(q):
            q.dma_start(x_res[:, 0:TILES, :], xv[:, 0:TILES, :]).then_inc(x_first, 16)
            q.dma_start(wr0[:], a["L0_ffn_w_router"]).then_inc(x_first, 16)
            rows = [
                (V_B1, a["L0_ffn_b1"].rearrange("e (c p) -> (e c) p", p=P)), (V_B2, a["L0_ffn_b2"]),
                (V_BK, r1(a["L0_attn_bk"])), (V_BV, r1(a["L0_attn_bv"])),
                (V_BDT, a["L1_attn_b_dt"].rearrange("(c p) -> c p", p=P)),
                (V_G, a["L1_attn_ln_g"].rearrange("(c p) -> c p", p=P)),
                (V_B, a["L1_attn_ln_b"].rearrange("(c p) -> c p", p=P))]
            for at, v in rows:
                q.dma_start(vec_rows[at:at + v.shape[0], :], v).then_inc(rows_loaded, 16)
            for at, v in ((V_BQ, a["L0_attn_bq"]), (V_BL, a["L0_attn_bl"])):
                q.dma_start(vec_rows[at:at + 1, :].rearrange("o (d h) -> o d h", d=HD),
                            v.rearrange("(o h d) -> o d h", o=1, d=HD),
                            allow_slow_non_contiguous=True).then_inc(rows_loaded, 16)
            assert len(rows) + 2 == N_ROWS
            if phases[0] != "moe0":
                load_x_rest(q)
                load_weights(q)
            for p in plan:
                p["sync"](q)
            for b in range(B):
                q.wait_ge(x_upd, B * (len(phases) - 1) + b + 1)
                q.dma_start(ov[:, b * TILES:(b + 1) * TILES, :], x_of(b)).then_inc(stored, 16)
            q.wait_ge(w_loaded, 16 * N_WEIGHTS)
            q.wait_ge(stored, 16 * B)

        @block.gpsimd
        def _(g):
            g.memset(ident[:], 0.0).then_inc(pool_chain, 1)
            g.memset(identb[:], 0.0).then_inc(pool_chain, 1)
            g.wait_ge(pool_chain, 2)
            for m in (ident, identb):
                g.affine_select(out=m[:], in_=m[:], compare_op=ALU.not_equal, fill=1.0, base=0, pattern=[[-1, P]],
                                channel_multiplier=1).then_inc(ident_ready, 1)
            for e in range(NE1):
                g.memset(first[:, :, e:e + 1], float(NE1 - e))
            g.memset(w_x[:, :, DTR + 2 * DS:], 1.0 / DI).then_inc(tables_ready, 1)
            g.memset(neg_half[:], -0.5).then_inc(pool_chain, 1)
            g.wait_ge(pool_chain, 3)
            norm_b(0)
            for p in plan:
                p["gpsimd"](g)

        @block.scalar
        def _(c):
            c.wait_ge(vecs_ps, 1)
            nc.scalar.copy(vecs[:], bank[0][:, 0:NVEC]).then_inc(vecs_ready, 1)
            norm_act(0, 0)
            for p in plan:
                p["scalar"](c)

        @block.vector
        def _(v):
            v.wait_ge(x_first, 32)
            norm_a(v, 0, 0)
            norm_c(v, 0, 0)
            v.wait_ge(tables_ready, 1)
            v.wait_ge(vecs_ready, 1)
            for p in plan:
                p["vector"](v)

        @block.tensor
        def _(t):
            t.wait_ge(ident_ready, 2)
            t.wait_ge(rows_loaded, 16 * N_ROWS)
            nc.tensor.transpose(bank[0][:, 0:NVEC], vec_rows[:], ident[0:NVEC, 0:NVEC]).then_inc(vecs_ps, 1)
            norm_pe(0)
            t.wait_ge(vecs_ready, 1)
            for p in plan:
                p["tensor"](t)


_INS = ['L0_attn_x', 'L0_attn_Wq', 'L0_attn_bq', 'L0_attn_Wk', 'L0_attn_bk', 'L0_attn_Wv', 'L0_attn_bv', 'L0_attn_Wl',
        'L0_attn_bl', 'L0_attn_Wo', 'L0_attn_bo', 'L0_ffn_w_router', 'L0_ffn_w1', 'L0_ffn_b1', 'L0_ffn_w2', 'L0_ffn_b2',
        'L1_attn_W_in', 'L1_attn_W_conv', 'L1_attn_W_xproj', 'L1_attn_W_dt', 'L1_attn_b_dt', 'L1_attn_W_out',
        'L1_attn_ln_g', 'L1_attn_ln_b', 'L1_ffn_router_w', 'L1_ffn_gate_w', 'L1_ffn_up_w', 'L1_ffn_down_w',
        'L1_ffn_shared_gate_w', 'L1_ffn_shared_up_w', 'L1_ffn_shared_down_w']


def kernel(**inputs):
    import numpy as _np
    import concourse.bacc as _bacc
    from concourse import mybir as _mybir
    from concourse.bass_utils import run_bass_kernel_spmd as _run

    nc = _bacc.Bacc("TRN2", target_bir_lowering=False, num_devices=1)
    arrays, aps = {}, {}
    for name in _INS:
        v = _np.ascontiguousarray(inputs[name])
        arrays[f"in_{name}"] = v
        aps[name] = nc.dram_tensor(f"in_{name}", v.shape, _mybir.dt.from_np(v.dtype), kind="ExternalInput").ap()
    out = nc.dram_tensor("out_x", (B, T, E), F32, kind="ExternalOutput").ap()
    build(nc, aps, out)
    r = _run(nc, [arrays], core_ids=[0])
    return r.results[0]["out_x"]
```

```python
from contextlib import ExitStack

import concourse.bass as bass
from concourse import mybir

ALU = mybir.AluOpType
ACT = mybir.ActivationFunctionType
F32 = mybir.dt.float32
F32R = mybir.dt.float32r
BF16 = mybir.dt.bfloat16
AX_X = mybir.AxisListType.X

P = 128
B, T, E = 8, 512, 128
TILES = T // P
NE0, HID = 8, 512
HC = HID // P
NE1, FE = 16, 64
PAIRS = NE1 // 2
H, HD = 16, 8
HG = 4
DI, DS, DTR = 256, 16, 64
DC = DI // P
EPS = 1e-5
BIG = 1e30

V_B1, V_B2 = 0, 32
V_BQ, V_BK, V_BV, V_BL = 40, 41, 42, 43
V_BDT, V_G, V_B = 44, 46, 48
NVEC = 50
N_ROWS, N_WEIGHTS = 9, 19

PHASES = ("moe0", "attn", "moe0", "moe1", "ssm", "moe1")


class Chain:

    def __init__(self, eng, sem, per):
        self.eng, self.sem, self.per, self.k, self.base = eng, sem, per, 0, 0

    def begin(self, n):
        self.base, self.k = n * self.per, 0

    def __call__(self, ins):
        self.k += 1
        ins.then_inc(self.sem, 1)
        self.eng.wait_ge(self.sem, self.base + self.k)

    def end(self):
        assert self.k == self.per, (self.k, self.per)


def build(nc, a, out, phases=PHASES):
    nc.disable_value_cache = True
    with ExitStack() as ctx:
        def sb(name, shape, dt=F32):
            return ctx.enter_context(nc.sbuf_tensor(name, shape, dt))

        def sem(name):
            return ctx.enter_context(nc.semaphore(name))

        bank = [ctx.enter_context(nc.psum_tensor(f"bank{i}", [P, 512], F32)) for i in range(8)]

        x_res = sb("x_res", [P, B * TILES, E])
        xnT = [sb(f"xnT{i}", [P, T]) for i in range(2)]
        xn = sb("xn", [P, TILES, E])
        staged = [sb(f"staged{i}", [P, 2, HID]) for i in range(2)]
        wr0 = sb("wr0", [P, NE0])
        gate_up = sb("gate_up", [P, 2, PAIRS + 1, P])
        down_w = sb("down_w", [P, PAIRS, E])
        sh_d = sb("sh_d", [P, E])
        wr1 = sb("wr1", [P, NE1])
        ident = sb("ident", [P, P])
        identb = sb("identb", [P, P], BF16)
        first = sb("first", [P, TILES, NE1])
        vec_rows = sb("vec_rows", [NVEC, P])
        vecs = sb("vecs", [P, NVEC])
        wq, wk, wv, wl, wo = [sb(f"w_{k}", [P, P]) for k in ("q", "k", "v", "l", "o")]
        wq_p, wl_p = sb("wq_p", [P, P]), sb("wl_p", [P, P])
        bl_bc = sb("bl_bc", [P, P])
        bo_bc = sb("bo_bc", [P, TILES, P])
        w_in = sb("w_in", [P, 2 * DI])
        w_conv = sb("w_conv", [P, DC, 3])
        w_x = sb("w_x", [P, DC, DTR + 2 * DS + 1])
        w_dt = sb("w_dt", [DTR, DI])
        w_out = sb("w_out", [P, DC, E])
        stats = sb("stats", [P, TILES, 6])
        mv = sb("mv", [P, TILES, 2])
        var = sb("var", [P, TILES])
        rs_y = sb("rs_y", [P, TILES])
        neg_half = sb("neg_half", [P, TILES])
        lg = sb("lg", [P, TILES, NE1])
        rt_a = sb("rt_a", [P, TILES, NE1])
        rt_b = sb("rt_b", [P, TILES, NE1])
        rt_c = sb("rt_c", [P, TILES, NE1])
        rt_th = sb("rt_th", [P, TILES, NE1])
        rt_m = sb("rt_m", [P, TILES])
        rt_n = sb("rt_n", [P, TILES])
        coef = sb("coef", [P, TILES, NE1])

        mem = {"phase": ExitStack(), "part": ExitStack(), "now": "phase", "count": 0}

        def new_phase():
            mem["part"].close()
            mem["phase"].close()
            mem["now"] = "phase"

        def new_part():
            mem["part"].close()
            mem["now"] = "part"

        def view(rows, cols, dt=F32, until=None):
            mem["count"] += 1
            return (until or mem[mem["now"]]).enter_context(nc.sbuf_tensor(f"shared{mem['count']}", [rows, cols], dt))[:, :]

        x_first, x_rest, w_loaded = sem("x_first"), sem("x_rest"), sem("w_loaded")
        rows_loaded, ident_ready, tables_ready = sem("rows_loaded"), sem("ident_ready"), sem("tables_ready")
        pool_chain, vecs_ps, vecs_ready = sem("pool_chain"), sem("vecs_ps"), sem("vecs_ready")
        x_upd = sem("x_upd")
        xn_ready, xnT_ps, xnT_ready = sem("xn_ready"), sem("xnT_ps"), sem("xnT_ready")
        ln_chain, mv_ready, var_ready, rs_ready = sem("ln_chain"), sem("mv_ready"), sem("var_ready"), sem("rs_ready")
        stored = sem("stored")
        w_staged = [sem(f"w_staged{i}") for i in range(2)]
        xv = a["L0_attn_x"].rearrange("b (i p) e -> p (b i) e", p=P)
        LN_STEPS = 1

        def x_of(b):
            return x_res[:, bass.ds(b * TILES, TILES), :]

        def need(eng, semaphore, value):
            if not isinstance(value, int) or value > 0:
                eng.wait_ge(semaphore, value)

        def prior(b):
            return b - 1 if isinstance(b, int) else (b * (B - 3) + 1) // (B - 2)

        def flat(v):
            return v.rearrange("p a b -> p (a b)")

        def rsqrt(var_sem, k, done):
            nc.gpsimd.nop(nofuse=True)
            nc.gpsimd.tensor_scalar(var[:], mv[:, :, 1], EPS, None, ALU.add).then_inc(var_sem, 1)
            nc.gpsimd.wait_ge(var_sem, k + 1)
            nc.gpsimd.tensor_tensor(rs_y[:], var[:], neg_half[:], ALU.pow).then_inc(done, 1)

        def norm_a(v, f, b):
            chain = Chain(v, ln_chain, LN_STEPS)
            chain.begin(f)
            x = x_of(b)
            need(v, xn_ready, f)
            if isinstance(f, int):
                need(v, x_upd, f - B + 1)
                if f == 1:
                    v.wait_ge(x_rest, 16)
            for i in range(TILES):
                last = nc.vector.bn_stats(stats[:, i, :], x[:, i, :])
            chain(last)
            nc.vector.nop(nofuse=True)
            chain.end()
            for i in range(TILES):
                last = nc.vector.bn_aggr(mv[:, i, :], stats[:, i, :])
            last.then_inc(mv_ready, 1)

        def norm_b(f):
            nc.gpsimd.wait_ge(mv_ready, f + 1)
            rsqrt(var_ready, f, rs_ready)

        def norm_c(v, f, b):
            x = x_of(b)
            v.wait_ge(rs_ready, f + 1)
            need(v, xnT_ps, f)
            for i in range(TILES):
                last = nc.vector.tensor_scalar(xn[:, i, :], x[:, i, :], mv[:, i, 0:1], rs_y[:, i:i + 1], ALU.subtract, ALU.mult)
            last.then_inc(xn_ready, 1)

        def norm_pe(f):
            need(nc.tensor, xn_ready, f + 1)
            need(nc.tensor, xnT_ready, f)
            for i in range(TILES):
                last = nc.tensor.transpose(bank[7][:, i * P:(i + 1) * P], xn[:, i, :], ident[:])
            last.then_inc(xnT_ps, 1)

        def norm_act(f, par):
            nc.scalar.wait_ge(xnT_ps, f + 1)
            nc.scalar.copy(xnT[par][:], bank[7][:]).then_inc(xnT_ready, 1)

        def after_phases(eng, n):
            if n:
                eng.wait_ge(x_upd, B * n)

        def sequences(eng, body, c0=0):
            body(c0, 0, True, False)
            with eng.Fori(0, (B - 2) // 2) as i:
                body(2 * i + (c0 + 1), 1, False, False)
                body(2 * i + (c0 + 2), 0, False, False)
            body(c0 + B - 1, 1, False, True)

        def load_x_rest(q):
            q.dma_start(x_res[:, TILES:, :], xv[:, TILES:, :]).then_inc(x_rest, 16)

        def load_weights(q):
            r1 = lambda v: v.rearrange("(o n) -> o n", o=1)
            weights = [
                (wq[:], a["L0_attn_Wq"]), (wk[:], a["L0_attn_Wk"]), (wv[:], a["L0_attn_Wv"]), (wl[:], a["L0_attn_Wl"]),
                (wo[:], a["L0_attn_Wo"]),
                (bl_bc[0:1, :], r1(a["L0_attn_bl"])), (bo_bc[0:1, 0, :], r1(a["L0_attn_bo"])),
                (wr1[:], a["L1_ffn_router_w"]),
                (flat(gate_up[:, 0, 1:, :]).rearrange("p (e f) -> p e f", f=FE), a["L1_ffn_gate_w"].rearrange("e p f -> p e f")),
                (flat(gate_up[:, 1, 1:, :]).rearrange("p (e f) -> p e f", f=FE), a["L1_ffn_up_w"].rearrange("e p f -> p e f")),
                (down_w[:], a["L1_ffn_down_w"].rearrange("(j t) f o -> (t f) j o", t=2)),
                (gate_up[:, 0, 0, :], a["L1_ffn_shared_gate_w"]), (gate_up[:, 1, 0, :], a["L1_ffn_shared_up_w"]), (sh_d[:], a["L1_ffn_shared_down_w"]),
                (w_in[:], a["L1_attn_W_in"]),
                (w_conv[:], a["L1_attn_W_conv"].rearrange("(c p) o k -> p c (o k)", p=P)),
                (w_x[:, :, 0:DTR + 2 * DS], a["L1_attn_W_xproj"].rearrange("(c p) n -> p c n", p=P)),
                (w_dt[:], a["L1_attn_W_dt"]),
                (w_out[:], a["L1_attn_W_out"].rearrange("(c p) o -> p c o", p=P))]
            for dst, src in weights:
                q.dma_start(dst, src).then_inc(w_loaded, 16)
            assert len(weights) == N_WEIGHTS

        moe_sems = {}

        def moe_phase(n, kind):
            ne = NE0 if kind == 0 else NE1
            c0 = B * phases[:n].count(phases[n])
            f0 = B * n - c0
            names = ("xh_ready", "xl_ready", "w_hi", "w_lo", "lg_ready", "z_ready", "th_ready", "coef_ready", "ct_ps", "ct_sb",
                     "row_loaded", "bc_ready", "up_ready", "act_done", "down_done", "back_ready", "rt_chain")
            names += (("hh_ready", "h3_ready", "hl_ready", "y_used", "mixed") if kind == 0 else
                      ("bc_half", "gated", "hid_ready", "acc_ready"))
            if kind not in moe_sems:
                moe_sems[kind] = {k: sem(f"moe{kind}_{k}") for k in names}
            s = moe_sems[kind]
            occ = phases[:n].count(phases[n])
            IT = PAIRS + 1
            new_phase()
            coefB = view(P, 8 * T).rearrange("p (e t) -> p e t", e=8)
            row = view(1, ne * T).rearrange("p (e t) -> p e t", e=ne)
            coefT = view(NE1, T)
            tmp = [view(P, T) for _ in range(2)]
            acc = [view(P, T) for _ in range(2)]
            xh, xl = ([view(P, T, F32R) for _ in range(2)] for _ in range(2))
            if kind == 0:
                RING = 2 * HC
                with ExitStack() as gone:
                    hid = [view(P, T, F32, gone) for _ in range(RING)]
                hl = [view(P, T, F32R) for _ in range(RING)]
                hh = [view(P, T, F32R) for _ in range(RING)]
                wh, wl_ = (view(P, NE0 * 2 * HID, F32R).rearrange("p (e k h) -> p e k h", e=NE0, k=2) for _ in range(2))
            else:
                hid = [view(P, T) for _ in range(5)]
                silu = [view(P, T) for _ in range(2)]
                gh, gl = (view(P, 2 * IT * P, F32R).rearrange("p (k j m) -> p k j m", k=2, j=IT) for _ in range(2))
            wr = wr0 if kind == 0 else wr1
            RT_STEPS = 17
            ROW_DMAS = 1 if kind == 0 else 2
            wide = lambda m: m[:].unsqueeze(2).to_broadcast([P, TILES, ne])

            def router_pe(b, par):
                nc.tensor.wait_ge(xnT_ready, f0 + b + 1)
                for i in range(TILES):
                    last = nc.tensor.matmul(bank[7][:, i * ne:(i + 1) * ne], xnT[par][:, i * P:(i + 1) * P], wr[:, 0:ne],
                                            start=True, stop=True)
                last.then_inc(s["lg_ready"], 1)

            def coef_pe(b):
                nc.tensor.wait_ge(s["coef_ready"], b + 1)
                need(nc.tensor, s["ct_sb"], b)
                if not isinstance(b, int) or b > 1:
                    nc.tensor.wait_ge(x_upd, f0 + b - 1)
                for i in range(TILES):
                    last = nc.tensor.transpose(bank[6][0:ne, i * P:(i + 1) * P], coef[:, i, 0:ne], ident[:])
                last.then_inc(s["ct_ps"], 1)

            def router_act(b):
                nc.scalar.wait_ge(s["z_ready"], b + 1)
                nc.scalar.activation(rt_th[:, :, 0:ne], lg[:, :, 0:ne], ACT.Tanh, scale=0.5).then_inc(s["th_ready"], 1)

            def coef_act(b):
                nc.scalar.wait_ge(s["ct_ps"], b + 1)
                need(nc.scalar, s["row_loaded"], 16 * ROW_DMAS * b)
                nc.scalar.copy(coefT[0:ne, :], bank[6][0:ne, :]).then_inc(s["ct_sb"], 1)

            z, q, r, sel, th = (m[:, :, 0:ne] for m in (lg, rt_a, rt_b, rt_c, rt_th))

            def router_a(v, b):
                chain = Chain(v, s["rt_chain"], RT_STEPS)
                chain.begin(b)
                ps = bank[7][:, 0:TILES * ne].rearrange("p (i e) -> p i e", i=TILES)
                v.wait_ge(s["lg_ready"], b + 1)
                need(v, s["coef_ready"], b)
                chain(nc.vector.tensor_reduce(rt_m[:], ps, AX_X, ALU.max))
                nc.vector.tensor_tensor(z, ps, wide(rt_m), ALU.subtract).then_inc(s["z_ready"], 1)
                v.wait_ge(s["z_ready"], b + 1)
                chain(nc.vector.scalar_tensor_tensor(out=q, in0=z, scalar=0.0, in1=first[:, :, 0:ne], op0=ALU.is_equal, op1=ALU.mult))
                chain(nc.vector.tensor_reduce(rt_n[:], q, AX_X, ALU.max))
                chain(nc.vector.tensor_tensor(sel, q, wide(rt_n), ALU.is_equal))
                return chain

            def router_b(chain):
                chain(nc.vector.scalar_tensor_tensor(out=r, in0=sel, scalar=-BIG, in1=z, op0=ALU.mult, op1=ALU.add))
                chain(nc.vector.tensor_reduce(rt_m[:], r, AX_X, ALU.max))
                chain(nc.vector.tensor_tensor(q, r, wide(rt_m), ALU.is_equal))
                chain(nc.vector.tensor_tensor(q, q, first[:, :, 0:ne], ALU.mult))
                chain(nc.vector.tensor_reduce(rt_n[:], q, AX_X, ALU.max))
                chain(nc.vector.tensor_tensor(q, q, wide(rt_n), ALU.is_equal))
                chain(nc.vector.tensor_tensor(sel, q, sel, ALU.add))

            def router_c(v, b, chain):
                v.wait_ge(s["th_ready"], b + 1)
                chain(nc.vector.tensor_scalar(r, th, -1.0, 1.0, ALU.mult, ALU.add))
                chain(nc.vector.reciprocal(r, r))
                chain(nc.vector.scalar_tensor_tensor(out=r, in0=th, scalar=1.0, in1=r, op0=ALU.add, op1=ALU.mult))
                chain(nc.vector.tensor_reduce(rt_n[:], r, AX_X, ALU.add))
                chain(nc.vector.reciprocal(rt_m[:], rt_n[:]))
                chain(nc.vector.tensor_tensor(r, r, sel, ALU.mult))
                chain.end()
                need(v, s["ct_ps"], b)
                nc.vector.scalar_tensor_tensor(out=coef[:, :, 0:ne], in0=r, scalar=0.5, in1=wide(rt_m), op0=ALU.mult,
                                               op1=ALU.mult).then_inc(s["coef_ready"], 1)

            opening = {}

            def row_sp(b, par, first_, last_):
                nc.sync.wait_ge(s["ct_sb"], b + 1)
                need(nc.sync, s["bc_ready"], 8 * b)
                for k in range(ROW_DMAS):
                    nc.sync.dma_start(row[0:1, 8 * k:8 * k + 8, :], coefT[k:ne:ROW_DMAS, :]).then_inc(s["row_loaded"], 16)

            def pool1(b, par, first_, last_):
                if more or not last_:
                    norm_b(f0 + b + 1)
                nc.gpsimd.wait_ge(s["row_loaded"], 16 * ROW_DMAS * (b + 1))
                for e in range(PAIRS):
                    need(nc.gpsimd, s["hid_ready"], PAIRS * (b - 1) + e + 1)
                    nc.gpsimd.nop(nofuse=True)
                    nc.gpsimd.partition_broadcast(coefB[:, e, :], row[0:1, 8 + e, :]).then_inc(s["bc_half"], 1)
                    nc.gpsimd.wait_ge(s["bc_half"], PAIRS * b + e + 1)
                    nc.gpsimd.nop(nofuse=True)
                    nc.gpsimd.partition_broadcast(coefB[0:FE, e, :], row[0:1, e, :], channels=FE).then_inc(s["bc_ready"], 1)

            def back_pe(b, par):
                nc.tensor.wait_ge(s["ct_sb"], b + 1)
                if kind == 0:
                    nc.tensor.wait_ge(s["mixed"], (NE0 - 1) * (b + 1))
                else:
                    nc.tensor.wait_ge(s["acc_ready"], b + 1)
                for i in range(TILES):
                    last = nc.tensor.transpose(bank[6][:, i * P:(i + 1) * P], acc[par][:, i * P:(i + 1) * P], ident[:])
                last.then_inc(s["back_ready"], 1)

            def back_dve(v, b):
                v.wait_ge(s["back_ready"], b + 1)
                nc.vector.tensor_tensor(flat(x_of(b % B)), bank[6][:], flat(x_of(b % B)), ALU.add).then_inc(x_upd, 1)

            more = n + 1 < len(phases)

            def hi_lo(out_bank, w_hi, w_lo, x_hi, x_lo, start, stop):
                nc.tensor.matmul(out_bank, w_hi, x_hi, start=start, stop=False)
                nc.tensor.matmul(out_bank, w_hi, x_lo, start=False, stop=False)
                return nc.tensor.matmul(out_bank, w_lo, x_hi, start=False, stop=stop)

            def xh_act(b, par):
                nc.scalar.wait_ge(xnT_ready, f0 + b + 1)
                nc.scalar.copy(xh[par][:], xnT[par][:]).then_inc(s["xh_ready"], 1)

            def xl_dve(v, b, par):
                v.wait_ge(s["xh_ready"], b + 1)
                nc.vector.tensor_tensor(xl[par][:], xnT[par][:], xh[par][:], ALU.subtract).then_inc(s["xl_ready"], 1)

            CH = NE0 * HC

            LAG = RING - 2 if kind == 0 else 0

            def load0(e):
                need(nc.sync, s["w_lo"], NE0 * occ + e - 1)
                nc.sync.dma_start(staged[e % 2][:, 0, :], a["L0_ffn_w1"][e]).then_inc(w_staged[e % 2], 16)
                nc.sync.dma_start(staged[e % 2][:, 1, :].rearrange("p (c o) -> p c o", o=E),
                                  a["L0_ffn_w2"][e].rearrange("(c p) o -> p c o", p=P)).then_inc(w_staged[e % 2], 16)

            def w_hi_act(e):
                nc.scalar.wait_ge(w_staged[e % 2], 32 * (occ * NE0 // 2 + e // 2 + 1))
                nc.scalar.copy(wh[:, e, :, :], staged[e % 2][:]).then_inc(s["w_hi"], 1)

            def w_lo_dve(v, e):
                v.wait_ge(s["w_hi"], NE0 * occ + e + 1)
                nc.vector.tensor_tensor(wl_[:, e, :, :], staged[e % 2][:], wh[:, e, :, :], ALU.subtract).then_inc(s["w_lo"], 1)

            def up0(b, par, k, first_):
                e, c = k // HC, k % HC
                if k == 0:
                    nc.tensor.wait_ge(s["xl_ready"], b + 1)
                if first_ and c == 0:
                    nc.tensor.wait_ge(s["w_lo"], NE0 * occ + e + 1)
                need(nc.tensor, s["act_done"], CH * b + k - 3)
                cols = slice(c * P, (c + 1) * P)
                hi_lo(bank[k % 4][:], wh[:, e, 0, cols], wl_[:, e, 0, cols], xh[par][:], xl[par][:], True, True).then_inc(s["up_ready"], 1)

            def down0(b, k):
                e, c = k // HC, k % HC
                nc.tensor.wait_ge(s["hl_ready"], CH * b + k + 1)
                if c == 0:
                    need(nc.tensor, s["y_used"], NE0 * b + e - 1)
                cols = slice(c * P, (c + 1) * P)
                hi_lo(bank[4 + e % 2][:], wh[:, e, 1, cols], wl_[:, e, 1, cols], hh[k % RING][:], hl[k % RING][:], c == 0,
                      c == HC - 1).then_inc(s["down_done"], 1)

            def gelu0(b, k):
                e, c = k // HC, k % HC
                nc.scalar.wait_ge(s["up_ready"], CH * b + k + 1)
                need(nc.scalar, s["down_done"], CH * b + k + 1 - RING)
                nc.scalar.activation(hid[k % RING][:], bank[k % 4][:], ACT.Gelu_apprx_tanh,
                                     bias=vecs[:, V_B1 + k:V_B1 + k + 1]).then_inc(s["act_done"], 1)

            def hh_act(b, k):
                e, c = k // HC, k % HC
                nc.scalar.wait_ge(s["act_done"], CH * b + k + 1)
                nc.scalar.copy(hh[k % RING][:], hid[k % RING][:]).then_inc(s["hh_ready"], 1)

            def hl_dve(v, b, k):
                e, c = k // HC, k % HC
                if c < HC - 1:
                    v.wait_ge(s["hh_ready"], (HC - 1) * (NE0 * b + e) + c + 1)
                else:
                    v.wait_ge(s["act_done"], CH * b + k + 1)
                    nc.vector.tensor_copy(hh[k % RING][:], hid[k % RING][:]).then_inc(s["h3_ready"], 1)
                    v.wait_ge(s["h3_ready"], NE0 * b + e + 1)
                nc.vector.tensor_tensor(hl[k % RING][:], hid[k % RING][:], hh[k % RING][:], ALU.subtract).then_inc(s["hl_ready"], 1)

            def combine0(v, b, par, e):
                v.wait_ge(s["down_done"], CH * b + HC * (e + 1))
                v.wait_ge(s["bc_ready"], NE0 * b + e + 1)
                into = acc[par] if e == 0 else tmp[e % 2]
                if e:
                    need(v, s["mixed"], (NE0 - 1) * b + (e - 2 if e > 2 else 1 - e))
                nc.vector.scalar_tensor_tensor(out=into[:], in0=bank[4 + e % 2][:], scalar=vecs[:, V_B2 + e:V_B2 + e + 1],
                                               in1=coefB[:, e, :], op0=ALU.add, op1=ALU.mult).then_inc(s["y_used"], 1)

            def mix_pool(b, par, e):
                nc.gpsimd.wait_ge(s["y_used"], NE0 * b + e + 1)
                if e > 1:
                    nc.gpsimd.wait_ge(s["mixed"], (NE0 - 1) * b + e - 1)
                nc.gpsimd.tensor_tensor(acc[par][:], tmp[e % 2][:], acc[par][:], ALU.add).then_inc(s["mixed"], 1)

            def pe0(b, par, first_, last_):
                for k in range(CH):
                    up0(b, par, k, first_)
                    if k >= LAG:
                        down0(b, k - LAG)
                    elif not first_:
                        down0(b - 1, CH - LAG + k)
                    if k == 10 and not first_:
                        back_pe(b - 1, 1 - par)
                    if k == 16 and (more or not last_):
                        norm_pe(f0 + b + 1)
                    if k == 20 and not last_:
                        router_pe(b + 1, 1 - par)
                    if k == 7 and first_:
                        coef_pe(b)
                    if k == 30 and not last_:
                        coef_pe(b + 1)

            def act0(b, par, first_, last_):
                for k in range(CH):
                    if first_ and k % HC == 2 and k // HC + 2 < NE0:
                        w_hi_act(k // HC + 2)
                    gelu0(b, k)
                    if k % HC:
                        hh_act(b, k - 1)
                    if k == 17 and (more or not last_):
                        norm_act(f0 + b + 1, 1 - par)
                    if k == 18 and not last_:
                        xh_act(b + 1, 1 - par)
                    if k == 23 and not last_:
                        router_act(b + 1)
                    if k == 7 and first_:
                        coef_act(b)
                    if k == 31 and not last_:
                        coef_act(b + 1)

            def dve0(v, b, par, first_, last_):
                for k in range(CH):
                    e, c = k // HC, k % HC
                    hl_dve(v, b, k)
                    if first_ and k == 0:
                        router_b(opening["router"])
                    if first_ and k == 1:
                        router_c(v, b, opening["router"])
                    if first_ and c == 2 and e + 2 < NE0:
                        w_lo_dve(v, e + 2)
                    if c == 0 and (e > 1 or not first_):
                        combine0(v, *((b, par, e - 2) if e > 1 else (b - 1, 1 - par, NE0 + e - 2)))
                    if k == 12 and not first_:
                        back_dve(v, b - 1)
                    if more or not last_:
                        if k == 6:
                            norm_a(v, f0 + b + 1, (b + 1) % B)
                        if k == 10:
                            norm_c(v, f0 + b + 1, (b + 1) % B)
                    if not last_:
                        if k == 18:
                            xl_dve(v, b + 1, 1 - par)
                        if k == 21:
                            router = router_a(v, b + 1)
                        if k == 23:
                            router_b(router)
                        if k == 26:
                            router_c(v, b + 1, router)

            def pool0(b, par, first_, last_):
                nc.gpsimd.wait_ge(s["row_loaded"], 16 * (b + 1))
                for e in range(NE0):
                    need(nc.gpsimd, s["y_used"], NE0 * (b - 1) + e + 1)
                    nc.gpsimd.nop(nofuse=True)
                    nc.gpsimd.partition_broadcast(coefB[:, e, :], row[0:1, e, :]).then_inc(s["bc_ready"], 1)
                    if e > 2 or (e < 2 and not first_):
                        mix_pool(*((b, par, e - 2) if e > 1 else (b - 1, 1 - par, NE0 + e - 2)))
                    if e == 1 and (more or not last_):
                        norm_b(f0 + b + 1)

            def sync0(b, par, first_, last_):
                if first_:
                    load0(2)
                    load0(3)
                row_sp(b, par, first_, last_)
                if first_:
                    for e in range(4, NE0):
                        load0(e)
                    if n == 0:
                        load_weights(nc.sync)

            SPLITS = ((0, 2), (2, IT))

            def g_hi_act():
                for k, (j0, j1) in enumerate(SPLITS):
                    nc.scalar.copy(gh[:, :, j0:j1, :], gate_up[:, :, j0:j1, :]).then_inc(s["w_hi"], 1)

            def g_lo_dve(v, k):
                j0, j1 = SPLITS[k]
                v.wait_ge(s["w_hi"], 2 * occ + k + 1)
                nc.vector.tensor_tensor(gl[:, :, j0:j1, :], gate_up[:, :, j0:j1, :], gh[:, :, j0:j1, :],
                                        ALU.subtract).then_inc(s["w_lo"], 1)

            def up1(b, par, j, first_):
                q = (par + j) % 2
                if j == 0:
                    nc.tensor.wait_ge(s["xl_ready"], b + 1)
                if first_ and j in (0, 2):
                    nc.tensor.wait_ge(s["w_lo"], 2 * occ + j // 2 + 1)
                need(nc.tensor, s["gated"], IT * b + j - 1)
                hi_lo(bank[2 * q][:], gh[:, 0, j, :], gl[:, 0, j, :], xh[par][:], xl[par][:], True, True)
                hi_lo(bank[2 * q + 1][:], gh[:, 1, j, :], gl[:, 1, j, :], xh[par][:], xl[par][:], True, True).then_inc(s["up_ready"], 1)

            def down1(b, par, j):
                if j == 0:
                    nc.tensor.wait_ge(s["gated"], IT * b + 1)
                    need(nc.tensor, s["acc_ready"], b - 1 if c0 else prior(b))
                else:
                    nc.tensor.wait_ge(s["hid_ready"], PAIRS * b + j)
                w = sh_d[:] if j == 0 else down_w[:, j - 1, :]
                nc.tensor.matmul(bank[4 + par][:], w, hid[slot(j)][:], start=(j == 0), stop=(j == IT - 1)).then_inc(s["down_done"], 1)

            def slot(j):
                return 4 if j == 0 else (j - 1) % 4

            def silu1(b, par, j):
                q = (par + j) % 2
                nc.scalar.wait_ge(s["up_ready"], IT * b + j + 1)
                nc.scalar.activation(silu[q][:], bank[2 * q][:], ACT.Silu).then_inc(s["act_done"], 1)

            def gate1(v, b, par, j):
                q = (par + j) % 2
                v.wait_ge(s["act_done"], IT * b + j + 1)
                if j == 0:
                    need(v, s["down_done"], IT * (b - 1) + 1)
                    nc.vector.scalar_tensor_tensor(out=hid[slot(0)][:], in0=silu[q][:], scalar=0.5, in1=bank[2 * q + 1][:],
                                                   op0=ALU.mult, op1=ALU.mult).then_inc(s["gated"], 1)
                    return
                need(v, s["hid_ready"], PAIRS * b + (j - 2 if j > 2 else 1 - j))
                nc.vector.tensor_tensor(tmp[q][:], silu[q][:], bank[2 * q + 1][:], ALU.mult).then_inc(s["gated"], 1)

            def weigh1(v, b, par, j):
                q = (par + j) % 2
                v.wait_ge(s["gated"], IT * b + j + 1)
                v.wait_ge(s["bc_ready"], PAIRS * b + j)
                need(v, s["down_done"], IT * b + j - (3 if j > 4 else 4))
                nc.vector.tensor_tensor(hid[slot(j)][:], tmp[q][:], coefB[:, j - 1, :], ALU.mult).then_inc(s["hid_ready"], 1)

            def sum1(b, par):
                nc.scalar.wait_ge(s["down_done"], IT * (b + 1))
                nc.scalar.copy(acc[par][:], bank[4 + par][:]).then_inc(s["acc_ready"], 1)

            LAG1 = 3

            def pe1(b, par, first_, last_):
                for j in range(IT):
                    up1(b, par, j, first_)
                    if j >= LAG1:
                        down1(b, par, j - LAG1)
                    elif not first_:
                        down1(b - 1, 1 - par, IT - LAG1 + j)
                    if j == 3 and (more or not last_):
                        norm_pe(f0 + b + 1)
                    if j == 4 and not last_:
                        router_pe(b + 1, 1 - par)
                    if j == 4 and not first_:
                        back_pe(b - 1, 1 - par)
                    if j == 2 and first_:
                        coef_pe(b)
                    if j == 8 and not last_:
                        coef_pe(b + 1)

            def act1(b, par, first_, last_):
                for j in range(IT):
                    silu1(b, par, j)
                    if j == 2 and not first_:
                        sum1(b - 1, 1 - par)
                    if j == 3 and (more or not last_):
                        norm_act(f0 + b + 1, 1 - par)
                        if not last_:
                            xh_act(b + 1, 1 - par)
                    if j == 4 and not last_:
                        router_act(b + 1)
                    if j == 2 and first_:
                        coef_act(b)
                    if j == 8 and not last_:
                        coef_act(b + 1)

            def dve1(v, b, par, first_, last_):
                for j in range(IT):
                    gate1(v, b, par, j)
                    if first_ and j == 0:
                        router_b(opening["router"])
                    if first_ and j == 1:
                        router_c(v, b, opening["router"])
                    if j > 1:
                        weigh1(v, b, par, j - 1)
                    elif j == 0 and not first_:
                        weigh1(v, b - 1, 1 - par, IT - 1)
                    if j == 5 and not first_:
                        back_dve(v, b - 1)
                    if more or not last_:
                        if j == 0:
                            norm_a(v, f0 + b + 1, (b + 1) % B)
                        if j == 1:
                            norm_c(v, f0 + b + 1, (b + 1) % B)
                    if not last_:
                        if j == 3:
                            xl_dve(v, b + 1, 1 - par)
                        if j == 4:
                            router = router_a(v, b + 1)
                        if j == 5:
                            router_b(router)
                        if j == 6:
                            router_c(v, b + 1, router)

            def tensor(t):
                after_phases(t, n)
                if kind == 1:
                    t.wait_ge(w_loaded, 16 * N_WEIGHTS)
                router_pe(c0, 0)
                sequences(t, pe0 if kind == 0 else pe1, c0)
                if kind == 0:
                    for k in range(LAG):
                        down0(c0 + B - 1, CH - LAG + k)
                else:
                    for j in range(IT - LAG1, IT):
                        down1(c0 + B - 1, 1, j)
                back_pe(c0 + B - 1, 1)

            def scalar(c):
                after_phases(c, n)
                xh_act(c0, 0)
                if kind == 0:
                    w_hi_act(0)
                    w_hi_act(1)
                else:
                    c.wait_ge(w_loaded, 16 * N_WEIGHTS)
                    g_hi_act()
                router_act(c0)
                sequences(c, act0 if kind == 0 else act1, c0)
                if kind == 1:
                    sum1(c0 + B - 1, 1)

            def vector(v):
                after_phases(v, n)
                xl_dve(v, c0, 0)
                if kind == 0:
                    w_lo_dve(v, 0)
                    w_lo_dve(v, 1)
                else:
                    g_lo_dve(v, 0)
                    g_lo_dve(v, 1)
                opening["router"] = router_a(v, c0)
                sequences(v, lambda b, par, f, l: (dve0 if kind == 0 else dve1)(v, b, par, f, l), c0)
                if kind == 0:
                    combine0(v, c0 + B - 1, 1, NE0 - 2)
                    combine0(v, c0 + B - 1, 1, NE0 - 1)
                else:
                    weigh1(v, c0 + B - 1, 1, IT - 1)
                back_dve(v, c0 + B - 1)

            def gpsimd(g):
                after_phases(g, n)
                sequences(g, pool0 if kind == 0 else pool1, c0)
                if kind == 0:
                    mix_pool(c0 + B - 1, 1, NE0 - 2)
                    mix_pool(c0 + B - 1, 1, NE0 - 1)

            def sync(q):
                if kind == 0:
                    load0(0)
                    load0(1)
                    if n == 0:
                        load_x_rest(q)
                after_phases(q, n)
                sequences(q, sync0 if kind == 0 else row_sp, c0)

            return {"tensor": tensor, "scalar": scalar, "vector": vector, "gpsimd": gpsimd, "sync": sync}

        def attn_phase(n):
            f0 = B * n
            names = ("q_ps", "kk_ps", "vv_ps", "k_ps", "v_ps", "q_sb", "kk_sb", "vv_sb", "k_sb", "v_sb", "q_split", "k_split",
                     "q_chain", "k1", "k_rest", "k2", "zero_tile", "zeroed", "m_consts", "qk_ones", "v9_ready", "mx_ready", "mx_read", "m_chain",
                     "m_split", "mT_ps", "mT_sb", "st_ready", "exp_done", "av_done", "o_sb", "oT_ps", "o_tok", "o_chain",
                     "otT_ps", "ot_sb", "z_ready", "x_bo")
            s = {k: sem(f"p{n}_{k}") for k in names}
            saved = {c: sem(f"p{n}_{c}_saved") for c in "qk"}
            ld = [[sem(f"p{n}_qk_loaded{i}{g}") for g in range(H // HG)] for i in range(2)]
            m_ld = [[sem(f"p{n}_m_loaded{i}{g}") for g in range(H // HG)] for i in range(2)]
            new_phase()
            qa = [view(P, H * T, BF16).rearrange("p (h t) -> p h t", h=H) for _ in range(2)]
            ka = [view(P, H * T, BF16).rearrange("p (h t) -> p h t", h=H) for _ in range(2)]
            v_all = view(P, B * TILES * H * (HD + 1)).rearrange("p (n h d) -> p n h d", h=H, d=HD + 1)
            v9 = [view(P, TILES * H * (HD + 1)).rearrange("p (n h d) -> p n h d", h=H, d=HD + 1) for _ in range(2)]
            mneg = view(P, TILES * H).rearrange("p (i h) -> p i h", i=TILES)
            mrest = view(P, TILES * HG).rearrange("p (i h) -> p i h", i=TILES)
            mparts = view(P, TILES * 3 * HG, BF16).rearrange("p (i j h) -> p i j h", i=TILES, j=3)
            rec = view(P, TILES * HG).rearrange("p (i h) -> p i h", i=TILES)
            mT = [[view(3 * HG, T, BF16) for _ in range(H // HG)] for _ in range(2)]
            zero3, ones3 = view(3, T, BF16), view(3, T, BF16)
            zeros = view(P, T, BF16)
            new_part()
            q_sb, kk_sb, vv_sb, k_sb = (view(P, T) for _ in range(4))
            rest = {"q": view(P, T), "k": view(P, T)}
            parts = {c: [view(P, 3 * T, BF16).rearrange("p (j t) -> p j t", j=3) for _ in range(2)] for c in "qk"}
            new_part()
            probs = [view(P, HG * T).rearrange("p (h t) -> p h t", h=HG) for _ in range(2)]
            o_sb = view(P, T)
            o_tok = view(P, T).rearrange("p (i e) -> p i e", i=TILES)
            ot_sb = view(P, T)
            xbo = view(P, T)
            scratch = {c: nc.dram_tensor(f"p{n}_{c}_parts", (B, 3, P, T), BF16, kind="Internal").ap() for c in "qk"}
            scale = float(HD) ** -0.5

            STEPS = (H // HG) * TILES

            def pe_a(b, par, first_, last_):
                x = xnT[par][:]
                nc.tensor.wait_ge(xnT_ready, f0 + b + 1)
                for i, (w, ps, sb_) in enumerate(((wq_p[:], "q_ps", "q_sb"), (wk[:], "kk_ps", "kk_sb"), (wv[:], "vv_ps", "vv_sb"))):
                    need(nc.tensor, s[sb_], b)
                    nc.tensor.matmul(bank[i][:], w, x, start=True, stop=True).then_inc(s[ps], 1)
                nc.tensor.wait_ge(s["kk_sb"], b + 1)
                need(nc.tensor, s["k_sb"], b)
                nc.tensor.matmul(bank[3][:], wl_p[:], kk_sb[:], start=True, stop=True).then_inc(s["k_ps"], 1)
                nc.tensor.wait_ge(s["vv_sb"], b + 1)
                need(nc.tensor, s["v_sb"], b)
                for i in range(TILES):
                    last = nc.tensor.matmul(bank[4][:, i * P:(i + 1) * P], vv_sb[:, i * P:(i + 1) * P], wl[:], start=True, stop=True)
                last.then_inc(s["v_ps"], 1)
                if not last_:
                    norm_pe(f0 + b + 1)

            def act_a(b, par, first_, last_):
                nc.scalar.wait_ge(s["zero_tile"], 1)
                clear(nc.scalar, ka, b)

                def biased(i, ps, dst, at, done, free, count):
                    nc.scalar.wait_ge(s[ps], b + 1)
                    need(nc.scalar, s[free], count)
                    nc.scalar.activation(dst[:], bank[i][:], ACT.Identity, bias=vecs[:, at:at + 1]).then_inc(s[done], 1)
                biased(1, "kk_ps", kk_sb, V_BK, "kk_sb", "k_ps", b)
                biased(2, "vv_ps", vv_sb, V_BV, "vv_sb", "v_ps", b)
                biased(0, "q_ps", q_sb, V_BQ, "q_sb", "q_split", b)
                biased(3, "k_ps", k_sb, V_BL, "k_sb", "k_split", b)
                k1_act(b, par)
                if not last_:
                    norm_act(f0 + b + 1, 1 - par)
                k2_act(b, par)

            def split_q(v, b, par):
                v.wait_ge(s["q_sb"], b + 1)
                need(v, saved["q"], 16 * b)
                chain = Chain(v, s["q_chain"], 3)
                chain.begin(b)
                p_, r = parts["q"][par], rest["q"]
                chain(nc.vector.tensor_copy(p_[:, 0, :], q_sb[:]))
                chain(nc.vector.tensor_tensor(r[:], q_sb[:], p_[:, 0, :], ALU.subtract))
                chain(nc.vector.tensor_copy(p_[:, 1, :], r[:]))
                chain.end()
                nc.vector.tensor_tensor(p_[:, 2, :], r[:], p_[:, 1, :], ALU.subtract).then_inc(s["q_split"], 1)

            def k1_act(b, par):
                nc.scalar.wait_ge(s["k_sb"], b + 1)
                need(nc.scalar, saved["k"], 16 * b)
                nc.scalar.copy(parts["k"][par][:, 0, :], k_sb[:]).then_inc(s["k1"], 1)

            def k2_act(b, par):
                nc.scalar.wait_ge(s["k_rest"], b + 1)
                nc.scalar.copy(parts["k"][par][:, 1, :], rest["k"][:]).then_inc(s["k2"], 1)

            def split_k(b, par):
                nc.gpsimd.wait_ge(s["k1"], b + 1)
                need(nc.gpsimd, s["k_split"], b)
                nc.gpsimd.tensor_tensor(rest["k"][:], k_sb[:], parts["k"][par][:, 0, :], ALU.subtract).then_inc(s["k_rest"], 1)
                nc.gpsimd.wait_ge(s["k2"], b + 1)
                nc.gpsimd.tensor_tensor(parts["k"][par][:, 2, :], rest["k"][:], parts["k"][par][:, 1, :],
                                        ALU.subtract).then_inc(s["k_split"], 1)

            def clear(eng, tiles, b):
                copy = eng.copy if eng is nc.scalar else eng.tensor_copy
                for m in tiles:
                    copy(m[:, bass.ds(b * (H // B), H // B), :],
                         zeros.unsqueeze(1).to_broadcast([P, H // B, T])).then_inc(s["zeroed"], 1)

            def dve_a(v, b, par, first_, last_):
                if not last_:
                    norm_a(v, f0 + b + 1, b + 1)
                if first_:
                    nc.vector.memset(zeros[:], 0.0).then_inc(s["zero_tile"], 1)
                    v.wait_ge(s["zero_tile"], 1)
                clear(nc.vector, qa, b)
                if not last_:
                    norm_c(v, f0 + b + 1, b + 1)
                v.wait_ge(s["v_ps"], b + 1)
                nc.vector.tensor_tensor(
                    v_all[:, bass.ds(b * TILES, TILES), :, 0:HD], bank[4][:].rearrange("p (i h d) -> p i h d", i=TILES, d=HD),
                    bl_bc[:].rearrange("p (h d) -> p h d", d=HD).unsqueeze(1).to_broadcast([P, TILES, H, HD]),
                    ALU.add).then_inc(s["v_sb"], 1)
                need(v, s["q_split"], b)
                split_q(v, b, par)
                if first_:
                    nc.vector.memset(bank[6][:], 0.0).then_inc(s["zeroed"], 1)
                    nc.vector.memset(v_all[:, :, :, HD:], 1.0).then_inc(s["zeroed"], 1)
                    nc.vector.memset(zero3, 0.0).then_inc(s["m_consts"], 1)
                    nc.vector.memset(ones3, 1.0).then_inc(s["m_consts"], 1)

            def pool_a(b, par, first_, last_):
                if not last_:
                    norm_b(f0 + b + 1)
                split_k(b, par)

            def first_loads(q):
                q.wait_ge(s["zeroed"], 4 * B + 2)
                q.wait_ge(s["m_consts"], 2)
                for c in "qk":
                    q.wait_ge(saved[c], 32)
                for m in ka:
                    q.dma_start(m[M0:M1, :, :], ones3.unsqueeze(1).to_broadcast([3, H, T])).then_inc(s["qk_ones"], 16)
                for i in range(2):
                    for g in range(GB):
                        load(i, i, g)

            def sp_a(b, par, first_, last_):
                if last_:
                    first_loads(nc.sync)
                for c in "qk":
                    nc.sync.wait_ge(s[c + "_split"], b + 1)
                    nc.sync.dma_start(scratch[c][bass.ds(b, 1)].rearrange("o j p t -> p (o j) t"), parts[c][par][:]).then_inc(saved[c], 16)

            NLD = 7
            M0, M1 = 6 * HD, 6 * HD + 3
            GB = H // HG

            def load(b, par, g):
                q, k = (scratch[c][bass.ds(b, 1)].rearrange("o j (d h) t -> (o j d) h t", h=H)[:, g * HG:(g + 1) * HG, :] for c in "qk")
                hs = slice(g * HG, (g + 1) * HG)
                for r, j, w in ((0, 0, 3), (3, 1, 2), (5, 2, 1)):
                    src = q[j * HD:(j + 1) * HD].unsqueeze(0).to_broadcast([w, HD, HG, T])
                    nc.sync.dma_start(qa[par][r * HD:(r + w) * HD, hs, :], src).then_inc(ld[par][g], 16)
                for r, j, w in ((0, 0, 3), (3, 0, 2), (5, 0, 1)):
                    nc.sync.dma_start(ka[par][r * HD:(r + w) * HD, hs, :], k[j * HD:(j + w) * HD]).then_inc(ld[par][g], 16)
                nc.sync.dma_start(qa[par][M0:M1, hs, :], zero3.unsqueeze(1).to_broadcast([3, HG, T])).then_inc(ld[par][g], 16)

            def max_pe(b, par, t, banks=2):
                h, i = t // TILES, t % TILES
                if t % (HG * TILES) == 0:
                    nc.tensor.wait_ge(ld[par][h // HG], 16 * NLD * (b // 2 + 1))
                need(nc.tensor, s["mx_read"], H * TILES * b + t + 1 - banks)
                nc.tensor.matmul(bank[t % banks][:], qa[par][:, h, i * P:(i + 1) * P], ka[par][:, h, :], start=True, stop=True).then_inc(s["mx_ready"], 1)

            def max_dve(v, b, t, banks=2):
                h, i = t // TILES, t % TILES
                v.wait_ge(s["mx_ready"], H * TILES * b + t + 1)
                nc.vector.tensor_reduce(mneg[:, i, h:h + 1], bank[t % banks][:], AX_X, ALU.max, negate=True).then_inc(s["mx_read"], 1)

            def msplit_dve(v, b, g):
                chain = Chain(v, s["m_chain"], 3)
                chain.begin(b * (H // HG) + g)
                v.wait_ge(s["mx_read"], H * TILES * b + HG * TILES * (g + 1))
                need(v, s["mT_ps"], b * (H // HG) + g)
                m = mneg[:, :, g * HG:(g + 1) * HG]
                chain(nc.vector.tensor_copy(mparts[:, :, 0, :], m))
                chain(nc.vector.tensor_tensor(mrest[:], m, mparts[:, :, 0, :], ALU.subtract))
                chain(nc.vector.tensor_copy(mparts[:, :, 1, :], mrest[:]))
                chain.end()
                nc.vector.tensor_tensor(mparts[:, :, 2, :], mrest[:], mparts[:, :, 1, :], ALU.subtract).then_inc(s["m_split"], 1)

            def mT_pe(b, g):
                nc.tensor.wait_ge(s["m_split"], b * GB + g + 1)
                for i in range(TILES):
                    last = nc.tensor.transpose(bank[7][:].bitcast(BF16)[0:3 * HG, i * P:(i + 1) * P],
                                               mparts[:, i, :, :].rearrange("p j h -> p (j h)"), identb[:])
                last.then_inc(s["mT_ps"], 1)

            def mT_act(b, par, g):
                nc.scalar.wait_ge(s["mT_ps"], b * GB + g + 1)
                nc.scalar.copy(mT[par][g][:], bank[7][:].bitcast(BF16)[0:3 * HG, 0:T]).then_inc(s["mT_sb"], 1)

            def m_sp(b, par, g):
                nc.sync.wait_ge(s["mT_sb"], b * GB + g + 1)
                nc.sync.dma_start(qa[par][M0:M1, g * HG:(g + 1) * HG, :], mT[par][g][:]).then_inc(m_ld[par][g], 16)

            def st_pe(b, par, st, hh):
                g, kt = st // TILES, st % TILES
                t = HG * st + hh
                if kt == 0 and hh == 0:
                    nc.tensor.wait_ge(m_ld[par][g], 16 * ((b // 2) + 1))
                need(nc.tensor, s["exp_done"], H * TILES * b + t - 3)
                nc.tensor.matmul(bank[2 + t % 4][:], ka[par][:, g * HG + hh, kt * P:(kt + 1) * P], qa[par][:, g * HG + hh, :],
                                 start=True, stop=True).then_inc(s["st_ready"], 1)

            def exp_act(b, st, hh):
                t = HG * st + hh
                if hh == 0:
                    need(nc.scalar, s["av_done"], STEPS * b + st - 1)
                nc.scalar.wait_ge(s["st_ready"], H * TILES * b + t + 1)
                nc.scalar.activation(probs[st % 2][:, hh, :], bank[2 + t % 4][:], ACT.Exp, scale=scale).then_inc(s["exp_done"], 1)

            def av_pe(b, par, st):
                g, kt = st // TILES, st % TILES
                nc.tensor.wait_ge(s["exp_done"], H * TILES * b + HG * (st + 1))
                if st == 0:
                    nc.tensor.wait_ge(s["v9_ready"], b + 1)
                if kt == 0:
                    need(nc.tensor, s["o_sb"], GB * b + g)
                for hh in range(HG):
                    last = nc.tensor.matmul(bank[6][32 * hh:32 * hh + HD + 1, :], v9[par][:, kt, g * HG + hh, :], probs[st % 2][:, hh, :],
                                            start=(kt == 0), stop=(kt == TILES - 1))
                last.then_inc(s["av_done"], 1)

            def o_act(b, g):
                nc.scalar.wait_ge(s["av_done"], STEPS * b + TILES * (g + 1))
                need(nc.scalar, s["oT_ps"], GB * b + g)
                nc.scalar.copy(o_sb[:], bank[6][:]).then_inc(s["o_sb"], 1)

            def o_pe(b, g):
                nc.tensor.wait_ge(s["o_sb"], GB * b + g + 1)
                for i in range(TILES):
                    last = nc.tensor.transpose(bank[7][:, i * P:(i + 1) * P], o_sb[:, i * P:(i + 1) * P], ident[:])
                last.then_inc(s["oT_ps"], 1)

            def o_dve(v, b, g):
                v.wait_ge(s["oT_ps"], GB * b + g + 1)
                if g == 0:
                    need(v, s["otT_ps"], b)
                o = bank[7][:].rearrange("p (i h c) -> p i h c", i=TILES, h=HG)
                need(v, s["o_tok"], GB * b + g)
                nc.vector.reciprocal(rec[:], o[:, :, :, HD]).then_inc(s["o_chain"], 1)
                v.wait_ge(s["o_chain"], GB * b + g + 1)
                nc.vector.tensor_tensor(
                    o_tok[:, :, g * HG * HD:(g + 1) * HG * HD].rearrange("p i (h d) -> p i h d", h=HG), o[:, :, :, 0:HD],
                    rec[:].unsqueeze(3).to_broadcast([P, TILES, HG, HD]), ALU.mult).then_inc(s["o_tok"], 1)

            def ot_pe(b):
                nc.tensor.wait_ge(s["o_tok"], GB * (b + 1))
                for i in range(TILES):
                    last = nc.tensor.transpose(bank[7][:, i * P:(i + 1) * P], o_tok[:, i, :], ident[:])
                last.then_inc(s["otT_ps"], 1)

            def ot_act(b):
                nc.scalar.wait_ge(s["otT_ps"], b + 1)
                nc.scalar.copy(ot_sb[:], bank[7][:]).then_inc(s["ot_sb"], 1)

            def z_pe(b):
                nc.tensor.wait_ge(s["ot_sb"], b + 1)
                for i in range(TILES):
                    last = nc.tensor.matmul(bank[7][:, i * P:(i + 1) * P], ot_sb[:, i * P:(i + 1) * P], wo[:], start=True, stop=True)
                last.then_inc(s["z_ready"], 1)

            def xbo_pool(b):
                need(nc.gpsimd, x_upd, f0 + b)
                nc.gpsimd.tensor_tensor(xbo[:], flat(x_of(b)), flat(bo_bc[:]), ALU.add).then_inc(s["x_bo"], 1)

            def z_dve(v, b):
                v.wait_ge(s["z_ready"], b + 1)
                v.wait_ge(s["x_bo"], b + 1)
                nc.vector.tensor_tensor(flat(x_of(b)), bank[7][:], xbo[:], ALU.add).then_inc(x_upd, 1)

            ORDER = (("exp", 0), ("exp", 1), ("max", 0), ("exp", 2), ("max", 1), ("sum", 0), ("max", 2), ("exp", 3), ("max", 3))

            def pe_b(b, par, first_, last_):
                for st in range(STEPS):
                    g, kt = st // TILES, st % TILES
                    for what, hh in ORDER:
                        if what == "exp":
                            st_pe(b, par, st, hh)
                        elif what == "max" and not last_:
                            max_pe(b + 1, 1 - par, HG * st + hh)
                        elif what == "sum" and st:
                            av_pe(b, par, st - 1)
                        elif what == "sum" and not first_:
                            av_pe(b - 1, 1 - par, STEPS - 1)
                    if st == 0:
                        need(nc.tensor, s["o_tok"], GB * b - 1)
                        nc.tensor.wait_ge(s["mT_sb"], GB * b + GB - 1)
                        mT_pe(b, GB - 1)
                    elif kt == 0 and not last_:
                        if g == 1:
                            need(nc.tensor, x_upd, f0 + b)
                        else:
                            nc.tensor.wait_ge(s["o_tok"], GB * b + g - 1)
                        nc.tensor.wait_ge(s["mT_sb"], GB * b + GB + g - 1)
                        mT_pe(b + 1, g - 1)
                    if st == 1 and not first_:
                        nc.tensor.wait_ge(s["mT_sb"], GB * b + GB)
                        o_pe(b - 1, GB - 1)
                    elif st > 1 and kt == 1:
                        if last_:
                            nc.tensor.wait_ge(x_upd, f0 + b)
                            nc.tensor.wait_ge(s["o_tok"], GB * b + g - 1)
                        else:
                            nc.tensor.wait_ge(s["mT_sb"], GB * b + GB + g)
                        o_pe(b, g - 1)
                    if st == 2 and not first_:
                        ot_pe(b - 1)
                    if st == 3 and not first_:
                        z_pe(b - 1)

            def act_b(b, par, first_, last_):
                for st in range(STEPS):
                    g, kt = st // TILES, st % TILES
                    for hh in range(HG):
                        exp_act(b, st, hh)
                        if hh == 1 and kt == 0:
                            if st:
                                o_act(b, g - 1)
                            elif not first_:
                                o_act(b - 1, GB - 1)
                    if kt == 0:
                        if st == 0:
                            mT_act(b, par, GB - 1)
                        elif not last_:
                            mT_act(b + 1, 1 - par, g - 1)
                    if st == 2 and not first_:
                        ot_act(b - 1)

            def dve_b(v, b, par, first_, last_):
                for st in range(STEPS):
                    g, kt = st // TILES, st % TILES
                    if not last_:
                        for hh in range(HG):
                            max_dve(v, b + 1, HG * st + hh)
                    if kt == 3 and not last_:
                        msplit_dve(v, b + 1, g)
                    if kt == 1:
                        if st > 1:
                            o_dve(v, b, g - 1)
                        elif not first_:
                            o_dve(v, b - 1, GB - 1)
                    if st == 3 and not first_:
                        z_dve(v, b - 1)

            def sp_b(b, par, first_, last_):
                m_sp(b, par, GB - 1)
                if last_:
                    return
                for g in range(GB):
                    nc.sync.wait_ge(s["st_ready"], H * TILES * b + HG * TILES * (g + 1))
                    load((b + 2) % B, par, g)
                    if g < GB - 1:
                        m_sp(b + 1, 1 - par, g)

            def pool_b(b, par, first_, last_):
                need(nc.gpsimd, s["av_done"], STEPS * prior(b))
                nc.gpsimd.nop(nofuse=True)
                nc.gpsimd.tensor_copy(v9[par][:].rearrange("p n h d -> p (n h d)"),
                                      v_all[:, bass.ds(b * TILES, TILES), :, :].rearrange("p n h d -> p (n h d)")).then_inc(s["v9_ready"], 1)
                xbo_pool(b)

            def tensor(t):
                after_phases(t, n)
                t.wait_ge(w_loaded, 16 * N_WEIGHTS)
                t.wait_ge(tables_ready, 2)
                sequences(t, pe_a)
                nc.tensor.wait_ge(s["k_sb"], B)
                nc.tensor.wait_ge(s["q_sb"], B)
                nc.tensor.wait_ge(s["vv_sb"], B)
                nc.tensor.wait_ge(s["v_sb"], B)
                nc.tensor.wait_ge(s["zeroed"], 4 * B + 2)
                nc.tensor.wait_ge(s["qk_ones"], 32)
                nc.tensor.wait_ge(xnT_ready, f0 + B)
                for t_ in range(H * TILES):
                    max_pe(0, 0, t_, 4)
                    if t_ % (HG * TILES) == 3 and t_ > 3:
                        need(nc.tensor, s["mT_sb"], t_ // (HG * TILES) - 1)
                        mT_pe(0, t_ // (HG * TILES) - 1)
                nc.tensor.wait_ge(s["mx_read"], H * TILES)
                sequences(t, pe_b)
                av_pe(B - 1, 1, STEPS - 1)
                nc.tensor.wait_ge(s["o_tok"], GB * B - 1)
                o_pe(B - 1, GB - 1)
                ot_pe(B - 1)
                for g in range(GB):
                    nc.tensor.wait_ge(ld[0][g], 16 * NLD * (B // 2 + 1))
                z_pe(B - 1)
                norm_pe(f0 + B)

            def scalar(c):
                after_phases(c, n)
                sequences(c, act_a)
                for g in range(GB - 1):
                    mT_act(0, 0, g)
                nc.scalar.wait_ge(s["q_split"], B)
                nc.scalar.wait_ge(s["k_split"], B)
                nc.scalar.wait_ge(s["v_ps"], B)
                for c_ in "qk":
                    nc.scalar.wait_ge(saved[c_], 16 * B)
                sequences(c, act_b)
                o_act(B - 1, GB - 1)
                ot_act(B - 1)
                norm_act(f0 + B, 0)

            def vector(v):
                after_phases(v, n)
                v.wait_ge(tables_ready, 2)
                sequences(v, lambda b, par, f, l: dve_a(v, b, par, f, l))
                for t_ in range(H * TILES):
                    max_dve(v, 0, t_, 4)
                    if t_ % (HG * TILES) == HG * TILES - 1:
                        msplit_dve(v, 0, t_ // (HG * TILES))
                for c_ in "qk":
                    v.wait_ge(saved[c_], 16 * B)
                v.wait_ge(s["v_ps"], B)
                v.wait_ge(s["k_split"], B)
                sequences(v, lambda b, par, f, l: dve_b(v, b, par, f, l))
                o_dve(v, B - 1, GB - 1)
                z_dve(v, B - 1)
                norm_a(v, f0 + B, 0)
                norm_c(v, f0 + B, 0)

            def gpsimd(g):
                g.wait_ge(w_loaded, 16 * N_WEIGHTS)
                g.partition_broadcast(bl_bc[:], bl_bc[0:1, :])
                for i in range(TILES):
                    last = g.partition_broadcast(bo_bc[:, TILES - 1 - i, :], bo_bc[0:1, 0, :])
                for w, w_p in ((wq, wq_p), (wl, wl_p)):
                    last = g.tensor_copy(w_p[:].rearrange("p (d h) -> p d h", d=HD), w[:].rearrange("p (h d) -> p d h", d=HD))
                last.then_inc(tables_ready, 1)
                after_phases(g, n)
                sequences(g, pool_a)
                nc.gpsimd.wait_ge(s["v_sb"], B)
                nc.gpsimd.wait_ge(s["q_split"], B)
                for c_ in "qk":
                    nc.gpsimd.wait_ge(saved[c_], 16 * B)
                sequences(g, pool_b)
                norm_b(f0 + B)

            def sync(q):
                after_phases(q, n)
                sequences(q, sp_a)
                for g in range(GB - 1):
                    m_sp(0, 0, g)
                sequences(q, sp_b)

            return {"tensor": tensor, "scalar": scalar, "vector": vector, "gpsimd": gpsimd, "sync": sync}

        def ssm_phase(n):
            f0 = B * n
            names = ("xs_ps", "xs_sb", "edges", "conv_chain", "conv", "xs_act", "z_act", "dtlo_ps", "dtlo_sb", "bc_ps", "bc_sb",
                     "bs_chain", "bs", "dt_ps", "relu", "abs", "e_sb", "ln", "dsum_chain", "dsum", "dm_ps", "decay", "decay_rows", "decay_exp",
                     "bs_ps", "scanned", "s_ps", "s_tok", "y", "y_chain", "y_mv", "y_var", "y_rs", "yn", "ynT_ps", "yg", "yz", "z_ready")
            s = {k: sem(f"p{n}_{k}") for k in names}
            new_phase()
            z_all = view(P, DC * B * T).rearrange("p (c b t) -> p c b t", c=DC, b=B)
            dtlo_all = view(DTR, B * T).rearrange("p (b t) -> p b t", b=B)
            decays = view(1, B * T).rearrange("p (b t) -> p b t", b=B)
            c_all = view(P, B * TILES * DS).rearrange("p (n d) -> p n d", d=DS)
            bs_all = view(P, TILES * B).rearrange("p (i b) -> p i b", i=TILES)
            s_tok = view(P, B * TILES).rearrange("p (b i) -> p b i", b=B)
            decay8, state8 = view(B, T), view(B, T)
            new_part()
            xs_pad = [view(P, T + 2) for _ in range(DC)]
            conv = [view(P, T) for _ in range(DC)]
            xs = [[view(P, T) for _ in range(DC)] for _ in range(2)]
            bcx = view(P, TILES * (2 * DS + 1)).rearrange("p (i n) -> p i n", i=TILES)
            bx = view(P, TILES * DS).rearrange("p (i d) -> p i d", i=TILES)
            new_part()
            relu_t, e_t = ([view(P, DC * T).rearrange("p (c t) -> p c t", c=DC) for _ in range(2)] for _ in range(2))
            ln_t = view(P, DC * T).rearrange("p (c t) -> p c t", c=DC)
            dsum_t = [view(P, T) for _ in range(2)]
            new_part()
            y = view(P, TILES * DS).rearrange("p (i d) -> p i d", i=TILES)
            yn = view(P, T)
            yg = [view(P, T) for _ in range(DC)]
            yz = [[view(P, T) for _ in range(DC)] for _ in range(2)]
            at_bc, n_bc = DTR, 2 * DS + 1

            def pe_1(b, par, first_, last_):
                nc.tensor.wait_ge(xnT_ready, f0 + b + 1)
                for c in range(DC):
                    need(nc.tensor, s["xs_sb"], DC * b)
                    nc.tensor.matmul(bank[c][:], w_in[:, c * P:(c + 1) * P], xnT[par][:], start=True, stop=True).then_inc(s["xs_ps"], 1)
                for c in range(DC):
                    need(nc.tensor, s["z_act"], DC * b)
                    nc.tensor.matmul(bank[2 + c][:], w_in[:, DI + c * P:DI + (c + 1) * P], xnT[par][:], start=True, stop=True).then_inc(s["xs_ps"], 1)
                if not first_:
                    x_proj(b - 1, 1 - par)
                if not last_:
                    norm_pe(f0 + b + 1)

            def x_proj(b, par):
                nc.tensor.wait_ge(s["xs_act"], DC * (b + 1))
                for c in range(DC):
                    last = nc.tensor.matmul(bank[4][0:DTR, :], w_x[:, c, 0:DTR], xs[par][c][:], start=(c == 0), stop=(c == DC - 1))
                last.then_inc(s["dtlo_ps"], 1)
                for i in range(TILES):
                    for c in range(DC):
                        last = nc.tensor.matmul(bank[5 + par][:, i * n_bc:(i + 1) * n_bc], xs[par][c][:, i * P:(i + 1) * P],
                                                w_x[:, c, at_bc:], start=(c == 0), stop=(c == DC - 1))
                last.then_inc(s["bc_ps"], 1)

            def xs_act(b, par):
                for c in range(DC):
                    nc.scalar.wait_ge(s["conv"], DC * b + c + 1)
                    nc.scalar.activation(xs[par][c][:], conv[c][:], ACT.Silu).then_inc(s["xs_act"], 1)

            def dtlo_act(b):
                nc.scalar.wait_ge(s["dtlo_ps"], b + 1)
                nc.scalar.copy(dtlo_all[:, bass.ds(b, 1), :], bank[4][0:DTR, :]).then_inc(s["dtlo_sb"], 1)

            def act_1(b, par, first_, last_):
                if not first_:
                    xs_act(b - 1, 1 - par)
                for c in range(DC):
                    nc.scalar.wait_ge(s["xs_ps"], 2 * DC * b + c + 1)
                    need(nc.scalar, s["conv"], DC * (b - 1) + c + 1)
                    nc.scalar.copy(xs_pad[c][:, 1:T + 1], bank[c][:]).then_inc(s["xs_sb"], 1)
                for c in range(DC):
                    nc.scalar.wait_ge(s["xs_ps"], 2 * DC * b + DC + c + 1)
                    nc.scalar.activation(z_all[:, c, bass.ds(b, 1), :], bank[2 + c][:], ACT.Silu).then_inc(s["z_act"], 1)
                if not first_:
                    dtlo_act(b - 1)
                if not last_:
                    norm_act(f0 + b + 1, 1 - par)

            def conv_dve(chain, v, b, c):
                v.wait_ge(s["xs_sb"], DC * b + c + 1)
                need(v, s["xs_act"], DC * (b - 1) + c + 1)
                w = [w_conv[:, c, k:k + 1] for k in range(3)]
                chain(nc.vector.tensor_scalar(conv[c][:], xs_pad[c][:, 1:T + 1], w[1], None, ALU.mult))
                chain(nc.vector.scalar_tensor_tensor(out=conv[c][:], in0=xs_pad[c][:, 0:T], scalar=w[0], in1=conv[c][:],
                                                     op0=ALU.mult, op1=ALU.add))
                nc.vector.scalar_tensor_tensor(out=conv[c][:], in0=xs_pad[c][:, 2:T + 2], scalar=w[2], in1=conv[c][:],
                                               op0=ALU.mult, op1=ALU.add).then_inc(s["conv"], 1)

            def bs_dve(v, b, par):
                chain = Chain(v, s["bs_chain"], 2)
                chain.begin(b)
                v.wait_ge(s["bc_ps"], b + 1)
                nc.vector.tensor_copy(bcx[:], bank[5 + par][:, 0:TILES * n_bc].rearrange("p (i n) -> p i n", i=TILES)).then_inc(s["bc_sb"], 1)
                v.wait_ge(s["bc_sb"], b + 1)
                chain(nc.vector.tensor_tensor(bx[:], bcx[:, :, 0:DS], bcx[:, :, 2 * DS:].to_broadcast([P, TILES, DS]), ALU.mult))
                chain(nc.vector.tensor_reduce(bs_all[:, :, bass.ds(b, 1)], bx[:], AX_X, ALU.add))
                chain.end()
                nc.vector.tensor_copy(c_all[:, bass.ds(b * TILES, TILES), :], bcx[:, :, DS:2 * DS]).then_inc(s["bs"], 1)
                v.wait_ge(s["bs"], b + 1)

            def dve_1(v, b, par, first_, last_):
                if not last_:
                    norm_a(v, f0 + b + 1, b + 1)
                chain = Chain(v, s["conv_chain"], 2 * DC)
                chain.begin(b)
                conv_dve(chain, v, b, 0)
                if not last_:
                    norm_c(v, f0 + b + 1, b + 1)
                for c in range(1, DC):
                    conv_dve(chain, v, b, c)
                chain.end()
                if not first_:
                    bs_dve(v, b - 1, 1 - par)

            def dt_pe(b, par):
                need(nc.tensor, s["abs"], DC * (b - 1))
                for c in range(DC):
                    last = nc.tensor.matmul(bank[2 * par + c][:], w_dt[:, c * P:(c + 1) * P],
                                            dtlo_all[:, bass.ds(b, 1), :].rearrange("p o t -> p (o t)"), start=True, stop=True)
                last.then_inc(s["dt_ps"], 1)

            def pe_2(b, par, first_, last_):
                if first_:
                    dt_pe(b, par)
                if not last_:
                    dt_pe(b + 1, 1 - par)
                if not first_:
                    mean_pe(b - 1, 1 - par)

            def mean_pe(b, par):
                nc.tensor.wait_ge(s["dsum"], b + 1)
                nc.tensor.matmul(bank[4 + par][0:1, :], w_x[:, 0, DTR + 2 * DS:], dsum_t[par][:], start=True, stop=True).then_inc(s["dm_ps"], 1)

            def act_2(b, par, first_, last_):
                for c in range(DC):
                    nc.scalar.wait_ge(s["abs"], DC * b + c + 1)
                    nc.scalar.activation(e_t[par][:, c, :], e_t[par][:, c, :], ACT.Exp, bias=vecs[:, V_BDT + c:V_BDT + c + 1]).then_inc(s["e_sb"], 1)
                nc.scalar.wait_ge(s["e_sb"], DC * (b + 1))
                need(nc.scalar, s["dsum"], b)
                nc.scalar.activation(ln_t[:], e_t[par][:], ACT.Ln, bias=1.0).then_inc(s["ln"], 1)
                if not first_:
                    dm_act(b - 1, 1 - par)

            def dm_act(b, par):
                nc.scalar.wait_ge(s["dm_ps"], b + 1)
                nc.scalar.copy(decays[0:1, bass.ds(b, 1), :], bank[4 + par][0:1, :]).then_inc(s["decay"], 1)

            def parts_dve(v, b, par):
                v.wait_ge(s["dt_ps"], b + 1)
                for c in range(DC):
                    nc.vector.tensor_scalar(relu_t[par][:, c, :], bank[2 * par + c][:], vecs[:, V_BDT + c:V_BDT + c + 1], 0.0,
                                            ALU.add, ALU.max).then_inc(s["relu"], 1)
                for c in range(DC):
                    v.wait_ge(s["relu"], DC * b + c + 1)
                    nc.vector.scalar_tensor_tensor(out=e_t[par][:, c, :], in0=relu_t[par][:, c, :], scalar=-2.0,
                                                   in1=bank[2 * par + c][:], op0=ALU.mult, op1=ALU.add).then_inc(s["abs"], 1)

            def dve_2(v, b, par, first_, last_):
                if first_:
                    parts_dve(v, b, par)
                if not last_:
                    parts_dve(v, b + 1, 1 - par)
                chain = Chain(v, s["dsum_chain"], 2)
                chain.begin(b)
                need(v, s["dm_ps"], prior(b))
                d = dsum_t[par]
                chain(nc.vector.tensor_tensor(d[:], relu_t[par][:, 0, :], relu_t[par][:, 1, :], ALU.add))
                v.wait_ge(s["ln"], b + 1)
                chain(nc.vector.tensor_tensor(d[:], d[:], ln_t[:, 0, :], ALU.add))
                chain.end()
                nc.vector.tensor_tensor(d[:], d[:], ln_t[:, 1, :], ALU.add).then_inc(s["dsum"], 1)

            def dve_4a(v, b):
                chain = Chain(v, s["y_chain"], 2)
                chain.begin(b)
                chain(nc.vector.tensor_tensor(y[:], c_all[:, bass.ds(b * TILES, TILES), :],
                                              s_tok[:, bass.ds(b, 1), :].rearrange("p o i -> p (o i)").unsqueeze(2).to_broadcast([P, TILES, DS]),
                                              ALU.mult))
                for i in range(TILES):
                    last = nc.vector.bn_stats(stats[:, i, :], y[:, i, :])
                chain(last)
                nc.vector.nop(nofuse=True)
                for i in range(TILES):
                    last = nc.vector.bn_aggr(mv[:, i, :], stats[:, i, :])
                last.then_inc(s["y_mv"], 1)
                chain.end()

            def yn_dve(v, b):
                v.wait_ge(s["y_rs"], b + 1)
                need(v, s["ynT_ps"], b)
                for i in range(TILES):
                    last = nc.vector.tensor_scalar(yn[:, i * P:(i + 1) * P].rearrange("p (r d) -> p r d", d=DS),
                                                   y[:, i, :].unsqueeze(1).to_broadcast([P, P // DS, DS]),
                                                   mv[:, i, 0:1], rs_y[:, i:i + 1], ALU.subtract, ALU.mult)
                last.then_inc(s["yn"], 1)
                v.wait_ge(s["yn"], b + 1)

            def dve_4b(v, b, par):
                for c in range(DC):
                    v.wait_ge(s["yg"], DC * b + c + 1)
                    need(v, s["z_ready"], prior(b))
                    nc.vector.tensor_tensor(yz[par][c][:], yg[c][:], z_all[:, c, bass.ds(b, 1), :].rearrange("p o t -> p (o t)"),
                                            ALU.mult).then_inc(s["yz"], 1)

            def dve_4c(v, b, par):
                v.wait_ge(s["z_ready"], b + 1)
                nc.vector.tensor_tensor(flat(x_of(b)), bank[2 + par][:], flat(x_of(b)), ALU.add).then_inc(x_upd, 1)

            def dve_4(v, b, par, first_, last_):
                if not last_:
                    dve_4a(v, b + 1)
                dve_4b(v, b, par)
                if not first_:
                    dve_4c(v, b - 1, 1 - par)
                if not last_:
                    yn_dve(v, b + 1)

            def pe_4(b, par, first_, last_):
                nc.tensor.wait_ge(s["yn"], b + 1)
                need(nc.tensor, s["yg"], DC * prior(b))
                for i in range(TILES):
                    last = nc.tensor.transpose(bank[par][:, i * P:(i + 1) * P], yn[:, i * P:(i + 1) * P], ident[:])
                last.then_inc(s["ynT_ps"], 1)
                if not first_:
                    z_pe4(b - 1, 1 - par)

            def z_pe4(b, par):
                nc.tensor.wait_ge(s["yz"], DC * (b + 1))
                need(nc.tensor, x_upd, f0 + b - 1)
                for i in range(TILES):
                    for c in range(DC):
                        last = nc.tensor.matmul(bank[2 + par][:, i * P:(i + 1) * P], yz[par][c][:, i * P:(i + 1) * P], w_out[:, c, :],
                                                start=(c == 0), stop=(c == DC - 1))
                last.then_inc(s["z_ready"], 1)

            def act_4(b, par, first_, last_):
                nc.scalar.wait_ge(s["ynT_ps"], b + 1)
                for c in range(DC):
                    need(nc.scalar, s["yz"], DC * (b - 1) + c + 1)
                    nc.scalar.activation(yg[c][:], bank[par][:], ACT.Identity, bias=vecs[:, V_B + c:V_B + c + 1],
                                         scale=vecs[:, V_G + c:V_G + c + 1]).then_inc(s["yg"], 1)

            def tensor(t):
                after_phases(t, n)
                t.wait_ge(w_loaded, 16 * N_WEIGHTS)
                sequences(t, pe_1)
                x_proj(B - 1, 1)
                nc.tensor.wait_ge(s["dtlo_sb"], B)
                nc.tensor.wait_ge(s["z_act"], DC * B)
                nc.tensor.wait_ge(s["bs"], B)
                sequences(t, pe_2)
                mean_pe(B - 1, 1)
                for i in range(TILES):
                    last = nc.tensor.transpose(bank[6][0:B, i * P:(i + 1) * P], bs_all[:, i, :], ident[:])
                last.then_inc(s["bs_ps"], 1)
                nc.tensor.wait_ge(s["scanned"], 1)
                for i in range(TILES):
                    last = nc.tensor.transpose(bank[6][:, i * B:(i + 1) * B], state8[:, i * P:(i + 1) * P], ident[0:B, 0:B])
                last.then_inc(s["s_ps"], 1)
                sequences(t, pe_4)
                z_pe4(B - 1, 1)
                norm_pe(f0 + B)

            def scalar(c):
                after_phases(c, n)
                nc.scalar.wait_ge(s["edges"], 2 * DC)
                sequences(c, act_1)
                xs_act(B - 1, 1)
                dtlo_act(B - 1)
                nc.scalar.wait_ge(s["bc_ps"], B)
                nc.scalar.wait_ge(s["bs"], B)
                sequences(c, act_2)
                dm_act(B - 1, 1)
                c.wait_ge(s["decay_rows"], 16)
                nc.scalar.activation(decay8[:], decay8[:], ACT.Exp, scale=-1.0).then_inc(s["decay_exp"], 1)
                nc.scalar.wait_ge(s["dm_ps"], B)
                sequences(c, act_4)
                norm_act(f0 + B, 0)

            def vector(v):
                after_phases(v, n)
                v.wait_ge(w_loaded, 16 * N_WEIGHTS)
                for c in range(DC):
                    for e in (0, T + 1):
                        nc.vector.memset(xs_pad[c][:, e:e + 1], 0.0).then_inc(s["edges"], 1)
                v.wait_ge(s["edges"], 2 * DC)
                sequences(v, lambda b, par, f, l: dve_1(v, b, par, f, l))
                bs_dve(v, B - 1, 1)
                v.wait_ge(s["xs_act"], DC * B)
                v.wait_ge(s["bs"], B)
                v.wait_ge(s["bc_ps"], B)
                sequences(v, lambda b, par, f, l: dve_2(v, b, par, f, l))
                v.wait_ge(s["bs_ps"], 1)
                v.wait_ge(s["decay_exp"], 1)
                nc.vector.tensor_tensor_scan(state8[:], decay8[:], bank[6][0:B, :], 0.0, ALU.mult, ALU.add).then_inc(s["scanned"], 1)
                v.wait_ge(s["s_ps"], 1)
                nc.vector.tensor_copy(s_tok[:].rearrange("p b i -> p i b"),
                                      bank[6][:, 0:TILES * B].rearrange("p (i b) -> p i b", i=TILES)).then_inc(s["s_tok"], 1)
                v.wait_ge(s["s_tok"], 1)
                v.wait_ge(s["dm_ps"], B)
                v.wait_ge(s["decay"], B)
                dve_4a(v, 0)
                yn_dve(v, 0)
                sequences(v, lambda b, par, f, l: dve_4(v, b, par, f, l))
                dve_4c(v, B - 1, 1)
                norm_a(v, f0 + B, 0)
                norm_c(v, f0 + B, 0)

            def y_pool(b, par, first_, last_):
                nc.gpsimd.wait_ge(s["y_mv"], b + 1)
                rsqrt(s["y_var"], b, s["y_rs"])

            def gpsimd(g):
                after_phases(g, n)
                sequences(g, lambda b, par, f, l: None if l else norm_b(f0 + b + 1))
                sequences(g, y_pool)
                norm_b(f0 + B)

            def sync(q):
                q.wait_ge(s["decay"], B)
                q.dma_start(decay8[:], decays[0:1, :, :]).then_inc(s["decay_rows"], 16)

            return {"tensor": tensor, "scalar": scalar, "vector": vector, "gpsimd": gpsimd, "sync": sync}

        make = {"attn": attn_phase, "ssm": ssm_phase, "moe0": lambda n: moe_phase(n, 0), "moe1": lambda n: moe_phase(n, 1)}
        plan = [make[p](n) for n, p in enumerate(phases)]
        new_phase()

        block = ctx.enter_context(nc.Block())
        ov = out.rearrange("b (i p) e -> p (b i) e", p=P)
        r1 = lambda v: v.rearrange("(o n) -> o n", o=1)

        @block.sync
        def _(q):
            q.dma_start(x_res[:, 0:TILES, :], xv[:, 0:TILES, :]).then_inc(x_first, 16)
            q.dma_start(wr0[:], a["L0_ffn_w_router"]).then_inc(x_first, 16)
            rows = [
                (V_B1, a["L0_ffn_b1"].rearrange("e (c p) -> (e c) p", p=P)), (V_B2, a["L0_ffn_b2"]),
                (V_BK, r1(a["L0_attn_bk"])), (V_BV, r1(a["L0_attn_bv"])),
                (V_BDT, a["L1_attn_b_dt"].rearrange("(c p) -> c p", p=P)),
                (V_G, a["L1_attn_ln_g"].rearrange("(c p) -> c p", p=P)),
                (V_B, a["L1_attn_ln_b"].rearrange("(c p) -> c p", p=P))]
            for at, v in rows:
                q.dma_start(vec_rows[at:at + v.shape[0], :], v).then_inc(rows_loaded, 16)
            for at, v in ((V_BQ, a["L0_attn_bq"]), (V_BL, a["L0_attn_bl"])):
                q.dma_start(vec_rows[at:at + 1, :].rearrange("o (d h) -> o d h", d=HD),
                            v.rearrange("(o h d) -> o d h", o=1, d=HD),
                            allow_slow_non_contiguous=True).then_inc(rows_loaded, 16)
            assert len(rows) + 2 == N_ROWS
            if phases[0] != "moe0":
                load_x_rest(q)
                load_weights(q)
            for p in plan:
                p["sync"](q)
            for b in range(B):
                q.wait_ge(x_upd, B * (len(phases) - 1) + b + 1)
                q.dma_start(ov[:, b * TILES:(b + 1) * TILES, :], x_of(b)).then_inc(stored, 16)
            q.wait_ge(w_loaded, 16 * N_WEIGHTS)
            q.wait_ge(stored, 16 * B)

        @block.gpsimd
        def _(g):
            g.memset(ident[:], 0.0).then_inc(pool_chain, 1)
            g.memset(identb[:], 0.0).then_inc(pool_chain, 1)
            g.wait_ge(pool_chain, 2)
            for m in (ident, identb):
                g.affine_select(out=m[:], in_=m[:], compare_op=ALU.not_equal, fill=1.0, base=0, pattern=[[-1, P]],
                                channel_multiplier=1).then_inc(ident_ready, 1)
            for e in range(NE1):
                g.memset(first[:, :, e:e + 1], float(NE1 - e))
            g.memset(w_x[:, :, DTR + 2 * DS:], 1.0 / DI).then_inc(tables_ready, 1)
            g.memset(neg_half[:], -0.5).then_inc(pool_chain, 1)
            g.wait_ge(pool_chain, 3)
            norm_b(0)
            for p in plan:
                p["gpsimd"](g)

        @block.scalar
        def _(c):
            c.wait_ge(vecs_ps, 1)
            nc.scalar.copy(vecs[:], bank[0][:, 0:NVEC]).then_inc(vecs_ready, 1)
            norm_act(0, 0)
            for p in plan:
                p["scalar"](c)

        @block.vector
        def _(v):
            v.wait_ge(x_first, 32)
            norm_a(v, 0, 0)
            norm_c(v, 0, 0)
            v.wait_ge(tables_ready, 1)
            v.wait_ge(vecs_ready, 1)
            for p in plan:
                p["vector"](v)

        @block.tensor
        def _(t):
            t.wait_ge(ident_ready, 2)
            t.wait_ge(rows_loaded, 16 * N_ROWS)
            nc.tensor.transpose(bank[0][:, 0:NVEC], vec_rows[:], ident[0:NVEC, 0:NVEC]).then_inc(vecs_ps, 1)
            norm_pe(0)
            t.wait_ge(vecs_ready, 1)
            for p in plan:
                p["tensor"](t)


_INS = ['L0_attn_x', 'L0_attn_Wq', 'L0_attn_bq', 'L0_attn_Wk', 'L0_attn_bk', 'L0_attn_Wv', 'L0_attn_bv', 'L0_attn_Wl',
        'L0_attn_bl', 'L0_attn_Wo', 'L0_attn_bo', 'L0_ffn_w_router', 'L0_ffn_w1', 'L0_ffn_b1', 'L0_ffn_w2', 'L0_ffn_b2',
        'L1_attn_W_in', 'L1_attn_W_conv', 'L1_attn_W_xproj', 'L1_attn_W_dt', 'L1_attn_b_dt', 'L1_attn_W_out',
        'L1_attn_ln_g', 'L1_attn_ln_b', 'L1_ffn_router_w', 'L1_ffn_gate_w', 'L1_ffn_up_w', 'L1_ffn_down_w',
        'L1_ffn_shared_gate_w', 'L1_ffn_shared_up_w', 'L1_ffn_shared_down_w']


def kernel(**inputs):
    import numpy as _np
    import concourse.bacc as _bacc
    from concourse import mybir as _mybir
    from concourse.bass_utils import run_bass_kernel_spmd as _run

    nc = _bacc.Bacc("TRN2", target_bir_lowering=False, num_devices=1)
    arrays, aps = {}, {}
    for name in _INS:
        v = _np.ascontiguousarray(inputs[name])
        arrays[f"in_{name}"] = v
        aps[name] = nc.dram_tensor(f"in_{name}", v.shape, _mybir.dt.from_np(v.dtype), kind="ExternalInput").ap()
    out = nc.dram_tensor("out_x", (B, T, E), F32, kind="ExternalOutput").ap()
    build(nc, aps, out)
    r = _run(nc, [arrays], core_ids=[0])
    return r.results[0]["out_x"]
```
